# Optimizing a Trainium2 kernel written in Bass

```python
import numpy as np
import jax
import jax.numpy as jnp

def _softmax(x, axis=-1):
    return jax.nn.softmax(x, axis=axis)

def _gelu(x):
    return jax.nn.gelu(x, approximate=True)

def _silu(x):
    return jax.nn.silu(x)

def _sigmoid(x):
    return jax.nn.sigmoid(x)

def _layernorm(x, axis=-1, eps=1e-05):
    m = jnp.mean(x, axis=axis, keepdims=True)
    v = jnp.var(x, axis=axis, keepdims=True)
    return (x - m) / jnp.sqrt(v + eps)

def _scatter_add(tgt, idx, src, axis=0):
    return tgt.at[idx].add(src)

def _segment_sum(src, seg, n):
    return jax.ops.segment_sum(src, seg, n)
kernel_name = 'mk_xattn_ffn_d4_seqx_r8_0f51ea'

def setup_inputs(seed: int=0):
    np.random.seed(seed)
    _w = jnp.asarray

    def _rec_inputs():
        import jax
        import jax.numpy as jnp
        _rk = jax.random.key(seed)
        x = -0.0002928 + 1 * jax.random.normal(jax.random.fold_in(_rk, 1), (32, 64, 128), jnp.float32)
        _lenS = 64 - jax.random.randint(jax.random.fold_in(_rk, 7), (32,), 0, max(1, 64 // 4) + 1, jnp.int32)
        _lenS2 = 64 - jax.random.randint(jax.random.fold_in(_rk, 8), (32,), 0, max(1, 64 // 4) + 1, jnp.int32)
        _ctx_1024P = jax.random.normal(jax.random.fold_in(_rk, 11), (32, 16, 128), jnp.float32)
        _ctx_1024c = jax.random.dirichlet(jax.random.fold_in(_rk, 511), 0.3 * jnp.ones((16,), jnp.float32), (32, 64))
        _ctx_1024t = jnp.einsum('bsk,bkd->bsd', _ctx_1024c, _ctx_1024P)
        _ctx_1024t = _ctx_1024t * jax.lax.rsqrt(jnp.mean(jnp.square(_ctx_1024t)) + 1e-12) * 0.953939
        ctx_1024 = -1.39393e-06 + 0.999914 * (_ctx_1024t + 0.3 * jax.random.normal(jax.random.fold_in(_rk, 611), (32, 64, 128), jnp.float32))
        _validS = jnp.arange(64)[None, :] < _lenS[:, None]
        _validS2 = jnp.arange(64)[None, :] < _lenS2[:, None]
        _causal = jnp.tril(jnp.ones((64, 64), dtype=bool))
        mask_BxS2_bf1 = jnp.ones((32, 64), dtype=bool)
        mask_BxSxS2_bk0 = jnp.logical_not(jnp.broadcast_to(_validS2[:, None, :], (32, 64, 64)))
        return (x, ctx_1024, mask_BxS2_bf1, mask_BxSxS2_bk0)
    x, ctx_1024, mask_BxS2_bf1, mask_BxSxS2_bk0 = _rec_inputs()

    def _L0_xattn_setup():
        import jax, jax.numpy as jnp
        import numpy as np
        NUM_HEADS = 16
        D_MODEL = 128
        D_K = D_MODEL // NUM_HEADS

        def _split_heads(x):
            B, S, _ = x.shape
            return x.reshape(B, S, NUM_HEADS, D_K).transpose(0, 2, 1, 3)
        key = jax.random.key(seed)
        ks = jax.random.split(key, 11)
        B, S = (2, 256)
        s = 1.0 / np.sqrt(D_MODEL)
        return {'Q': jax.random.normal(ks[0], (B, S, D_MODEL), jnp.float32), 'K': jax.random.normal(ks[1], (B, S, D_MODEL), jnp.float32), 'V': jax.random.normal(ks[2], (B, S, D_MODEL), jnp.float32), 'Wq': jax.random.normal(ks[3], (D_MODEL, D_MODEL), jnp.float32) * s, 'bq': jnp.zeros((D_MODEL,), jnp.float32), 'Wk': jax.random.normal(ks[4], (D_MODEL, D_MODEL), jnp.float32) * s, 'bk': jnp.zeros((D_MODEL,), jnp.float32), 'Wv': jax.random.normal(ks[5], (D_MODEL, D_MODEL), jnp.float32) * s, 'bv': jnp.zeros((D_MODEL,), jnp.float32), 'Wo': jax.random.normal(ks[6], (D_MODEL, D_MODEL), jnp.float32) * s, 'bo': jnp.zeros((D_MODEL,), jnp.float32)}
    _L0_xattn_all = _L0_xattn_setup()
    _L0_xattn_in = {k: v for k, v in _L0_xattn_all.items() if k in ('Wq', 'bq', 'Wk', 'bk', 'Wv', 'bv', 'Wo', 'bo')}
    del _L0_xattn_all

    def _L0_ffn_setup():
        import jax, jax.numpy as jnp
        import numpy as np
        N_EMBD = 128
        N_STATE = 512
        key = jax.random.key(seed)
        k_x, k_w1, k_b1, k_w2, k_b2 = jax.random.split(key, 5)
        x = jax.random.normal(k_x, (4, 256, N_EMBD), dtype=jnp.float32)
        w1 = jax.random.normal(k_w1, (N_EMBD, N_STATE), dtype=jnp.float32) * (1.0 / np.sqrt(N_EMBD))
        b1 = jax.random.normal(k_b1, (N_STATE,), dtype=jnp.float32) * 0.02
        w2 = jax.random.normal(k_w2, (N_STATE, N_EMBD), dtype=jnp.float32) * (1.0 / np.sqrt(N_STATE))
        b2 = jax.random.normal(k_b2, (N_EMBD,), dtype=jnp.float32) * 0.02
        return {'x': x, 'w1': w1, 'b1': b1, 'w2': w2, 'b2': b2}
    _L0_ffn_all = _L0_ffn_setup()
    _L0_ffn_in = {k: v for k, v in _L0_ffn_all.items() if k in ('w1', 'b1', 'w2', 'b2')}
    del _L0_ffn_all

    def _L1_xattn_setup():
        import jax, jax.numpy as jnp
        import numpy as np
        DIM = 128
        NUM_HEADS = 16
        DIM_HEAD = 64
        INNER = NUM_HEADS * DIM_HEAD
        SCALE = DIM_HEAD ** (-0.5)

        def _layernorm(x, gamma, beta, eps=1e-05):
            mu = jnp.mean(x, axis=-1, keepdims=True)
            var = jnp.mean(jnp.square(x - mu), axis=-1, keepdims=True)
            return (x - mu) * jax.lax.rsqrt(var + eps) * gamma + beta
        key = jax.random.key(seed)
        ks = jax.random.split(key, 8)
        B, SQ, SK = (2, 256, 512)
        x = jax.random.normal(ks[0], (B, SQ, DIM), dtype=jnp.float32)
        context = jax.random.normal(ks[1], (B, SK, DIM), dtype=jnp.float32)
        ln_gamma = jnp.ones((DIM,), jnp.float32)
        ln_beta = jnp.zeros((DIM,), jnp.float32)
        w_q = jax.random.normal(ks[2], (DIM, INNER), dtype=jnp.float32) / np.sqrt(DIM)
        w_kv = jax.random.normal(ks[3], (DIM, 2 * INNER), dtype=jnp.float32) / np.sqrt(DIM)
        w_out = jax.random.normal(ks[4], (INNER, DIM), dtype=jnp.float32) / np.sqrt(INNER)
        b_out = jnp.zeros((DIM,), jnp.float32)
        gate = jnp.array([0.5], jnp.float32)
        return {'x': x, 'context': context, 'ln_gamma': ln_gamma, 'ln_beta': ln_beta, 'w_q': w_q, 'w_kv': w_kv, 'w_out': w_out, 'b_out': b_out, 'gate': gate}
    _L1_xattn_all = _L1_xattn_setup()
    _L1_xattn_in = {k: v for k, v in _L1_xattn_all.items() if k in ('ln_gamma', 'ln_beta', 'w_q', 'w_kv', 'w_out', 'b_out', 'gate')}
    del _L1_xattn_all

    def _L1_ffn_setup():
        import jax, jax.numpy as jnp
        import numpy as np
        B, T, D = (4, 256, 128)
        I = 128
        E_ROUTED = 14
        N_SHARED = 2
        TOPK = 2

        def _ffn(x, w1, b1, w2, b2):
            h = jax.nn.gelu(jnp.einsum('btd,di->bti', x, w1) + b1, approximate=False)
            return jnp.einsum('bti,id->btd', h, w2) + b2
        key = jax.random.key(seed)
        ks = jax.random.split(key, 12)
        s = 0.02
        return {'x': jax.random.normal(ks[0], (B, T, D), dtype=jnp.float32), 'router_w': jax.random.normal(ks[1], (D, E_ROUTED), dtype=jnp.float32) * s, 'router_b': jnp.zeros((E_ROUTED,), dtype=jnp.float32), 'shared_w1': jax.random.normal(ks[2], (N_SHARED, D, I), dtype=jnp.float32) * s, 'shared_b1': jnp.zeros((N_SHARED, I), dtype=jnp.float32), 'shared_w2': jax.random.normal(ks[3], (N_SHARED, I, D), dtype=jnp.float32) * s, 'shared_b2': jnp.zeros((N_SHARED, D), dtype=jnp.float32), 'routed_w1': jax.random.normal(ks[4], (E_ROUTED, D, I), dtype=jnp.float32) * s, 'routed_b1': jnp.zeros((E_ROUTED, I), dtype=jnp.float32), 'routed_w2': jax.random.normal(ks[5], (E_ROUTED, I, D), dtype=jnp.float32) * s, 'routed_b2': jnp.zeros((E_ROUTED, D), dtype=jnp.float32)}
    _L1_ffn_all = _L1_ffn_setup()
    _L1_ffn_in = {k: v for k, v in _L1_ffn_all.items() if k in ('router_w', 'router_b', 'shared_w1', 'shared_b1', 'shared_w2', 'shared_b2', 'routed_w1', 'routed_b1', 'routed_w2', 'routed_b2')}
    del _L1_ffn_all

    def _L2_xattn_setup():
        import jax, jax.numpy as jnp
        import numpy as np
        D_MODEL = 128
        FFN = 512
        E = 8
        K = 2
        B, S = (4, 64)
        key = jax.random.key(seed)
        ks = jax.random.split(key, 8)
        scale_in = 1.0 / np.sqrt(D_MODEL)
        scale_ffn = 1.0 / np.sqrt(FFN)
        return {'x': jax.random.normal(ks[0], (B, S, D_MODEL), jnp.float32), 'context': jax.random.normal(ks[1], (B, S, D_MODEL), jnp.float32), 'Wg': jax.random.normal(ks[2], (D_MODEL, E), jnp.float32) * scale_in, 'bg': jnp.zeros((E,), jnp.float32), 'W1': jax.random.normal(ks[3], (E, D_MODEL, FFN), jnp.float32) * scale_in, 'b1': jnp.zeros((E, FFN), jnp.float32), 'W2': jax.random.normal(ks[4], (E, FFN, D_MODEL), jnp.float32) * scale_ffn, 'b2': jnp.zeros((E, D_MODEL), jnp.float32)}
    _L2_xattn_all = _L2_xattn_setup()
    _L2_xattn_in = {k: v for k, v in _L2_xattn_all.items() if k in ('Wg', 'bg', 'W1', 'b1', 'W2', 'b2')}
    del _L2_xattn_all

    def _L2_ffn_setup():
        import jax, jax.numpy as jnp
        import numpy as np
        TOP_K = 2
        key = jax.random.key(seed)
        k0, k1, k2, k3, k4 = jax.random.split(key, 5)
        B, S, H, I, E = (4, 256, 128, 352, 8)
        s_h = 1.0 / np.sqrt(H)
        s_i = 1.0 / np.sqrt(I)
        return {'x': jax.random.normal(k0, (B, S, H), jnp.float32), 'w_router': jax.random.normal(k1, (E, H), jnp.float32) * s_h, 'w_gate': jax.random.normal(k2, (E, I, H), jnp.float32) * s_h, 'w_up': jax.random.normal(k3, (E, I, H), jnp.float32) * s_h, 'w_down': jax.random.normal(k4, (E, H, I), jnp.float32) * s_i}
    _L2_ffn_all = _L2_ffn_setup()
    _L2_ffn_in = {k: v for k, v in _L2_ffn_all.items() if k in ('w_router', 'w_gate', 'w_up', 'w_down')}
    del _L2_ffn_all

    def _L3_xattn_setup():
        import math
        import jax, jax.numpy as jnp
        import numpy as np
        NUM_HEADS = 16
        EMBED_DIM = 128
        HEAD_DIM = EMBED_DIM // NUM_HEADS
        N, S = (2, 256)

        def _mha(Q, K, V, Wq, Wk, Wv, Wo, padding_mask, attention_mask):
            n, s, e = Q.shape
            q = (Q @ Wq.T).reshape(n, s, NUM_HEADS, HEAD_DIM).transpose(0, 2, 1, 3)
            k = (K @ Wk.T).reshape(n, s, NUM_HEADS, HEAD_DIM).transpose(0, 2, 1, 3)
            v = (V @ Wv.T).reshape(n, s, NUM_HEADS, HEAD_DIM).transpose(0, 2, 1, 3)
            scores = jnp.einsum('nhqd,nhkd->nhqk', q, k) / math.sqrt(HEAD_DIM)
            neg_inf = jnp.float32(-jnp.inf)
            pm = padding_mask[:, None, :, None]
            scores = jnp.where(pm, scores, neg_inf)
            scores = jnp.where(attention_mask[:, None, :, :], scores, neg_inf)
            attn = jax.nn.softmax(scores, axis=-1)
            attn = jnp.where(jnp.isnan(attn), 0.0, attn)
            out = jnp.einsum('nhqk,nhkd->nhqd', attn, v)
            out = out.transpose(0, 2, 1, 3).reshape(n, s, e)
            out = out @ Wo.T
            return out
        key = jax.random.key(seed)
        ks = jax.random.split(key, 7)
        scale = 1.0 / math.sqrt(EMBED_DIM)
        Q = jax.random.normal(ks[0], (N, S, EMBED_DIM), dtype=jnp.float32)
        K = jax.random.normal(ks[1], (N, S, EMBED_DIM), dtype=jnp.float32)
        V = jax.random.normal(ks[2], (N, S, EMBED_DIM), dtype=jnp.float32)
        Wq = jax.random.normal(ks[3], (EMBED_DIM, EMBED_DIM), dtype=jnp.float32) * scale
        Wk = jax.random.normal(ks[4], (EMBED_DIM, EMBED_DIM), dtype=jnp.float32) * scale
        Wv = jax.random.normal(ks[5], (EMBED_DIM, EMBED_DIM), dtype=jnp.float32) * scale
        Wo = jax.random.normal(ks[6], (EMBED_DIM, EMBED_DIM), dtype=jnp.float32) * scale
        padding_mask = jnp.ones((N, S), dtype=bool)
        attention_mask = jnp.broadcast_to(jnp.tril(jnp.ones((S, S), dtype=bool)), (N, S, S))
        return {'Q': Q, 'K': K, 'V': V, 'Wq': Wq, 'Wk': Wk, 'Wv': Wv, 'Wo': Wo, 'padding_mask': padding_mask, 'attention_mask': attention_mask}
    _L3_xattn_all = _L3_xattn_setup()
    _L3_xattn_in = {k: v for k, v in _L3_xattn_all.items() if k in ('Wq', 'Wk', 'Wv', 'Wo')}
    del _L3_xattn_all

    def _L3_ffn_setup():
        import jax, jax.numpy as jnp
        import numpy as np
        BLOCK = 32
        W_BITS = 4
        ACT_BITS = 16

        def act_qdq(x):
            qmax = 2.0 ** (ACT_BITS - 1) - 1.0
            scale = jnp.maximum(jnp.max(jnp.abs(x)) / qmax, 1e-12)
            return jnp.clip(jnp.round(x / scale), -qmax - 1.0, qmax) * scale

        def fixed_qdq_u16(x):
            scale = 1.0 / 65536.0
            return jnp.clip(jnp.round(x / scale), 0.0, 65535.0) * scale

        def lpbq_dequant(w):
            O, I = w.shape
            qmax = 2.0 ** (W_BITS - 1) - 1.0
            wb = w.reshape(O, I // BLOCK, BLOCK)
            s = jnp.maximum(jnp.max(jnp.abs(wb), axis=-1, keepdims=True) / qmax, 1e-12)
            wq = jnp.clip(jnp.round(wb / s), -qmax - 1.0, qmax) * s
            return wq.reshape(O, I)
        key = jax.random.key(seed)
        k1, k2, k3, k4 = jax.random.split(key, 4)
        B, S, H, I = (2, 512, 128, 384)
        x = jax.random.normal(k1, (B, S, H), jnp.float32)
        w_gate = jax.random.normal(k2, (I, H), jnp.float32) * 0.02
        w_up = jax.random.normal(k3, (I, H), jnp.float32) * 0.02
        w_down = jax.random.normal(k4, (H, I), jnp.float32) * 0.02
        return {'x': x, 'w_gate': w_gate, 'w_up': w_up, 'w_down': w_down}
    _L3_ffn_all = _L3_ffn_setup()
    _L3_ffn_in = {k: v for k, v in _L3_ffn_all.items() if k in ('w_gate', 'w_up', 'w_down')}
    del _L3_ffn_all
    return {'x': x, 'ctx_1024': ctx_1024, 'mask_BxS2_bf1': mask_BxS2_bf1, 'mask_BxSxS2_bk0': mask_BxSxS2_bk0, 'L0_xattn_Wq': _L0_xattn_in['Wq'], 'L0_xattn_bq': _L0_xattn_in['bq'], 'L0_xattn_Wk': _L0_xattn_in['Wk'], 'L0_xattn_bk': _L0_xattn_in['bk'], 'L0_xattn_Wv': _L0_xattn_in['Wv'], 'L0_xattn_bv': _L0_xattn_in['bv'], 'L0_xattn_Wo': _L0_xattn_in['Wo'], 'L0_xattn_bo': _L0_xattn_in['bo'], 'L0_ffn_w1': _L0_ffn_in['w1'], 'L0_ffn_b1': _L0_ffn_in['b1'], 'L0_ffn_w2': _L0_ffn_in['w2'], 'L0_ffn_b2': _L0_ffn_in['b2'], 'L1_xattn_ln_gamma': _L1_xattn_in['ln_gamma'], 'L1_xattn_ln_beta': _L1_xattn_in['ln_beta'], 'L1_xattn_w_q': _L1_xattn_in['w_q'], 'L1_xattn_w_kv': _L1_xattn_in['w_kv'], 'L1_xattn_w_out': _L1_xattn_in['w_out'], 'L1_xattn_b_out': _L1_xattn_in['b_out'], 'L1_xattn_gate': _L1_xattn_in['gate'], 'L1_ffn_router_w': _L1_ffn_in['router_w'], 'L1_ffn_router_b': _L1_ffn_in['router_b'], 'L1_ffn_shared_w1': _L1_ffn_in['shared_w1'], 'L1_ffn_shared_b1': _L1_ffn_in['shared_b1'], 'L1_ffn_shared_w2': _L1_ffn_in['shared_w2'], 'L1_ffn_shared_b2': _L1_ffn_in['shared_b2'], 'L1_ffn_routed_w1': _L1_ffn_in['routed_w1'], 'L1_ffn_routed_b1': _L1_ffn_in['routed_b1'], 'L1_ffn_routed_w2': _L1_ffn_in['routed_w2'], 'L1_ffn_routed_b2': _L1_ffn_in['routed_b2'], 'L2_xattn_Wg': _L2_xattn_in['Wg'], 'L2_xattn_bg': _L2_xattn_in['bg'], 'L2_xattn_W1': _L2_xattn_in['W1'], 'L2_xattn_b1': _L2_xattn_in['b1'], 'L2_xattn_W2': _L2_xattn_in['W2'], 'L2_xattn_b2': _L2_xattn_in['b2'], 'L2_ffn_w_router': _L2_ffn_in['w_router'], 'L2_ffn_w_gate': _L2_ffn_in['w_gate'], 'L2_ffn_w_up': _L2_ffn_in['w_up'], 'L2_ffn_w_down': _L2_ffn_in['w_down'], 'L3_xattn_Wq': _L3_xattn_in['Wq'], 'L3_xattn_Wk': _L3_xattn_in['Wk'], 'L3_xattn_Wv': _L3_xattn_in['Wv'], 'L3_xattn_Wo': _L3_xattn_in['Wo'], 'L3_ffn_w_gate': _L3_ffn_in['w_gate'], 'L3_ffn_w_up': _L3_ffn_in['w_up'], 'L3_ffn_w_down': _L3_ffn_in['w_down']}

def reference(x, ctx_1024, mask_BxS2_bf1, mask_BxSxS2_bk0, L0_xattn_Wq, L0_xattn_bq, L0_xattn_Wk, L0_xattn_bk, L0_xattn_Wv, L0_xattn_bv, L0_xattn_Wo, L0_xattn_bo, L0_ffn_w1, L0_ffn_b1, L0_ffn_w2, L0_ffn_b2, L1_xattn_ln_gamma, L1_xattn_ln_beta, L1_xattn_w_q, L1_xattn_w_kv, L1_xattn_w_out, L1_xattn_b_out, L1_xattn_gate, L1_ffn_router_w, L1_ffn_router_b, L1_ffn_shared_w1, L1_ffn_shared_b1, L1_ffn_shared_w2, L1_ffn_shared_b2, L1_ffn_routed_w1, L1_ffn_routed_b1, L1_ffn_routed_w2, L1_ffn_routed_b2, L2_xattn_Wg, L2_xattn_bg, L2_xattn_W1, L2_xattn_b1, L2_xattn_W2, L2_xattn_b2, L2_ffn_w_router, L2_ffn_w_gate, L2_ffn_w_up, L2_ffn_w_down, L3_xattn_Wq, L3_xattn_Wk, L3_xattn_Wv, L3_xattn_Wo, L3_ffn_w_gate, L3_ffn_w_up, L3_ffn_w_down):
    import jax
    import jax.numpy as jnp

    def _L0_xattn_ref(Q, K, V, Wq, bq, Wk, bk, Wv, bv, Wo, bo):
        import jax, jax.numpy as jnp
        import numpy as np
        NUM_HEADS = 16
        D_MODEL = 128
        D_K = D_MODEL // NUM_HEADS

        def _split_heads(x):
            B, S, _ = x.shape
            return x.reshape(B, S, NUM_HEADS, D_K).transpose(0, 2, 1, 3)
        q = _split_heads(Q @ Wq + bq)
        k = _split_heads(K @ Wk + bk)
        v = _split_heads(V @ Wv + bv)
        scores = jnp.einsum('bhqd,bhkd->bhqk', q, k) / jnp.sqrt(jnp.asarray(D_K, q.dtype))
        attn = jax.nn.softmax(scores, axis=-1)
        out = jnp.einsum('bhqk,bhkd->bhqd', attn, v)
        B, H, S, Dk = out.shape
        combined = out.transpose(0, 2, 1, 3).reshape(B, S, H * Dk)
        return combined @ Wo + bo

    def _L0_ffn_ref(x, w1, b1, w2, b2):
        import jax, jax.numpy as jnp
        import numpy as np
        N_EMBD = 128
        N_STATE = 512
        h = jax.nn.gelu(jnp.einsum('bse,eh->bsh', x, w1) + b1, approximate=False)
        return jnp.einsum('bsh,he->bse', h, w2) + b2

    def _L1_xattn_ref(x, context, ln_gamma, ln_beta, w_q, w_kv, w_out, b_out, gate):
        import jax, jax.numpy as jnp
        import numpy as np
        DIM = 128
        NUM_HEADS = 16
        DIM_HEAD = 64
        INNER = NUM_HEADS * DIM_HEAD
        SCALE = DIM_HEAD ** (-0.5)

        def _layernorm(x, gamma, beta, eps=1e-05):
            mu = jnp.mean(x, axis=-1, keepdims=True)
            var = jnp.mean(jnp.square(x - mu), axis=-1, keepdims=True)
            return (x - mu) * jax.lax.rsqrt(var + eps) * gamma + beta
        B, SQ, _ = x.shape
        SK = context.shape[1]
        xn = _layernorm(x, ln_gamma, ln_beta)
        q = (xn @ w_q).reshape(B, SQ, NUM_HEADS, DIM_HEAD)
        kv = context @ w_kv
        k, v = jnp.split(kv, 2, axis=-1)
        k = k.reshape(B, SK, NUM_HEADS, DIM_HEAD)
        v = v.reshape(B, SK, NUM_HEADS, DIM_HEAD)
        scores = jnp.einsum('bqhd,bkhd->bhqk', q * SCALE, k)
        attn = jax.nn.softmax(scores, axis=-1)
        out = jnp.einsum('bhqk,bkhd->bqhd', attn, v).reshape(B, SQ, INNER)
        out = out @ w_out + b_out
        return out * jnp.tanh(gate[0])

    def _L1_ffn_ref(x, router_w, router_b, shared_w1, shared_b1, shared_w2, shared_b2, routed_w1, routed_b1, routed_w2, routed_b2):
        import jax, jax.numpy as jnp
        import numpy as np
        B, T, D = (4, 256, 128)
        I = 128
        E_ROUTED = 14
        N_SHARED = 2
        TOPK = 2

        def _ffn(x, w1, b1, w2, b2):
            h = jax.nn.gelu(jnp.einsum('btd,di->bti', x, w1) + b1, approximate=False)
            return jnp.einsum('bti,id->btd', h, w2) + b2
        shared_out = jnp.zeros_like(x)
        for s in range(N_SHARED):
            shared_out = shared_out + _ffn(x, shared_w1[s], shared_b1[s], shared_w2[s], shared_b2[s])
        logits = jnp.einsum('btd,de->bte', x, router_w) + router_b
        affinities = jax.nn.softmax(logits, axis=-1)
        topk_vals, topk_idx = jax.lax.top_k(affinities, TOPK)
        gates = jnp.sum(jax.nn.one_hot(topk_idx, E_ROUTED, dtype=x.dtype) * topk_vals[..., None], axis=-2)
        routed_out = jnp.zeros_like(x)
        for e in range(E_ROUTED):
            expert_out = _ffn(x, routed_w1[e], routed_b1[e], routed_w2[e], routed_b2[e])
            routed_out = routed_out + gates[..., e:e + 1] * expert_out
        return shared_out + routed_out + x

    def _L2_xattn_ref(x, context, Wg, bg, W1, b1, W2, b2):
        import jax, jax.numpy as jnp
        import numpy as np
        D_MODEL = 128
        FFN = 512
        E = 8
        K = 2
        B, S = (4, 64)
        logits = jnp.einsum('bsd,de->bse', context, Wg) + bg
        scores_topk, idx_topk = jax.lax.top_k(logits, K)
        weights = jax.nn.softmax(scores_topk, axis=-1)
        combine = jnp.sum(jax.nn.one_hot(idx_topk, E, dtype=weights.dtype) * weights[..., None], axis=-2)
        h = jax.nn.relu(jnp.einsum('bsd,edf->bsef', x, W1) + b1)
        y = jnp.einsum('bsef,efd->bsed', h, W2) + b2
        out = jnp.einsum('bsed,bse->bsd', y, combine)
        return out

    def _L2_ffn_ref(x, w_router, w_gate, w_up, w_down):
        import jax, jax.numpy as jnp
        import numpy as np
        TOP_K = 2
        B, S, H = x.shape
        E = w_router.shape[0]
        xf = x.reshape(-1, H)
        logits = jnp.einsum('th,eh->te', xf, w_router)
        probs = jax.nn.softmax(logits, axis=-1)
        topw, topi = jax.lax.top_k(probs, TOP_K)
        topw = topw / jnp.sum(topw, axis=-1, keepdims=True)
        onehot = (topi[..., None] == jnp.arange(E)).astype(x.dtype)
        combine = jnp.einsum('tk,tke->te', topw, onehot)
        gate = jax.nn.silu(jnp.einsum('th,eih->eti', xf, w_gate))
        up = jnp.einsum('th,eih->eti', xf, w_up)
        down = jnp.einsum('eti,ehi->eth', gate * up, w_down)
        out = jnp.einsum('eth,te->th', down, combine)
        return out.reshape(B, S, H)

    def _L3_xattn_ref(Q, K, V, Wq, Wk, Wv, Wo, padding_mask, attention_mask):
        import math
        import jax, jax.numpy as jnp
        import numpy as np
        NUM_HEADS = 16
        EMBED_DIM = 128
        HEAD_DIM = EMBED_DIM // NUM_HEADS
        N, S = (2, 256)

        def _mha(Q, K, V, Wq, Wk, Wv, Wo, padding_mask, attention_mask):
            n, s, e = Q.shape
            q = (Q @ Wq.T).reshape(n, s, NUM_HEADS, HEAD_DIM).transpose(0, 2, 1, 3)
            k = (K @ Wk.T).reshape(n, s, NUM_HEADS, HEAD_DIM).transpose(0, 2, 1, 3)
            v = (V @ Wv.T).reshape(n, s, NUM_HEADS, HEAD_DIM).transpose(0, 2, 1, 3)
            scores = jnp.einsum('nhqd,nhkd->nhqk', q, k) / math.sqrt(HEAD_DIM)
            neg_inf = jnp.float32(-jnp.inf)
            pm = padding_mask[:, None, :, None]
            scores = jnp.where(pm, scores, neg_inf)
            scores = jnp.where(attention_mask[:, None, :, :], scores, neg_inf)
            attn = jax.nn.softmax(scores, axis=-1)
            attn = jnp.where(jnp.isnan(attn), 0.0, attn)
            out = jnp.einsum('nhqk,nhkd->nhqd', attn, v)
            out = out.transpose(0, 2, 1, 3).reshape(n, s, e)
            out = out @ Wo.T
            return out
        return _mha(Q, K, V, Wq, Wk, Wv, Wo, padding_mask, attention_mask)

    def _L3_ffn_ref(x, w_gate, w_up, w_down):
        import jax, jax.numpy as jnp
        import numpy as np
        BLOCK = 32
        W_BITS = 4
        ACT_BITS = 16

        def act_qdq(x):
            qmax = 2.0 ** (ACT_BITS - 1) - 1.0
            scale = jnp.maximum(jnp.max(jnp.abs(x)) / qmax, 1e-12)
            return jnp.clip(jnp.round(x / scale), -qmax - 1.0, qmax) * scale

        def fixed_qdq_u16(x):
            scale = 1.0 / 65536.0
            return jnp.clip(jnp.round(x / scale), 0.0, 65535.0) * scale

        def lpbq_dequant(w):
            O, I = w.shape
            qmax = 2.0 ** (W_BITS - 1) - 1.0
            wb = w.reshape(O, I // BLOCK, BLOCK)
            s = jnp.maximum(jnp.max(jnp.abs(wb), axis=-1, keepdims=True) / qmax, 1e-12)
            wq = jnp.clip(jnp.round(wb / s), -qmax - 1.0, qmax) * s
            return wq.reshape(O, I)
        x = act_qdq(x)
        up = act_qdq(x @ lpbq_dequant(w_up).T)
        gate = act_qdq(x @ lpbq_dequant(w_gate).T)
        sig = fixed_qdq_u16(jax.nn.sigmoid(gate))
        gate = act_qdq(gate * sig)
        o = act_qdq(gate * up)
        return o @ lpbq_dequant(w_down).T
    x = x + _L0_xattn_ref(_layernorm(x, axis=-1), ctx_1024, ctx_1024, L0_xattn_Wq, L0_xattn_bq, L0_xattn_Wk, L0_xattn_bk, L0_xattn_Wv, L0_xattn_bv, L0_xattn_Wo, L0_xattn_bo)
    x = x + _L0_ffn_ref(_layernorm(x, axis=-1), L0_ffn_w1, L0_ffn_b1, L0_ffn_w2, L0_ffn_b2)
    x = x + _L1_xattn_ref(_layernorm(x, axis=-1), ctx_1024, L1_xattn_ln_gamma, L1_xattn_ln_beta, L1_xattn_w_q, L1_xattn_w_kv, L1_xattn_w_out, L1_xattn_b_out, L1_xattn_gate)
    x = x + _L1_ffn_ref(_layernorm(x, axis=-1), L1_ffn_router_w, L1_ffn_router_b, L1_ffn_shared_w1, L1_ffn_shared_b1, L1_ffn_shared_w2, L1_ffn_shared_b2, L1_ffn_routed_w1, L1_ffn_routed_b1, L1_ffn_routed_w2, L1_ffn_routed_b2)
    x = x + _L2_xattn_ref(_layernorm(x, axis=-1), ctx_1024, L2_xattn_Wg, L2_xattn_bg, L2_xattn_W1, L2_xattn_b1, L2_xattn_W2, L2_xattn_b2)
    x = x + _L2_ffn_ref(_layernorm(x, axis=-1), L2_ffn_w_router, L2_ffn_w_gate, L2_ffn_w_up, L2_ffn_w_down)
    x = x + _L3_xattn_ref(_layernorm(x, axis=-1), ctx_1024, ctx_1024, L3_xattn_Wq, L3_xattn_Wk, L3_xattn_Wv, L3_xattn_Wo, mask_BxS2_bf1, mask_BxSxS2_bk0)
    x = x + _L3_ffn_ref(_layernorm(x, axis=-1), L3_ffn_w_gate, L3_ffn_w_up, L3_ffn_w_down)
    return x

_drawn_inputs = setup_inputs


def setup_inputs(seed=0):
    import zlib

    import numpy as np

    out = dict(_drawn_inputs(seed))
    spreads = {'L0_xattn_bq': (0.0, 0.1),
     'L0_xattn_bk': (0.0, 0.8),
     'L0_xattn_bv': (0.0, 0.1),
     'L0_xattn_bo': (0.0, 0.1),
     'L1_xattn_ln_gamma': (1.0, 0.6),
     'L1_xattn_ln_beta': (0.0, 0.481),
     'L1_xattn_b_out': (0.0, 0.1),
     'L1_ffn_router_b': (0.0, 0.8),
     'L1_ffn_shared_b1': (0.0, 0.595),
     'L1_ffn_shared_b2': (0.0, 0.1),
     'L1_ffn_routed_b1': (0.0, 0.8),
     'L1_ffn_routed_b2': (0.0, 0.581),
     'L2_xattn_bg': (0.0, 0.1),
     'L2_xattn_b1': (0.0, 0.28),
     'L2_xattn_b2': (0.0, 0.1)}
    factors = {'L0_ffn_b1': 3.844,
     'L0_ffn_b2': 2.854,
     'L1_ffn_router_w': 5.599,
     'L1_ffn_routed_w1': 8.0,
     'L1_ffn_routed_w2': 8.0,
     'L3_ffn_w_gate': 8.0,
     'L3_ffn_w_up': 8.0,
     'L3_ffn_w_down': 8.0}
    for name, (base, spread) in spreads.items():
        noise = np.random.default_rng([zlib.crc32(name.encode()), seed]).standard_normal(out[name].shape)
        drawn = base * np.exp(spread * noise) if base else spread * noise
        out[name] = jnp.asarray(drawn.astype(out[name].dtype))
    for name, factor in factors.items():
        out[name] = (out[name] * factor).astype(out[name].dtype)
    return out
```

```python
from contextlib import ExitStack

import concourse.bass as bass
from concourse import mybir

ALU = mybir.AluOpType
ACT = mybir.ActivationFunctionType
F32 = mybir.dt.float32
U8 = mybir.dt.uint8
AX = mybir.AxisListType.X

P = 128
B, S, D = 32, 64, 128
TOK = B * S
NT = TOK // P
GT = 4
NG = NT // GT
GW = GT * P
H = 16
HP = H // 2
EPS = 1e-5
NEG = -1.0e30
ROUND = 1.5 * 2.0 ** 23


def live(t):
    return not isinstance(t, int) or 0 <= t < NT


def past(t, k):
    return not isinstance(t, int) or t >= k


def before_end(t, k):
    return not isinstance(t, int) or t < NT - k


def pipeline(eng, step, lo, hi, end):
    for n in range(lo):
        step(n, n % 2)
    with eng.Fori(lo, hi - 1, 2) as i:
        step(i, lo % 2)
        step(i + 1, (lo + 1) % 2)
    for n in range(hi, end):
        step(n, n % 2)


class Layer:

    def __init__(self):
        self.tensor = self.vector = self.scalar = self.gpsimd = self.sync = None
        self.done = None


def tile_of(x, t):
    return x[:, bass.ds(t, 1), :].rearrange("p a d -> p (a d)")


def columns(x, t, n):
    return x[:, bass.ds(t * n, n)]


def apart(eng, m):
    eng.sem_inc(m.passed, 1)


class Signal:

    def __init__(self, sem, base):
        self.sem, self.base = sem, base

    def __call__(self, n):
        return self.sem, self.base + n


class Shared:

    def __init__(self, nc, ctx):
        self.nc, self.ctx, self.counted = nc, ctx, {}

    def sb(self, name, shape, dt=F32):
        return self.ctx.enter_context(self.nc.sbuf_tensor(name, shape, dt))

    def ps(self, name, shape, dt=F32):
        return self.ctx.enter_context(self.nc.psum_tensor(name, shape, dt))

    def sem(self, name):
        return self.ctx.enter_context(self.nc.semaphore(name))

    def counted_semaphore(self, name, total):
        sem, base = self.counted.get(name) or (self.sem(name), 0)
        self.counted[name] = (sem, base + total)
        return Signal(sem, base)


class Norm:

    def __init__(self, sh, sb, tag, m, kind="norm"):
        self.st, self.mv = sb(f"{tag}_stats", [P, 2, 6]), sb(f"{tag}_meanvar", [P, 2, 2])
        self.ve, self.rs = sb(f"{tag}_vareps", [P, 2, 1]), sb(f"{tag}_rstd", [P, 2, 1])
        self.stats_chain = sh.counted_semaphore(f"{kind}_stats_chain", 2 * NT)
        self.var_ready = sh.counted_semaphore(f"{kind}_var_ready", NT)
        self.rstd_ready = sh.counted_semaphore(f"{kind}_rstd_ready", NT)
        self.nhalf, self.passed = m.nhalf, m.passed

    def stats(self, dve, x, t, p):
        if past(t, 2):
            dve.wait_ge(*self.rstd_ready(t - 1))
        dve.bn_stats(self.st[:, p, :], x).then_inc(self.stats_chain.sem, 1)
        dve.wait_ge(*self.stats_chain(2 * t + 1))
        apart(dve, self)
        dve.bn_aggr(self.mv[:, p, :], self.st[:, p, :]).then_inc(self.stats_chain.sem, 1)
        dve.wait_ge(*self.stats_chain(2 * t + 2))
        dve.tensor_scalar(self.ve[:, p, :], self.mv[:, p, 1:2], EPS, None, ALU.add).then_inc(self.var_ready.sem, 1)

    def rstd(self, pool, t, p, applied):
        pool.wait_ge(*self.var_ready(t + 1))
        if past(t, 2):
            pool.wait_ge(*applied(t - 1))
        pool.tensor_tensor(self.rs[:, p, :], self.ve[:, p, :], self.nhalf[:, :], ALU.pow).then_inc(self.rstd_ready.sem, 1)

    def apply(self, dve, out, x, t, p):
        dve.wait_ge(*self.rstd_ready(t + 1))
        return dve.tensor_scalar(out, x, self.mv[:, p, 0:1], self.rs[:, p, 0:1], ALU.subtract, ALU.mult)


def small_head_attention(sh, m, tag, start, w, bias, masked):
    nc = sh.nc
    dh = D // H
    scale = float(dh) ** -0.5
    L = Layer()
    with ExitStack() as scope:
        def sb(name, shape, dt=F32):
            return scope.enter_context(nc.sbuf_tensor(f"{tag}_{name}", shape, dt))

        norm = Norm(sh, sb, f"{tag}_ln", m)
        xn = sb("xn", [P, 2, P])
        xnT = sb("xnT", [P, 2, P])
        qT = sb("qT", [P, 2, P])
        kT = sb("kT", [P, 2, P])
        ctx2 = sb("ctx2", [P, 2, 2, 2, S])
        kexp = sb("kexp", [P, 2, 2, H, S])
        prob = sb("prob", [P, 2, H, S])
        probT = sb("probT", [P, 2, HP, P])
        vbd = sb("vbd", [P, 2, 2, H, dh + 1])
        mx = sb("mx", [P, 2, H])
        rc = sb("rc", [P, 2, H])
        on = sb("on", [P, 2, P])
        oT = sb("oT", [P, 2, P])
        tmp = sb("tmp", [P, 2, P])

    J0, J1 = m.banks[0], m.banks[1]
    pS, pP, pO = m.wide[0], m.wide[1], m.banks[6]
    sv = pS.rearrange("p a (h k) -> p (a h) k", k=S)

    signal = sh.counted_semaphore
    MC = RC = 2 if masked else 1
    vones = signal("vones_set", 5)
    xn_ready, xnT_ready, xnT_ps = signal("xn_ready", NT), signal("xnT_ready", NT), signal("xnT_in_psum", NT)
    q_ps, q_ready = signal("q_in_psum", NT), signal("q_ready", NT)
    k_ps, k_ready, kexp_ready = signal("k_in_psum", NT), signal("k_ready", NT), signal("kexp_ready", NT)
    v_ps, v_ready, ctx2_ready = signal("v_in_psum", NT), signal("v_ready", NT), signal("ctx2_ready", NT)
    scores_ready, max_chain, sub_ready = signal("scores_ready", NT), signal("max_chain", MC * NT), signal("sub_ready", NT)
    prob_ready, probT_ps, probT_ready = signal("prob_ready", NT), signal("probT_in_psum", 2 * NT), signal("probT_ready", 2 * NT)
    o_ps, rc_chain, on_ready = signal("o_in_psum", NT), signal("rc_chain", RC * NT), signal("on_ready", NT)
    oT_ps, oT_ready, out_ps, tmp_ready = signal("oT_in_psum", NT), signal("oT_ready", NT), signal("out_in_psum", NT), signal("tmp_ready", NT)
    x_done = signal("x_done", NT)
    L.done = x_done(NT)

    def tensor(pe):
        m.begin(pe, start)

        def keys_values(t, p):
            if past(t, 1):
                pe.wait_ge(*xnT_ready(t))
            pe.matmul(J0[:, 0:P], w["k"], columns(m.ctxT, t, P), start=True, stop=True).then_inc(k_ps.sem, 1)
            if past(t, 1):
                pe.wait_ge(*q_ready(t))
            pe.wait_ge(*ctx2_ready(t + 1))
            for b in range(2):
                mm = pe.matmul(J1[:, b * P:(b + 1) * P], ctx2[:, p, b].rearrange("p u s -> p (u s)"), w["v"],
                               start=True, stop=True)
            mm.then_inc(v_ps.sem, 1)

        def turn_x(t, p):
            pe.wait_ge(*xn_ready(t + 1))
            pe.wait_ge(*k_ready(t + 1))
            pe.transpose(J0[:, 0:P], xn[:, p, :], m.ident[:, :]).then_inc(xnT_ps.sem, 1)

        def queries(t, p):
            pe.wait_ge(*xnT_ready(t + 1))
            pe.wait_ge(*v_ready(t + 1))
            pe.matmul(J1[:, 0:P], w["q"], xnT[:, p, :], start=True, stop=True).then_inc(q_ps.sem, 1)

        def scores(t, p):
            pe.wait_ge(*q_ready(t + 1))
            pe.wait_ge(*kexp_ready(t + 1))
            if past(t, 1):
                pe.wait_ge(*sub_ready(t))
            for half in range(2):
                for b in range(2):
                    rhs = kexp[:, p, b, half * HP:(half + 1) * HP, :].rearrange("p h k -> p (h k)")
                    mm = pe.matmul(pS[b * S:(b + 1) * S, half, :], qT[:, p, b * S:(b + 1) * S], rhs,
                                   start=True, stop=True)
            mm.then_inc(scores_ready.sem, 1)

        def turn_probs(t, p):
            pe.wait_ge(*prob_ready(t + 1))
            if past(t, 2):
                pe.wait_ge(*tmp_ready(t - 1))
            elif past(t, 1):
                pe.wait_ge(*probT_ready(2 * t))
            for c in range(HP):
                tr = pe.transpose(pP[:, c // 4, c % 4 * P:c % 4 * P + P],
                                  prob[:, p, 2 * c:2 * c + 2, :].rearrange("p h k -> p (h k)"), m.ident[:, :])
                if c % 4 == 3:
                    tr.then_inc(probT_ps.sem, 1)

        def weigh_values(t, p):
            pe.wait_ge(*probT_ready(2 * t + 2))
            pe.wait_ge(*v_ready(t + 1))
            if past(t, 1):
                pe.wait_ge(*on_ready(t))
            for c in range(HP):
                for b in range(2):
                    mm = pe.matmul(pO[b * S:(b + 1) * S, c * 18:c * 18 + 18], probT[:, p, c, b * S:(b + 1) * S],
                                   vbd[:, p, b, 2 * c:2 * c + 2, :].rearrange("p h d -> p (h d)"),
                                   start=True, stop=True)
            mm.then_inc(o_ps.sem, 1)

        def turn_out(t, p):
            pe.wait_ge(*on_ready(t + 1))
            if before_end(t, 1):
                pe.wait_ge(*probT_ready(2 * t + 4))
            else:
                pe.wait_ge(*tmp_ready(t))
            pe.transpose(pP[:, 0, 0:P], on[:, p, :], m.ident[:, :]).then_inc(oT_ps.sem, 1)

        def project(t, p):
            pe.wait_ge(*oT_ready(t + 1))
            pe.matmul(pP[:, 1, 0:P], oT[:, p, :], w["o"], start=True, stop=True).then_inc(out_ps.sem, 1)

        def step(n, p):
            q = 1 - p
            if live(n - 1):
                turn_x(n - 1, q)
            if live(n - 2):
                turn_probs(n - 2, p)
            if live(n - 1):
                queries(n - 1, q)
            if live(n):
                keys_values(n, p)
            if live(n - 1):
                scores(n - 1, q)
            if live(n - 3):
                turn_out(n - 3, q)
            if live(n - 2):
                weigh_values(n - 2, p)
            if live(n - 3):
                project(n - 3, q)

        pipeline(pe, step, 5, NT - 1, NT + 3)

    def scalar(act):
        m.begin(act, start)

        def evac(dst, src, ready, n, done, bias=None):
            act.wait_ge(*ready(n))
            if bias is None:
                act.activation(dst, src, ACT.Copy).then_inc(done.sem, 1)
            else:
                act.activation(dst, src, ACT.Identity, bias=bias).then_inc(done.sem, 1)

        def step(n, p):
            q = 1 - p
            if live(n - 1):
                t = n - 1
                if past(t, 2):
                    act.wait_ge(*q_ps(t - 1))
                evac(xnT[:, q, :], J0[:, 0:P], xnT_ps, t + 1, xnT_ready)
            if live(n - 2):
                t = n - 2
                if past(t, 2):
                    act.wait_ge(*o_ps(t - 1))
                for half in range(2):
                    evac(probT[:, p, 4 * half:4 * half + 4, :].rearrange("p c q -> p (c q)"), pP[:, half, :],
                         probT_ps, 2 * t + half + 1, probT_ready)
            if live(n - 1):
                t = n - 1
                if past(t, 2):
                    act.wait_ge(*scores_ready(t - 1))
                evac(qT[:, q, :], J1[:, 0:P], q_ps, t + 1, q_ready, bias["q"])
            if live(n):
                t = n
                if past(t, 2):
                    act.wait_ge(*kexp_ready(t - 1))
                evac(kT[:, p, :], J0[:, 0:P], k_ps, t + 1, k_ready, bias["k"])
            if live(n - 3):
                t = n - 3
                if past(t, 2):
                    act.wait_ge(*out_ps(t - 1))
                evac(oT[:, q, :], pP[:, 0, 0:P], oT_ps, t + 1, oT_ready, bias["v"])
            if live(n - 1):
                t = n - 1
                act.wait_ge(*sub_ready(t + 1))
                pr = prob[:, q].rearrange("p h k -> p (h k)")
                act.activation(pr, pr, ACT.Exp, scale=scale).then_inc(prob_ready.sem, 1)

        pipeline(act, step, 5, NT - 1, NT + 3)

    def gpsimd(pool):
        m.begin(pool, start)
        pool.memset(vbd[:, :, :, :, :].rearrange("p a b h d -> p (a b h d)"), 0.0).then_inc(vones.sem, 1)
        for u in range(2):
            for a in range(2):
                pool.wait_ge(*vones(1 + 2 * u + a))
                pool.memset(vbd[u * S:(u + 1) * S, a, :, u::2, dh:dh + 1], 1.0).then_inc(vones.sem, 1)
        pool.wait_ge(*vones(5))

        def context(t, p):
            if past(t, 2):
                pool.wait_ge(*v_ps(t - 1))
            src = columns(m.ctxT, t, P).rearrange("p (b s) -> p b s", b=2)
            for u in range(2):
                cp = pool.tensor_copy(ctx2[:, p, :, u, :], src)
            cp.then_inc(ctx2_ready.sem, 1)

        def step(n, p):
            if live(n):
                t = n
                pool.wait_ge(*k_ready(t + 1))
                if past(t, 2):
                    pool.wait_ge(*scores_ready(t - 1))
                for b in range(2):
                    kk = kT[:, p, b * S:(b + 1) * S].rearrange("p (o k) -> p o k", o=1)
                    ke = pool.tensor_tensor(kexp[:, p, b], kk.broadcast_to([P, H, S]),
                                            m.hmask[:, :].rearrange("p (h o) -> p h o", o=1).broadcast_to([P, H, S]),
                                            ALU.mult)
                ke.then_inc(kexp_ready.sem, 1)
            if live(n + 1):
                norm.rstd(pool, n + 1, 1 - p, xn_ready)
                context(n + 1, 1 - p)

        norm.rstd(pool, 0, 0, xn_ready)
        context(0, 0)
        pipeline(pool, step, 5, NT - 1, NT + 3)

    def vector(dve):
        m.begin(dve, start)
        dve.wait_ge(*vones(5))

        def step(n, p):
            q = 1 - p
            if live(n):
                if past(n, 2):
                    dve.wait_ge(*xnT_ps(n - 1))
                norm.apply(dve, xn[:, p, :], tile_of(m.X, n), n, p).then_inc(xn_ready.sem, 1)
            if live(n + 1):
                norm.stats(dve, tile_of(m.X, n + 1), n + 1, q)
            if live(n):
                dve.wait_ge(*v_ps(n + 1))
                if past(n, 2):
                    dve.wait_ge(*o_ps(n - 1))
                for b in range(2):
                    vv = dve.tensor_tensor(vbd[:, p, b, :, 0:dh],
                                           J1[:, b * P:(b + 1) * P].rearrange("p (h d) -> p h d", d=dh),
                                           m.vmask[:, :, 0:dh], ALU.mult)
                vv.then_inc(v_ready.sem, 1)
            if live(n - 1):
                t = n - 1
                dve.wait_ge(*scores_ready(t + 1))
                if past(t, 2):
                    dve.wait_ge(*probT_ps(2 * t - 2))
                mxb = mx[:, q, :].rearrange("p (h o) -> p h o", o=1).broadcast_to([P, H, S])
                src, c = sv, 0
                if masked:
                    mb = m.maskbias[:, bass.ds(t, 1), :].broadcast_to([P, H, S])
                    dve.tensor_tensor(prob[:, q], sv, mb, ALU.add).then_inc(max_chain.sem, 1)
                    dve.wait_ge(*max_chain(MC * t + 1))
                    src, c = prob[:, q], 1
                dve.tensor_reduce(mx[:, q, :], src, AX, ALU.max).then_inc(max_chain.sem, 1)
                dve.wait_ge(*max_chain(MC * t + c + 1))
                dve.tensor_tensor(prob[:, q], src, mxb, ALU.subtract).then_inc(sub_ready.sem, 1)
            if live(n - 2):
                t = n - 2
                dve.wait_ge(*o_ps(t + 1))
                ov = pO[:, 0:H * (dh + 1)].rearrange("p (h e) -> p h e", e=dh + 1)
                dve.reciprocal(rc[:, p, :], ov[:, :, dh]).then_inc(rc_chain.sem, 1)
                dve.wait_ge(*rc_chain(RC * t + 1))
                if masked:
                    dve.tensor_scalar(rc[:, p, :], rc[:, p, :], m.rowvalid[:, bass.ds(t, 1)], None,
                                      ALU.mult).then_inc(rc_chain.sem, 1)
                    dve.wait_ge(*rc_chain(RC * t + 2))
                if past(t, 2):
                    dve.wait_ge(*oT_ps(t - 1))
                dve.tensor_tensor(on[:, p, :].rearrange("p (h d) -> p h d", d=dh), ov[:, :, 0:dh],
                                  rc[:, p, :].rearrange("p (h o) -> p h o", o=1).broadcast_to([P, H, dh]),
                                  ALU.mult).then_inc(on_ready.sem, 1)
            if live(n - 3):
                t = n - 3
                dve.wait_ge(*out_ps(t + 1))
                xt = tile_of(m.X, t)
                if bias["o"] is None:
                    dve.tensor_copy(tmp[:, q, :], pP[:, 1, 0:P]).then_inc(tmp_ready.sem, 1)
                else:
                    dve.tensor_tensor(tmp[:, q, :], pP[:, 1, 0:P], bias["o"], ALU.add).then_inc(tmp_ready.sem, 1)
                dve.wait_ge(*tmp_ready(t + 1))
                dve.tensor_tensor(xt, xt, tmp[:, q, :], ALU.add).then_inc(x_done.sem, 1)

        norm.stats(dve, tile_of(m.X, 0), 0, 0)
        pipeline(dve, step, 5, NT - 1, NT + 3)

    L.tensor, L.scalar, L.gpsimd, L.vector = tensor, scalar, gpsimd, vector
    return L


def wide_head_attention(sh, m, tag, start, w):
    nc = sh.nc
    dh = 64
    scale = float(dh) ** -0.5
    L = Layer()
    with ExitStack() as scope:
        def sb(name, shape, dt=F32):
            return scope.enter_context(nc.sbuf_tensor(f"{tag}_{name}", shape, dt))

        outer = Norm(sh, sb, f"{tag}_outer", m)
        inner = Norm(sh, sb, f"{tag}_inner", m, "inner_norm")
        x1 = sb("x1", [P, 2, P])
        xn = sb("xn", [P, 2, P])
        xnT = sb("xnT", [P, 2, P])
        qT = sb("qT", [P, 2, HP, P])
        kbd = sb("kbd", [P, 2, 2, HP, 2, S])
        ctx1 = sb("ctx1", [P, 2, P])
        vbd = sb("vbd", [P, 2, 2, HP, 2, dh])
        prob = sb("prob", [P, 2, H, S])
        probT = sb("probT", [P, 2, HP, P])
        mx = sb("mx", [P, 2, H])
        sm = sb("sm", [P, 2, H])
        rc = sb("rc", [P, 2, H])
        on = sb("on", [P, 2, H * dh])
        oT = sb("oT", [P, 2, HP, P])
        tmp = sb("tmp", [P, 2, P])

    J0, J1 = m.banks[0], m.banks[1]
    pS, pP, pO = m.wide[0], m.wide[1], m.wide[2]
    sv = pS.rearrange("p a (h k) -> p (a h) k", k=S)
    ov = pO.rearrange("p a (h k) -> p (a h) k", k=dh)

    signal = sh.counted_semaphore
    zeros = signal("blocks_zeroed", 2)
    x1_ready, xn_ready, xnT_ready, xnT_ps = signal("x1_ready", NT), signal("xn_ready", NT), signal("xnT_ready", NT), signal("xnT_in_psum", NT)
    q_ps, q_ready = signal("q_in_psum", 2 * NT), signal("q_ready", 2 * NT)
    k_ps, k_ready = signal("k_in_psum", 2 * NT), signal("k_ready", 4 * NT)
    v_ps, v_ready, ctx1_ready = signal("v_in_psum", 2 * NT), signal("v_ready", 4 * NT), signal("ctx1_ready", NT)
    scores_ready, mx_ready, sub_ready = signal("scores_ready", NT), signal("mx_ready", NT), signal("sub_ready", NT)
    prob_ready, probT_ps, probT_ready = signal("prob_ready", NT), signal("probT_in_psum", 2 * NT), signal("probT_ready", 2 * NT)
    o_ps, sm_ready, rc_ready, on_ready = signal("o_in_psum", NT), signal("sm_ready", NT), signal("rc_ready", NT), signal("on_ready", NT)
    oT_ps, oT_ready, out_ps, tmp_ready = signal("oT_in_psum", 2 * NT), signal("oT_ready", 2 * NT), signal("out_in_psum", NT), signal("tmp_ready", NT)
    x_done = signal("x_done", NT)
    L.done = x_done(NT)

    def tensor(pe):
        m.begin(pe, start)

        def keys(t, p):
            for j in range(2):
                if past(t, 1):
                    pe.wait_ge(*q_ready(2 * t - 1 + j))
                for c in range(4):
                    cc = 4 * j + c
                    mm = pe.matmul((J1, J0)[j][:, c * P:(c + 1) * P], w["k"][:, cc * P:(cc + 1) * P],
                                   columns(m.ctxT, t, P), start=True, stop=True)
                mm.then_inc(k_ps.sem, 1)

        def values(t, p):
            pe.wait_ge(*ctx1_ready(t + 1))
            wv = w["v"].rearrange("p (c u d) -> p c u d", u=2, d=dh)
            for b in range(2):
                pe.wait_ge(*k_ready(4 * t + 2 * b + 2))
                for u in range(2):
                    mm = pe.matmul((J1, J0)[b][u * S:(u + 1) * S, :], ctx1[:, p, b * S:(b + 1) * S], wv[:, :, u, :],
                                   start=True, stop=True)
                mm.then_inc(v_ps.sem, 1)

        def turn_x(t, p):
            pe.wait_ge(*xn_ready(t + 1))
            pe.wait_ge(*v_ready(4 * t + 4))
            pe.transpose(J0[:, 0:P], xn[:, p, :], m.ident[:, :]).then_inc(xnT_ps.sem, 1)

        def queries(t, p):
            pe.wait_ge(*xnT_ready(t + 1))
            for j in range(2):
                for c in range(4):
                    cc = 4 * j + c
                    mm = pe.matmul((J1, J0)[j][:, c * P:(c + 1) * P], w["q"][:, cc * P:(cc + 1) * P], xnT[:, p, :],
                                   start=True, stop=True)
                mm.then_inc(q_ps.sem, 1)

        def scores(t, p):
            pe.wait_ge(*q_ready(2 * t + 2))
            if past(t, 1):
                pe.wait_ge(*sub_ready(t))
            for c in range(HP):
                for b in range(2):
                    mm = pe.matmul(pS[b * S:(b + 1) * S, c // 4, c % 4 * P:c % 4 * P + P],
                                   qT[:, p, c, b * S:(b + 1) * S],
                                   kbd[:, p, b, c].rearrange("p u k -> p (u k)"), start=True, stop=True)
            mm.then_inc(scores_ready.sem, 1)

        def turn_probs(t, p):
            pe.wait_ge(*prob_ready(t + 1))
            if past(t, 2):
                pe.wait_ge(*tmp_ready(t - 1))
            elif past(t, 1):
                pe.wait_ge(*probT_ready(2 * t))
            for c in range(HP):
                tr = pe.transpose(pP[:, c // 4, c % 4 * P:c % 4 * P + P],
                                  prob[:, p, 2 * c:2 * c + 2, :].rearrange("p h k -> p (h k)"), m.ident[:, :])
                if c % 4 == 3:
                    tr.then_inc(probT_ps.sem, 1)

        def weigh_values(t, p):
            pe.wait_ge(*probT_ready(2 * t + 2))
            if past(t, 1):
                pe.wait_ge(*on_ready(t))
            for c in range(HP):
                for b in range(2):
                    mm = pe.matmul(pO[b * S:(b + 1) * S, c // 4, c % 4 * P:c % 4 * P + P],
                                   probT[:, p, c, b * S:(b + 1) * S],
                                   vbd[:, p, b, c].rearrange("p u d -> p (u d)"), start=True, stop=True)
            mm.then_inc(o_ps.sem, 1)

        def turn_out(t, p):
            pe.wait_ge(*on_ready(t + 1))
            if before_end(t, 1):
                pe.wait_ge(*probT_ready(2 * t + 4))
            else:
                pe.wait_ge(*tmp_ready(t))
            for c in range(HP):
                tr = pe.transpose(pP[:, c // 4, c % 4 * P:c % 4 * P + P], on[:, p, c * P:(c + 1) * P], m.ident[:, :])
                if c % 4 == 3:
                    tr.then_inc(oT_ps.sem, 1)

        def project(t, p):
            pe.wait_ge(*oT_ready(2 * t + 2))
            for c in range(HP):
                mm = pe.matmul(pP[:, 0, 0:P], oT[:, p, c, :], w["o"][:, c, :], start=(c == 0), stop=(c == HP - 1))
            mm.then_inc(out_ps.sem, 1)

        def step(n, p):
            q = 1 - p
            if live(n - 1):
                turn_x(n - 1, q)
            if live(n - 2):
                turn_probs(n - 2, p)
            if live(n - 1):
                queries(n - 1, q)
            if live(n):
                keys(n, p)
            if live(n - 1):
                scores(n - 1, q)
            if live(n):
                values(n, p)
            if live(n - 3):
                turn_out(n - 3, q)
            if live(n - 2):
                weigh_values(n - 2, p)
            if live(n - 3):
                project(n - 3, q)

        pipeline(pe, step, 5, NT - 1, NT + 3)

    def scalar(act):
        m.begin(act, start)
        act.wait_ge(*zeros(2))

        def step(n, p):
            q = 1 - p
            if live(n - 1):
                t = n - 1
                act.wait_ge(*xnT_ps(t + 1))
                if past(t, 2):
                    act.wait_ge(*q_ps(2 * t - 2))
                act.activation(xnT[:, q, :], J0[:, 0:P], ACT.Identity, bias=w["beta"],
                               scale=w["gamma"]).then_inc(xnT_ready.sem, 1)
            if live(n - 2):
                t = n - 2
                if past(t, 2):
                    act.wait_ge(*o_ps(t - 1))
                for half in range(2):
                    act.wait_ge(*probT_ps(2 * t + half + 1))
                    act.activation(probT[:, p, 4 * half:4 * half + 4, :].rearrange("p c q -> p (c q)"),
                                   pP[:, half, :], ACT.Copy).then_inc(probT_ready.sem, 1)
            if live(n - 1):
                t = n - 1
                if past(t, 2):
                    act.wait_ge(*scores_ready(t - 1))
                for j in range(2):
                    act.wait_ge(*q_ps(2 * t + j + 1))
                    act.activation(qT[:, q, 4 * j:4 * j + 4, :].rearrange("p c q -> p (c q)"), (J1, J0)[j],
                                   ACT.Copy).then_inc(q_ready.sem, 1)
            if live(n):
                t = n
                if past(t, 2):
                    act.wait_ge(*scores_ready(t - 1))
                for j in range(2):
                    act.wait_ge(*k_ps(2 * t + j + 1))
                    for u in range(2):
                        src = (J1, J0)[j][u * S:(u + 1) * S, :].rearrange("p (c b k) -> p b c k", b=2, k=S)
                        act.activation(kbd[u * S:(u + 1) * S, p, :, 4 * j:4 * j + 4, u, :], src,
                                       ACT.Copy).then_inc(k_ready.sem, 1)
            if live(n - 3):
                t = n - 3
                if past(t, 2):
                    act.wait_ge(*out_ps(t - 1))
                for j in range(2):
                    act.wait_ge(*oT_ps(2 * t + j + 1))
                    act.activation(oT[:, q, 4 * j:4 * j + 4, :].rearrange("p c q -> p (c q)"), pP[:, j, :],
                                   ACT.Copy).then_inc(oT_ready.sem, 1)
            if live(n - 1):
                t = n - 1
                act.wait_ge(*sub_ready(t + 1))
                pr = prob[:, q].rearrange("p h k -> p (h k)")
                act.activation(pr, pr, ACT.Exp, scale=scale).then_inc(prob_ready.sem, 1)

        pipeline(act, step, 5, NT - 1, NT + 3)

    def gpsimd(pool):
        m.begin(pool, start)
        pool.memset(kbd[:, :, :, :, :, :].rearrange("p a b c u k -> p (a b c u k)"), 0.0).then_inc(zeros.sem, 1)
        pool.memset(vbd[:, :, :, :, :, :].rearrange("p a b c u k -> p (a b c u k)"), 0.0).then_inc(zeros.sem, 1)

        def context(t, p):
            if past(t, 2):
                pool.wait_ge(*v_ps(2 * t - 2))
            pool.tensor_copy(ctx1[:, p, :], columns(m.ctxT, t, P)).then_inc(ctx1_ready.sem, 1)

        def step(n, p):
            if live(n):
                inner.rstd(pool, n, p, xn_ready)
            if live(n + 1):
                outer.rstd(pool, n + 1, 1 - p, x1_ready)
                context(n + 1, 1 - p)

        outer.rstd(pool, 0, 0, x1_ready)
        context(0, 0)
        pipeline(pool, step, 5, NT - 1, NT + 3)

    def vector(dve):
        m.begin(dve, start)
        dve.wait_ge(*zeros(2))

        def step(n, p):
            q = 1 - p
            if live(n):
                outer.apply(dve, x1[:, p, :], tile_of(m.X, n), n, p).then_inc(x1_ready.sem, 1)
                dve.wait_ge(*x1_ready(n + 1))
                inner.stats(dve, x1[:, p, :], n, p)
            if live(n - 1):
                t = n - 1
                dve.wait_ge(*scores_ready(t + 1))
                if past(t, 2):
                    dve.wait_ge(*probT_ps(2 * t - 2))
                dve.tensor_reduce(mx[:, q, :], sv, AX, ALU.max).then_inc(mx_ready.sem, 1)
                dve.wait_ge(*mx_ready(t + 1))
                dve.tensor_tensor(prob[:, q], sv,
                                  mx[:, q, :].rearrange("p (h o) -> p h o", o=1).broadcast_to([P, H, S]),
                                  ALU.subtract).then_inc(sub_ready.sem, 1)
            if live(n):
                if past(n, 2):
                    dve.wait_ge(*xnT_ps(n - 1))
                inner.apply(dve, xn[:, p, :], x1[:, p, :], n, p).then_inc(xn_ready.sem, 1)
            if live(n + 1):
                outer.stats(dve, tile_of(m.X, n + 1), n + 1, q)
            if live(n):
                if past(n, 2):
                    dve.wait_ge(*o_ps(n - 1))
                for b in range(2):
                    dve.wait_ge(*v_ps(2 * n + b + 1))
                    for u in range(2):
                        src = (J1, J0)[b][u * S:(u + 1) * S, :].rearrange("p (c d) -> p c d", d=dh)
                        dve.tensor_copy(vbd[u * S:(u + 1) * S, p, b, :, u, :], src).then_inc(v_ready.sem, 1)
            if live(n - 2):
                t = n - 2
                dve.wait_ge(*prob_ready(t + 1))
                dve.tensor_reduce(sm[:, p, :], prob[:, p], AX, ALU.add).then_inc(sm_ready.sem, 1)
                dve.wait_ge(*sm_ready(t + 1))
                dve.reciprocal(rc[:, p, :], sm[:, p, :]).then_inc(rc_ready.sem, 1)
                dve.wait_ge(*rc_ready(t + 1))
                dve.wait_ge(*o_ps(t + 1))
                if past(t, 2):
                    dve.wait_ge(*oT_ps(2 * t - 2))
                dve.tensor_tensor(on[:, p, :].rearrange("p (h d) -> p h d", d=dh), ov,
                                  rc[:, p, :].rearrange("p (h o) -> p h o", o=1).broadcast_to([P, H, dh]),
                                  ALU.mult).then_inc(on_ready.sem, 1)
            if live(n - 3):
                t = n - 3
                dve.wait_ge(*out_ps(t + 1))
                xt = tile_of(m.X, t)
                dve.tensor_tensor(tmp[:, q, :], pP[:, 0, 0:P], w["bo"], ALU.add).then_inc(tmp_ready.sem, 1)
                dve.wait_ge(*tmp_ready(t + 1))
                dve.scalar_tensor_tensor(out=xt, in0=tmp[:, q, :], scalar=w["gate"], in1=xt, op0=ALU.mult,
                                         op1=ALU.add).then_inc(x_done.sem, 1)

        outer.stats(dve, tile_of(m.X, 0), 0, 0)
        pipeline(dve, step, 5, NT - 1, NT + 3)

    L.tensor, L.scalar, L.gpsimd, L.vector = tensor, scalar, gpsimd, vector
    return L


def experts(sh, m, tag, start, spec):
    nc = sh.nc
    E, C, gated, router, ER = spec["E"], spec["C"], spec.get("gated"), spec.get("router"), spec.get("ER", 0)
    L = Layer()
    with ExitStack() as scope:
        def sb(name, shape, dt=F32):
            return scope.enter_context(nc.sbuf_tensor(f"{tag}_{name}", shape, dt))

        norm = Norm(sh, sb, f"{tag}_ln", m)
        xn = sb("xn", [P, 2, P])
        XNT = sb("XNT", [P, TOK])
        w1 = sb("w1", [P, 2, (2 if gated else 1) * C * P])
        w2 = sb("w2", [P, 2, C, D])
        h = sb("h", [P, 2, C, GW])
        rtile = sb("rtile", [P, 2, P])
        if gated:
            raw = sb("raw", [P, 2, 3, C * P])
            sg = sb("sg", [P, 2, GW])
        if router:
            LG = sb("logits", [P, NT, ER])
            gates = sb("gates", [P, NT, E])
            A, Bt, Ct, O1, O2 = (sb(f"work{i}", [P, NT, ER]) for i in range(5))
            m1, m2, rm, ws, wa, wb = (sb(f"row{i}", [P, NT]) for i in range(6))
        if router and spec.get("b2"):
            R = P // E
            gT = sb("gT", [P, E * NT // P, P])
            b2sel = sb("b2sel", [P, R, D])

    J0, J1 = m.banks[0], m.banks[1]
    ring = m.banks[2:6]
    Y = [m.banks[6], m.banks[7]]

    signal = sh.counted_semaphore
    b2 = bool(router and spec.get("b2"))
    EXPS = (2 if spec["whole"] else 1) if router else 0
    LINKS = (17 if E > ER else 16) if router else 0
    ND = 5 if gated else 2
    units = NG * E
    xn_ready, xnT_ps, xnT_ready = signal("xn_ready", NT), signal("xnT_in_psum", NT), signal("xnT_ready", NT)
    rtile_ready, lg_ps, lg_ready = signal("rtile_ready", NT if router else 0), signal("logits_in_psum", NT if router else 0), signal("logits_ready", NT if router else 0)
    x_plus = signal("x_plus_norm", NT if spec.get("residual") else 0)
    g_chain, exp_in, exp_out, gates_ready = signal("gates_chain", LINKS), signal("exp_in", EXPS), signal("exp_out", EXPS), signal("gates_ready", 1 if router else 0)
    gT_ps, gT_ready, b2_ps, b2_added, sel_ready = (signal("gT_in_psum", 1 if b2 else 0), signal("gT_ready", 1 if b2 else 0), signal("b2_in_psum", NG if b2 else 0),
                                                   signal("b2_added", NG if b2 or not router else 0), signal("b2sel_ready", R if b2 else 0))
    w_loaded = [signal("w_loaded_even", ND * 16 * ((E + 1) // 2)), signal("w_loaded_odd", ND * 16 * (E // 2))]
    w_turned_ps, w_turned, zeroed = signal("w_turned_ps", 3 * E if gated else 0), signal("w_turned", 3 * E if gated else 0), signal("raw_zeroed", 1 if gated else 0)
    a_ps, s_ready, h_ready, y_ps, combined = (signal("hidden_in_psum", units * C), signal("silu_ready", units * C if gated else 0), signal("h_ready", units * C),
                                              signal("y_in_psum", units), signal("combined", units))
    L.done = combined(units)

    def over_experts(eng, one, middle):
        if E == 1:
            one(0, 0)
            return
        one(0, 0)
        one(1, 1)
        with eng.Fori(2, E - 3, 2) as e:
            one(e, 0)
            one(e + 1, 1)
        middle()
        one(E - 2, 0)
        one(E - 1, 1)

    def order(first, second):
        first(0)
        for g in range(1, NG):
            first(g)
            second(g - 1)
        second(NG - 1)

    def has(e, k):
        return not isinstance(e, int) or e >= k

    def has_next(e):
        return not isinstance(e, int) or e < E - 1

    def loads(e, p):
        return ND * 8 * (e - p) + ND * 16

    def sync(sp):
        m.begin(sp, start)
        if gated:
            sp.wait_ge(*zeroed(1))

        def one(e, p):
            if has(e, 2):
                if gated:
                    sp.wait_ge(*w_turned_ps(3 * e - 3))
                else:
                    sp.wait_ge(*y_ps(NG * e - NG))
            if gated:
                for k in range(2):
                    src = spec["weights"][k][bass.ds(e, 1)].rearrange("o i h -> (o i) h")
                    sp.dma_start(raw[:, p, k, 0:2 * P].rearrange("p (c h) -> p c h", h=P),
                                 src[0:2 * P, :].rearrange("(c p) h -> p c h", p=P)).then_inc(w_loaded[p].sem, 16)
                    sp.dma_start(raw[0:96, p, k, 2 * P:3 * P], src[2 * P:352, :]).then_inc(w_loaded[p].sem, 16)
                sp.dma_start(raw[:, p, 2, 0:352], spec["weights"][2][bass.ds(e, 1)].rearrange("o h i -> (o h) i")
                             ).then_inc(w_loaded[p].sem, 16)
            else:
                s1, s2, ee = spec["weights"](e)
                sp.dma_start(w1[:, p, :], s1[bass.ds(ee, 1)].rearrange("o d f -> (o d) f")).then_inc(w_loaded[p].sem, 16)
                sp.dma_start(w2[:, p, :, :], s2[bass.ds(ee, 1)].rearrange("o (c p) d -> p (o c) d", p=P)
                             ).then_inc(w_loaded[p].sem, 16)

        over_experts(sp, one, lambda: None)

    def tensor(pe):
        m.begin(pe, start)

        def turn_x(t, p):
            pe.wait_ge(*xn_ready(t + 1))
            if past(t, 1):
                pe.wait_ge(*xnT_ready(t))
            pe.transpose(J0[:, 0:P], xn[:, p, :], m.ident[:, :]).then_inc(xnT_ps.sem, 1)

        def route(t, p):
            pe.wait_ge(*rtile_ready(t + 1))
            if past(t, 1):
                pe.wait_ge(*lg_ready(t))
            pe.matmul(J1[:, 0:ER], rtile[:, p, :], spec["wr"], start=True, stop=True).then_inc(lg_ps.sem, 1)

        def step(n, p):
            if live(n - 1):
                turn_x(n - 1, 1 - p)
            if router and live(n - 2):
                route(n - 2, p)

        pipeline(pe, step, 5, NT - 1, NT + 2)
        pe.wait_ge(*xnT_ready(NT))

        def turn_weights(e, p):
            pe.wait_ge(*w_loaded[p](loads(e, p)))
            for k in range(3):
                if has(e, 1) or k == 2:
                    pe.wait_ge(*w_turned(3 * e + k - (1 if k == 2 else 2) if k != 2 else 3 * e + 1))
                elif router:
                    pe.wait_ge(*lg_ready(NT))
                for c in range(C):
                    tr = pe.transpose((J0, J1, J0)[k][:, c * P:(c + 1) * P], raw[:, p, k, c * P:(c + 1) * P],
                                      m.ident[:, :])
                tr.then_inc(w_turned_ps.sem, 1)

        if gated:
            turn_weights(0, 0)

        def one(e, p):
            if gated:
                pe.wait_ge(*w_turned(3 * e + 3))
            else:
                pe.wait_ge(*w_loaded[p](loads(e, p)))

            def first(g):
                x = XNT[:, g * GW:(g + 1) * GW]
                for c in range(C):
                    k = C * NG * e + C * g + c
                    if gated:
                        if has(e, 1) or C * g + c >= 2:
                            pe.wait_ge(*h_ready(k - 1))
                        b = (C * g + c) % 2 * 2
                        pe.matmul(ring[b], w1[:, p, c * P:(c + 1) * P], x, start=True, stop=True)
                        pe.matmul(ring[b + 1], w1[:, p, (C + c) * P:(C + c + 1) * P], x, start=True,
                                  stop=True).then_inc(a_ps.sem, 1)
                    else:
                        if has(e, 1) or C * g + c >= 4:
                            pe.wait_ge(*h_ready(k - 3))
                        pe.matmul(ring[(C * g + c) % 4], w1[:, p, c * P:(c + 1) * P], x, start=True,
                                  stop=True).then_inc(a_ps.sem, 1)
                if gated and g == 1 and has_next(e):
                    turn_weights(e + 1, 1 - p)

            def second(g):
                u = NG * e + g
                for c in range(C):
                    pe.wait_ge(*h_ready(C * u + c + 1))
                    if c == 0 and (has(e, 1) or g >= 2):
                        pe.wait_ge(*combined(u - 1))
                    for i in range(GT):
                        mm = pe.matmul(Y[g % 2][:, i * P:(i + 1) * P], h[:, g % 2, c, i * P:(i + 1) * P],
                                       w2[:, p, c, :], start=(c == 0 and i == 0), stop=(c == C - 1),
                                       skip_group_check=True)
                mm.then_inc(y_ps.sem, 1)

            order(first, second)

        def middle():
            if not (router and spec.get("b2")):
                return
            pe.wait_ge(*gates_ready(1))
            pe.wait_ge(*sel_ready(R))
            gv = gates[:, :, :].rearrange("p t e -> p (t e)")
            for j in range(E * NT // P):
                tr = pe.transpose(J0[:, j * P:(j + 1) * P], gv[:, j * P:(j + 1) * P], m.ident[:, :])
            tr.then_inc(gT_ps.sem, 1)
            pe.wait_ge(*gT_ready(1))
            for g in range(NG):
                if g >= 1:
                    pe.wait_ge(*b2_added(g))
                lo = g * GT % R
                pe.matmul(J1[:, :], gT[:, g * GT // R, :], b2sel[:, lo:lo + GT, :].rearrange("p t d -> p (t d)"),
                          start=True, stop=True).then_inc(b2_ps.sem, 1)

        over_experts(pe, one, middle)

    def scalar(act):
        m.begin(act, start)

        def step(n, p):
            q = 1 - p
            if live(n - 1):
                t = n - 1
                act.wait_ge(*xnT_ps(t + 1))
                if router == "x":
                    if past(t, 2):
                        act.wait_ge(*lg_ps(t - 1))
                    act.activation(rtile[:, q, :], J0[:, 0:P], ACT.Copy).then_inc(rtile_ready.sem, 1)
                apart(act, m)
                act.activation(columns(XNT, t, P), J0[:, 0:P], ACT.Copy).then_inc(xnT_ready.sem, 1)

        pipeline(act, step, 5, NT - 1, NT + 2)
        if router:
            act.wait_ge(*exp_in(1))
            act.activation(wb[:, :], wb[:, :], ACT.Exp).then_inc(exp_out.sem, 1)
            if spec["whole"]:
                act.wait_ge(*exp_in(2))
                act.activation(A[:, :, :], A[:, :, :], ACT.Exp).then_inc(exp_out.sem, 1)

        def turned(e, p):
            for k in range(3):
                act.wait_ge(*w_turned_ps(3 * e + k + 1))
                if has(e, 2) and k == 0:
                    act.wait_ge(*y_ps(NG * e - NG))
                dst = w2[:, p].rearrange("p c d -> p (c d)") if k == 2 else w1[:, p, k * C * P:(k + 1) * C * P]
                act.activation(dst, (J0, J1, J0)[k][:, 0:C * P], ACT.Copy).then_inc(w_turned.sem, 1)

        if gated:
            turned(0, 0)

        def one(e, p):
            if not gated:
                act.wait_ge(*w_loaded[p](loads(e, p)))

            def first(g):
                u = NG * e + g
                for c in range(C):
                    k = C * u + c
                    act.wait_ge(*a_ps(k + 1))
                    if gated:
                        if has(e, 1) or C * g + c >= 2:
                            act.wait_ge(*h_ready(k - 1))
                        b = (C * g + c) % 2
                        act.activation(sg[:, b, :], ring[2 * b], ACT.Silu).then_inc(s_ready.sem, 1)
                    else:
                        if c == 0 and (has(e, 1) or g >= 2):
                            act.wait_ge(*y_ps(u - 1))
                        apart(act, m)
                        act.activation(h[:, g % 2, c, :], ring[(C * g + c) % 4], spec["func"],
                                       bias=spec["b1"][:, bass.ds(e * C + c, 1)]).then_inc(h_ready.sem, 1)
                if gated and g == 1 and has_next(e):
                    turned(e + 1, 1 - p)

            order(first, lambda g: None)

        def middle():
            if router and spec.get("b2"):
                act.wait_ge(*gT_ps(1))
                act.activation(gT[:, :, :].rearrange("p j q -> p (j q)"), J0[:, 0:E * NT // P * P],
                               ACT.Copy).then_inc(gT_ready.sem, 1)

        over_experts(act, one, middle)

    def gpsimd(pool):
        m.begin(pool, start)
        if gated:
            pool.memset(raw[:, :, :, :].rearrange("p a k f -> p (a k f)"), 0.0).then_inc(zeroed.sem, 1)
        if router and spec.get("b2"):
            for t in range(R):
                pool.tensor_scalar(b2sel[:, t, :], spec["b2rep"][:, :], spec["tmask"][:, t:t + 1], None,
                                   ALU.mult).then_inc(sel_ready.sem, 1)

        def context(t, p):
            if past(t, 2):
                pool.wait_ge(*lg_ps(t - 1))
            pool.tensor_copy(rtile[:, p, :], columns(m.ctxT, t, P)).then_inc(rtile_ready.sem, 1)

        def step(n, p):
            if live(n):
                if router == "ctx":
                    context(n, p)
            if live(n + 1):
                norm.rstd(pool, n + 1, 1 - p, xn_ready)

        norm.rstd(pool, 0, 0, xn_ready)
        pipeline(pool, step, 5, NT - 1, NT + 2)

    def vector(dve):
        m.begin(dve, start)

        def step(n, p):
            if live(n):
                if past(n, 2):
                    dve.wait_ge(*xnT_ps(n - 1))
                xt = tile_of(m.X, n)
                norm.apply(dve, xn[:, p, :], xt, n, p).then_inc(xn_ready.sem, 1)
            if live(n + 1):
                norm.stats(dve, tile_of(m.X, n + 1), n + 1, 1 - p)
            if live(n) and spec.get("residual"):
                dve.wait_ge(*xn_ready(n + 1))
                dve.tensor_tensor(xt, xt, xn[:, p, :], ALU.add).then_inc(x_plus.sem, 1)
            if router and live(n - 2):
                t = n - 2
                dve.wait_ge(*lg_ps(t + 1))
                dst = tile_of(LG, t)
                if spec.get("br") is None:
                    dve.tensor_copy(dst, J1[:, 0:ER]).then_inc(lg_ready.sem, 1)
                else:
                    dve.tensor_tensor(dst, J1[:, 0:ER], spec["br"], ALU.add).then_inc(lg_ready.sem, 1)

        norm.stats(dve, tile_of(m.X, 0), 0, 0)
        pipeline(dve, step, 5, NT - 1, NT + 2)

        links = [0]

        def link(ins):
            ins.then_inc(g_chain.sem, 1)
            links[0] += 1
            dve.wait_ge(*g_chain(links[0]))

        def wide(r):
            return r[:, :].rearrange("p (t o) -> p t o", o=1).broadcast_to([P, NT, ER])

        def take_best(logits, best, onehot):
            link(dve.tensor_reduce(best[:, :], logits[:, :, :], AX, ALU.max))
            link(dve.tensor_tensor(Bt[:, :, :], logits[:, :, :], wide(best), ALU.is_ge))
            rev = m.rev[:, 16 - ER:16].rearrange("p (o e) -> p o e", o=1).broadcast_to([P, NT, ER])
            link(dve.tensor_tensor(Bt[:, :, :], Bt[:, :, :], rev, ALU.mult))
            link(dve.tensor_reduce(rm[:, :], Bt[:, :, :], AX, ALU.max))
            link(dve.tensor_tensor(onehot[:, :, :], Bt[:, :, :], wide(rm), ALU.is_equal))

        dve.wait_ge(*xn_ready(NT))
        if router:
            dve.wait_ge(*lg_ready(NT))
            if spec.get("residual"):
                dve.wait_ge(*x_plus(NT))
            take_best(LG, m1, O1)
            link(dve.scalar_tensor_tensor(out=Ct[:, :, :].rearrange("p t e -> p (t e)"),
                                          in0=O1[:, :, :].rearrange("p t e -> p (t e)"), scalar=NEG,
                                          in1=LG[:, :, :].rearrange("p t e -> p (t e)"), op0=ALU.mult, op1=ALU.add))
            take_best(Ct, m2, O2)
            dve.tensor_tensor(wb[:, :], m2[:, :], m1[:, :], ALU.subtract).then_inc(exp_in.sem, 1)
            if spec["whole"]:
                dve.tensor_tensor(A[:, :, :], LG[:, :, :], wide(m1), ALU.subtract).then_inc(exp_in.sem, 1)
                dve.wait_ge(*exp_out(2))
                link(dve.tensor_reduce(ws[:, :], A[:, :, :], AX, ALU.add))
            else:
                dve.wait_ge(*exp_out(1))
                link(dve.tensor_scalar(ws[:, :], wb[:, :], 1.0, None, ALU.add))
            link(dve.reciprocal(wa[:, :], ws[:, :]))
            link(dve.tensor_tensor(wb[:, :], wb[:, :], wa[:, :], ALU.mult))
            link(dve.tensor_tensor(O1[:, :, :], O1[:, :, :], wide(wa), ALU.mult))
            link(dve.tensor_tensor(O2[:, :, :], O2[:, :, :], wide(wb), ALU.mult))
            if E > ER:
                link(dve.memset(gates[:, :, ER:E], 1.0))
            dve.tensor_tensor(gates[:, :, 0:ER], O1[:, :, :], O2[:, :, :], ALU.add).then_inc(gates_ready.sem, 1)
            dve.wait_ge(*gates_ready(1))
            assert links[0] == LINKS
        else:
            for g in range(NG):
                xg = m.X[:, g * GT:(g + 1) * GT, :]
                dve.tensor_tensor(xg, xg, spec["bo"].rearrange("p (o d) -> p o d", o=1).broadcast_to([P, GT, D]),
                                  ALU.add).then_inc(b2_added.sem, 1)
            dve.wait_ge(*b2_added(NG))

        def one(e, p):
            def first(g):
                if not gated:
                    return
                u = NG * e + g
                for c in range(C):
                    dve.wait_ge(*s_ready(C * u + c + 1))
                    if c == 0 and (has(e, 1) or g >= 2):
                        dve.wait_ge(*y_ps(u - 1))
                    b = (C * g + c) % 2
                    dve.tensor_tensor(h[:, g % 2, c, :], sg[:, b, :], ring[2 * b + 1], ALU.mult).then_inc(h_ready.sem, 1)

            def second(g):
                u = NG * e + g
                dve.wait_ge(*y_ps(u + 1))
                if has(e, 1):
                    dve.wait_ge(*combined(u - NG + 1))
                if not router:
                    xg = m.X[:, g * GT:(g + 1) * GT, :].rearrange("p t d -> p (t d)")
                    dve.tensor_tensor(xg, xg, Y[g % 2], ALU.add).then_inc(combined.sem, 1)
                    return
                for i in range(GT):
                    t = g * GT + i
                    st = dve.scalar_tensor_tensor(out=m.X[:, t, :], in0=Y[g % 2][:, i * P:(i + 1) * P],
                                                  scalar=gates[:, t, bass.ds(e, 1)], in1=m.X[:, t, :],
                                                  op0=ALU.mult, op1=ALU.add)
                st.then_inc(combined.sem, 1)

            order(first, second)

        def middle():
            if router and spec.get("b2"):
                dve.wait_ge(*combined(NG * (E - 2)))
                for g in range(NG):
                    dve.wait_ge(*b2_ps(g + 1))
                    xg = m.X[:, g * GT:(g + 1) * GT, :].rearrange("p t d -> p (t d)")
                    dve.tensor_tensor(xg, xg, J1[:, :], ALU.add).then_inc(b2_added.sem, 1)
                dve.wait_ge(*b2_added(NG))

        over_experts(dve, one, middle)

    L.tensor, L.scalar, L.gpsimd, L.vector, L.sync = tensor, scalar, gpsimd, vector, sync
    return L


def quantised_ffn(sh, m, tag, start, w):
    nc = sh.nc
    C = 3
    K = C * NG
    QMAX = 32767.0
    L = Layer()
    with ExitStack() as scope:
        def sb(name, shape, dt=F32):
            return scope.enter_context(nc.sbuf_tensor(f"{tag}_{name}", shape, dt))

        norm = Norm(sh, sb, f"{tag}_ln", m)
        xn = sb("xn", [P, 2, P])
        XNT = sb("XNT", [P, TOK])
        G, U, SG = (sb(name, [P, K, GW]) for name in ("gate", "up", "sig"))
        am = sb("amax", [P, 5, 2 * K])
        a1, b1 = sb("amax_rows", [P, 5]), sb("amax_all", [P, 5])
        scale, inv = sb("scale", [P, 5]), sb("inv", [P, 5])
        us = sb("up_times_gate_scale", [P, 1])

    J0, J1 = m.banks[0], m.banks[1]
    signal = sh.counted_semaphore
    xn_ready, xnT_ps, xnT_ready, xmax = signal("xn_ready", NT), signal("xnT_in_psum", NT), signal("xnT_ready", NT), signal("x_max", NT)
    rows_max, turned, one_max, spread_ps = signal("rows_max", 5), signal("rows_turned", 5), signal("one_max", 5), signal("max_spread", 5)
    scale_set, inv_set, us_set = signal("scale_set", 5), signal("inv_set", 5), signal("us_set", 1)
    x_a, x_q = signal("x_scaled", NG), signal("x_quantised", NG)
    gu_ps, gu_here, gu_max = signal("gate_up_in_psum", 2 * K), signal("gate_up_here", 2 * K), signal("gate_up_max", 2 * K)
    g_a, g_q, sig, sig_a, sig_q = (signal("gate_scaled", K), signal("gate_quantised", K), signal("sigmoid", K), signal("sigmoid_scaled", K),
                                   signal("sigmoid_quantised", K))
    gs, gs_max = signal("gated", K), signal("gated_max", K)
    gs_a, u_a, u_q, o_here, o_max = (signal("gated_scaled", K), signal("up_scaled", K), signal("up_quantised", K), signal("o_here", K),
                                     signal("o_max", K))
    o_a, o_q, y_ps, x_done = signal("o_scaled", K), signal("o_quantised", K), signal("y_in_psum", NG), signal("x_done", NG)
    X_, G_, U_, S_, O_ = range(5)
    L.done = x_done(NG)

    def piece(x, k):
        return x[:, bass.ds(k, 1), :].rearrange("p o f -> p (o f)")

    def passes(eng, step, n, lag):
        for i in range(lag):
            step(i)
        with eng.Fori(lag, n) as i:
            step(i)
        for i in range(n, n + lag):
            step(i)

    def on(k):
        return not isinstance(k, int) or 0 <= k < K

    def quantise(dve, x, r, by=None):
        s = scale[:, r:r + 1] if by is None else by
        return dve.tensor_scalar(x, x, ROUND, s, ALU.subtract, ALU.mult)

    def tensor(pe):
        m.begin(pe, start)

        def turn_x(t, p):
            pe.wait_ge(*xn_ready(t + 1))
            if past(t, 1):
                pe.wait_ge(*xnT_ready(t))
            pe.transpose(J0[:, 0:P], xn[:, p, :], m.ident[:, :]).then_inc(xnT_ps.sem, 1)

        def step(n, p):
            if live(n - 1):
                turn_x(n - 1, 1 - p)

        pipeline(pe, step, 5, NT - 1, NT + 1)
        pe.wait_ge(*xnT_ready(NT))

        def spread_max(r):
            pe.wait_ge(*rows_max(r + 1))
            pe.transpose(J0[0:1, 0:P], a1[:, r:r + 1], m.ident[:, :]).then_inc(turned.sem, 1)
            pe.wait_ge(*one_max(r + 1))
            pe.matmul(J1[:, 0:1], m.ones[0:1, :], b1[0:1, r:r + 1], start=True, stop=True).then_inc(spread_ps.sem, 1)

        spread_max(X_)

        def gate_up(g):
            pe.wait_ge(*x_q(g + 1))
            for j in range(2 * C):
                if not isinstance(g, int) or g >= 1:
                    pe.wait_ge(*gu_here(2 * C * g - 2 * C + j + 1))
                pe.matmul(m.banks[2 + j], w["gu"][:, j * P:(j + 1) * P], columns(XNT, g, GW), start=True,
                          stop=True).then_inc(gu_ps.sem, 1)

        gate_up(0)
        with pe.Fori(1, NG) as g:
            gate_up(g)
        for r in (G_, U_, S_, O_):
            spread_max(r)
        for g in range(NG):
            for c in range(C):
                pe.wait_ge(*o_q(C * g + c + 1))
                if c == 0 and g >= 2:
                    pe.wait_ge(*x_done(g - 1))
                for i in range(GT):
                    mm = pe.matmul(m.banks[2 + g % 2][:, i * P:(i + 1) * P], G[:, C * g + c, i * P:(i + 1) * P],
                                   w["d"][:, c * P:(c + 1) * P], start=(c == 0 and i == 0), stop=(c == C - 1),
                                   skip_group_check=True)
            mm.then_inc(y_ps.sem, 1)

    def scalar(act):
        m.begin(act, start)

        def step(n, p):
            if live(n - 1):
                act.wait_ge(*xnT_ps(n))
                apart(act, m)
                act.activation(columns(XNT, n - 1, P), J0[:, 0:P], ACT.Copy).then_inc(xnT_ready.sem, 1)

        pipeline(act, step, 5, NT - 1, NT + 1)

        def gate_up(g):
            for j in range(2 * C):
                act.wait_ge(*gu_ps(2 * C * g + j + 1))
                apart(act, m)
                act.activation(piece((G, U)[j // C], C * g + j % C), m.banks[2 + j], ACT.Copy).then_inc(gu_here.sem, 1)

        with act.Fori(0, NG) as g:
            gate_up(g)

        def scaled(x, r, done):
            act.activation(x, x, ACT.Identity, bias=m.round[:, 0:1], scale=inv[:, r:r + 1]).then_inc(done.sem, 1)

        act.wait_ge(*inv_set(G_ + 1))
        act.wait_ge(*gu_here(2 * K))

        def gate_pass(n):
            if on(n):
                scaled(piece(G, n), G_, g_a)
            if on(n - 1):
                act.wait_ge(*g_q(n))
                apart(act, m)
                act.activation(piece(SG, n - 1), piece(G, n - 1), ACT.Sigmoid).then_inc(sig.sem, 1)
            if on(n - 2):
                act.wait_ge(*sig(n - 1))
                apart(act, m)
                act.activation(piece(SG, n - 2), piece(SG, n - 2), ACT.Identity, bias=m.round[:, 0:1],
                               scale=65536.0).then_inc(sig_a.sem, 1)

        passes(act, gate_pass, K, 2)
        act.wait_ge(*inv_set(U_ + 1))
        with act.Fori(0, K) as k:
            scaled(piece(U, k), U_, u_a)
        act.wait_ge(*inv_set(S_ + 1))
        with act.Fori(0, K) as k:
            scaled(piece(G, k), S_, gs_a)
        act.wait_ge(*inv_set(O_ + 1))
        with act.Fori(0, K) as k:
            scaled(piece(G, k), O_, o_a)

    def gpsimd(pool):
        m.begin(pool, start)

        def step(n, p):
            if live(n + 1):
                norm.rstd(pool, n + 1, 1 - p, xn_ready)

        norm.rstd(pool, 0, 0, xn_ready)
        pipeline(pool, step, 5, NT - 1, NT + 1)

    def vector(dve):
        m.begin(dve, start)

        def step(n, p):
            if live(n):
                if past(n, 2):
                    dve.wait_ge(*xnT_ps(n - 1))
                    dve.wait_ge(*xmax(n - 1))
                norm.apply(dve, xn[:, p, :], tile_of(m.X, n), n, p).then_inc(xn_ready.sem, 1)
            if live(n + 1):
                norm.stats(dve, tile_of(m.X, n + 1), n + 1, 1 - p)
            if live(n):
                dve.wait_ge(*xn_ready(n + 1))
                dve.tensor_reduce(am[:, X_, bass.ds(n, 1)], xn[:, p, :], AX, ALU.max,
                                  apply_absolute_value=True).then_inc(xmax.sem, 1)

        norm.stats(dve, tile_of(m.X, 0), 0, 0)
        pipeline(dve, step, 5, NT - 1, NT + 1)

        def find_scale(r, src, seen, count):
            dve.wait_ge(*seen(count))
            dve.tensor_reduce(a1[:, r:r + 1], src, AX, ALU.max).then_inc(rows_max.sem, 1)
            dve.wait_ge(*turned(r + 1))
            dve.tensor_reduce(b1[0:1, r:r + 1], J0[0:1, 0:P], AX, ALU.max).then_inc(one_max.sem, 1)
            dve.wait_ge(*spread_ps(r + 1))
            dve.tensor_scalar(scale[:, r:r + 1], J1[:, 0:1], 1.0 / QMAX, 1e-12, ALU.mult, ALU.max).then_inc(scale_set.sem, 1)
            dve.wait_ge(*scale_set(r + 1))
            dve.reciprocal(inv[:, r:r + 1], scale[:, r:r + 1]).then_inc(inv_set.sem, 1)
            dve.wait_ge(*inv_set(r + 1))

        find_scale(X_, am[:, X_, 0:NT], xmax, NT)
        dve.wait_ge(*xnT_ready(NT))

        def quantise_x(n):
            if isinstance(n, int) and n >= NG:
                pass
            else:
                dve.tensor_scalar(columns(XNT, n, GW), columns(XNT, n, GW), inv[:, X_:X_ + 1], ROUND, ALU.mult,
                                  ALU.add).then_inc(x_a.sem, 1)
            if not isinstance(n, int) or n >= 1:
                dve.wait_ge(*x_a(n))
                quantise(dve, columns(XNT, n - 1, GW), X_).then_inc(x_q.sem, 1)

        passes(dve, quantise_x, NG, 1)

        def greatest(g):
            for j in range(2 * C):
                dve.wait_ge(*gu_here(2 * C * g + j + 1))
                dve.tensor_reduce(am[:, (G_, U_)[j // C], bass.ds(C * g + j % C, 1)],
                                  piece((G, U)[j // C], C * g + j % C), AX, ALU.max,
                                  apply_absolute_value=True).then_inc(gu_max.sem, 1)

        with dve.Fori(0, NG) as g:
            greatest(g)
        find_scale(G_, am[:, G_, 0:K], gu_max, 2 * K)
        find_scale(U_, am[:, U_, 0:K], gu_max, 2 * K)

        def gate_pass(n):
            if on(n):
                dve.wait_ge(*g_a(n + 1))
                quantise(dve, piece(G, n), G_).then_inc(g_q.sem, 1)
            if on(n - 2):
                k = n - 2
                dve.wait_ge(*sig_a(k + 1))
                dve.tensor_scalar(piece(SG, k), piece(SG, k), ROUND, 65535.0, ALU.subtract, ALU.min).then_inc(sig_q.sem, 1)
            if on(n - 3):
                k = n - 3
                dve.wait_ge(*sig_q(k + 1))
                dve.scalar_tensor_tensor(out=piece(G, k), in0=piece(SG, k), scalar=1.0 / 65536.0, in1=piece(G, k),
                                         op0=ALU.mult, op1=ALU.mult).then_inc(gs.sem, 1)
            if on(n - 4):
                k = n - 4
                dve.wait_ge(*gs(k + 1))
                dve.tensor_reduce(am[:, S_, bass.ds(k, 1)], piece(G, k), AX, ALU.max,
                                  apply_absolute_value=True).then_inc(gs_max.sem, 1)

        passes(dve, gate_pass, K, 4)
        find_scale(S_, am[:, S_, 0:K], gs_max, K)
        dve.tensor_tensor(us[:, :], scale[:, U_:U_ + 1], scale[:, S_:S_ + 1], ALU.mult).then_inc(us_set.sem, 1)
        dve.wait_ge(*us_set(1))

        def o_pass(n):
            if on(n):
                dve.wait_ge(*u_a(n + 1))
                quantise(dve, piece(U, n), U_, us[:, 0:1]).then_inc(u_q.sem, 1)
            if on(n - 1):
                k = n - 1
                dve.wait_ge(*u_q(k + 1))
                dve.wait_ge(*gs_a(k + 1))
                dve.scalar_tensor_tensor(out=piece(G, k), in0=piece(G, k), scalar=ROUND, in1=piece(U, k),
                                         op0=ALU.subtract, op1=ALU.mult).then_inc(o_here.sem, 1)
            if on(n - 2):
                k = n - 2
                dve.wait_ge(*o_here(k + 1))
                dve.tensor_reduce(am[:, O_, bass.ds(k, 1)], piece(G, k), AX, ALU.max,
                                  apply_absolute_value=True).then_inc(o_max.sem, 1)

        passes(dve, o_pass, K, 2)
        find_scale(O_, am[:, O_, 0:K], o_max, K)
        with dve.Fori(0, K) as k:
            dve.wait_ge(*o_a(k + 1))
            quantise(dve, piece(G, k), O_).then_inc(o_q.sem, 1)
        for g in range(NG):
            dve.wait_ge(*y_ps(g + 1))
            xg = m.X[:, g * GT:(g + 1) * GT, :].rearrange("p t d -> p (t d)")
            dve.tensor_tensor(xg, xg, m.banks[2 + g % 2], ALU.add).then_inc(x_done.sem, 1)

    L.tensor, L.scalar, L.gpsimd, L.vector = tensor, scalar, gpsimd, vector
    return L


def block_quantised_weights(sh, m, ins, load, loaded, count):
    C, NB = 3, 12
    raw, q = sh.sb("qw_raw", [P, 3, C * P]), sh.sb("qw_rounded", [P, 3, C * P])
    s, rs = sh.sb("qw_scale", [P, 3, NB]), sh.sb("qw_inverse", [P, 3, NB])
    gu, d = sh.sb("qw_gate_up", [P, 2 * C * P]), sh.sb("qw_down", [P, C * P])
    for k, name in enumerate(("gate", "up")):
        load(raw[:, k, :].rearrange("p (c h) -> p c h", h=P), ins[f"L3_ffn_w_{name}"].rearrange("(c p) h -> p c h", p=P))
    load(raw[:, 2, :], ins["L3_ffn_w_down"])
    chain = sh.sem("qw_chain")
    turned_ps, turned = sh.sem("qw_turned_ps"), sh.sem("qw_turned")
    flat = lambda x: x[:, :, :].rearrange("p k f -> p (k f)")
    blocks = lambda x: flat(x).rearrange("p (n b) -> p n b", b=32)
    spread = lambda x: flat(x).rearrange("p (n o) -> p n o", o=1).broadcast_to([P, 3 * NB, 32])

    def vector(dve):
        dve.wait_ge(loaded, count())
        dve.tensor_reduce(flat(s), blocks(raw), AX, ALU.max, apply_absolute_value=True).then_inc(chain, 1)
        dve.wait_ge(chain, 1)
        dve.tensor_scalar(flat(s), flat(s), 1.0 / 7.0, 1e-12, ALU.mult, ALU.max).then_inc(chain, 1)
        dve.wait_ge(chain, 2)
        dve.reciprocal(flat(rs), flat(s)).then_inc(chain, 1)
        dve.wait_ge(chain, 3)
        dve.tensor_tensor(blocks(q), blocks(raw), spread(rs), ALU.mult).then_inc(chain, 1)
        dve.wait_ge(chain, 4)
        dve.tensor_scalar(flat(q), flat(q), ROUND, ROUND, ALU.add, ALU.subtract).then_inc(chain, 1)
        dve.wait_ge(chain, 5)
        dve.tensor_scalar(flat(q), flat(q), 7.0, -8.0, ALU.min, ALU.max).then_inc(chain, 1)
        dve.wait_ge(chain, 6)
        dve.tensor_tensor(blocks(q), blocks(q), spread(s), ALU.mult).then_inc(chain, 1)

    def tensor(pe):
        pe.wait_ge(chain, 7)
        for k in range(3):
            if k >= 1:
                pe.wait_ge(turned, k)
            for c in range(C):
                tr = pe.transpose(m.banks[4][:, c * P:(c + 1) * P], q[:, k, c * P:(c + 1) * P], m.ident[:, :])
            tr.then_inc(turned_ps, 1)

    def scalar(act):
        for k in range(3):
            act.wait_ge(turned_ps, k + 1)
            dst = d[:, :] if k == 2 else gu[:, k * C * P:(k + 1) * C * P]
            act.activation(dst, m.banks[4][:, 0:C * P], ACT.Copy).then_inc(turned, 1)

    L = Layer()
    L.tensor, L.scalar, L.vector, L.done = tensor, scalar, vector, (turned, 3)
    return L, {"gu": gu, "d": d}


def build(nc, ins, out, which=tuple(range(8))):
    ctx = ExitStack()
    with ctx:
        sh = Shared(nc, ctx)
        sb, sem = sh.sb, sh.sem

        class M:
            pass

        m = M()
        m.X = sb("X", [P, NT, D])
        m.ctxT = sb("ctxT", [P, TOK])
        m.ident = sb("ident", [P, P])
        m.nhalf = sb("nhalf", [P, 1])
        m.hmask = sb("hmask", [P, H])
        m.vmask = sb("vmask", [P, H, S])
        m.maskbias = sb("maskbias", [P, NT, S])
        m.rowvalid = sb("rowvalid", [P, NT])
        ctx_raw = sb("ctx_raw", [P, NT, D])
        psum = sh.ps("psum", [P, 8, 512])
        m.banks = [psum[:, i, :] for i in range(8)]
        m.wide = [psum[:, 2:4, :], psum[:, 4:6, :], psum[:, 6:8, :]]

        loaded, consts, turned_ps, turned = sem("loaded"), sem("consts"), sem("turned_ps"), sem("turned")
        m.passed = sem("passed")
        NLOAD = [0]
        NCONST = [0]
        loads = []

        def load(dst, src):
            loads.append((dst, src))
            NLOAD[0] += 16

        load(ctx_raw[:, :, :], ins["ctx_1024"].rearrange("(t u) s d -> (u s) t d", u=2))
        load(m.X[:, :, :], ins["x"].rearrange("(t u) s d -> (u s) t d", u=2))

        rows, cols = sb("rows", [P, P]), sb("cols", [P, P])
        row = [0]

        def columns_of(src):
            n = src.shape[0]
            load(rows[row[0]:row[0] + n, :], src)
            row[0] += n
            return cols[:, row[0] - n:row[0]]

        def column(src):
            return columns_of(src.rearrange("(o p) -> o p", o=1))

        def spread(name, src):
            c = sb(name, [P, src.shape[0]])
            load(c[:, :], src.rearrange("(o n) -> o n", o=1).partition_broadcast(P))
            return c[:, :]

        def matrix(name, src):
            c = sb(name, [P, src.shape[1]])
            load(c[:, :], src)
            return c[:, :]

        w0 = {k: matrix(f"L0w{k}", ins[f"L0_xattn_W{k}"]) for k in "qkvo"}
        b0 = {k: column(ins[f"L0_xattn_b{k}"]) for k in "qkv"}
        b0["o"] = spread("L0bo", ins["L0_xattn_bo"])
        w1 = {"q": matrix("L1wq", ins["L1_xattn_w_q"]), "k": matrix("L1wk", ins["L1_xattn_w_kv"][:, 0:1024]),
              "v": matrix("L1wv", ins["L1_xattn_w_kv"][:, 1024:2048]),
              "gamma": column(ins["L1_xattn_ln_gamma"]), "beta": column(ins["L1_xattn_ln_beta"]),
              "bo": spread("L1bo", ins["L1_xattn_b_out"])}
        w1o = sb("L1wo", [P, HP, D])
        load(w1o[:, :, :], ins["L1_xattn_w_out"].rearrange("(c p) d -> p c d", p=P))
        w1["o"] = w1o
        gate_raw, gate = spread("L1gate_raw", ins["L1_xattn_gate"]), sb("L1gate", [P, 1])
        w1["gate"] = gate[:, 0:1]
        gate_ready = sem("gate_ready")
        b2 = {}
        for name, E, parts in (("L1", 16, [("L1_ffn_routed_b2", 14), ("L1_ffn_shared_b2", 2)]),
                               ("L2", 8, [("L2_xattn_b2", 8)])):
            b2[name] = sb(f"{name}b2rep", [P, D])
            for r in range(P // E):
                at = r * E
                for src, k in parts:
                    load(b2[name][at:at + k, :], ins[src])
                    at += k
        f0b2 = spread("F0b2", ins["L0_ffn_b2"])
        wr1, br1 = matrix("L1wr", ins["L1_ffn_router_w"]), spread("L1br", ins["L1_ffn_router_b"])
        wr2, br2 = matrix("L2wr", ins["L2_xattn_Wg"]), spread("L2br", ins["L2_xattn_bg"])
        wr3 = columns_of(ins["L2_ffn_w_router"])
        b1_0 = columns_of(ins["L0_ffn_b1"].rearrange("(c p) -> c p", p=P))
        b1_1 = columns_of(ins["L1_ffn_routed_b1"])
        columns_of(ins["L1_ffn_shared_b1"])
        b1_1 = cols[:, row[0] - 16:row[0]]
        b1_2 = columns_of(ins["L2_xattn_b1"].rearrange("e (c p) -> (e c) p", p=P))
        m.rev = sb("rev", [P, 16])
        tmask16, tmask8 = sb("tmask16", [P, 8]), sb("tmask8", [P, 16])
        mask_rows, mask_keys = sb("mask_rows", [NT, P], U8), sb("mask_keys", [P, NT, S], U8)
        load(mask_rows[:, :], ins["mask_BxS2_bf1"].rearrange("(t u) s -> t (u s)", u=2))
        load(mask_keys[:, :, :], ins["mask_BxSxS2_bk0"].rearrange("(t u) s k -> (u s) t k", u=2))
        rows_f, rows_c, valid = sb("rows_f", [NT, P]), sb("rows_c", [P, NT]), sb("valid", [P, NT, S])
        mask_set, mask_ps, mask_turned = sem("mask_set"), sem("mask_ps"), sem("mask_turned")
        w3_raw, w3_sb = sb("L3w_raw", [P, 4, P]), sb("L3w", [P, 4, P])
        for k, c in enumerate("qkvo"):
            load(w3_raw[:, k, :], ins[f"L3_xattn_W{c}"])
        w3 = {c: w3_sb[:, k, :] for k, c in enumerate("qkvo")}
        m.ones, m.round = sb("ones", [P, P]), sb("round", [P, 1])
        QW, qw = block_quantised_weights(sh, m, ins, load, loaded, lambda: NLOAD[0])
        PRE = NT // 4
        m.setup = None

        def begin(eng, start):
            for s, v in start:
                eng.wait_ge(s, v)

        m.begin = begin
        PRE += 2
        start0 = [(loaded, NLOAD[0]), (consts, 18), (turned, PRE)]

        makers = {
            0: lambda st: small_head_attention(sh, m, "A0", st, w0, b0, False),
            2: lambda st: wide_head_attention(sh, m, "A1", st + [(gate_ready, 1)], w1),
        }
        makers[1] = lambda st: experts(sh, m, "F0", st, dict(
            E=1, C=4, func=ACT.Gelu, bo=f0b2,
            weights=lambda e: (ins["L0_ffn_w1"].rearrange("(o d) f -> o d f", o=1),
                               ins["L0_ffn_w2"].rearrange("(o d) f -> o d f", o=1),
                               e), b1=b1_0))

        def weights1(e):
            if isinstance(e, int) and e >= 14:
                return ins["L1_ffn_shared_w1"], ins["L1_ffn_shared_w2"], e - 14
            return ins["L1_ffn_routed_w1"], ins["L1_ffn_routed_w2"], e

        makers[3] = lambda st: experts(sh, m, "E1", st, dict(
            E=16, C=1, func=ACT.Gelu, router="x", ER=14, wr=wr1, br=br1, whole=True, residual=True, b2=True,
            b2rep=b2["L1"], tmask=tmask16, b1=b1_1, weights=weights1))
        makers[4] = lambda st: experts(sh, m, "E2", st, dict(
            E=8, C=4, func=ACT.Relu, router="ctx", ER=8, wr=wr2, br=br2, whole=False, b2=True,
            b2rep=b2["L2"], tmask=tmask8, b1=b1_2,
            weights=lambda e: (ins["L2_xattn_W1"], ins["L2_xattn_W2"], e)))
        makers[5] = lambda st: experts(sh, m, "E3", st, dict(
            E=8, C=3, gated=True, router="x", ER=8, wr=wr3, br=None, whole=False,
            weights=(ins["L2_ffn_w_gate"], ins["L2_ffn_w_up"], ins["L2_ffn_w_down"])))
        makers[6] = lambda st: small_head_attention(sh, m, "A3", st + [(mask_set, 3)], w3, dict.fromkeys("qkvo"), True)
        makers[7] = lambda st: quantised_ffn(sh, m, "Q3", st + [QW.done], qw)
        layers, st = [], start0
        for k in which:
            layers.append(makers[k](st))
            st = [layers[-1].done]
        final = layers[-1].done

        stored = sem("stored")
        block = ctx.enter_context(nc.Block())

        @block.sync
        def _(sp):
            for dst, src in loads:
                sp.dma_start(dst, src).then_inc(loaded, 16)
            for L in layers:
                if L.sync:
                    L.sync(sp)
            sp.wait_ge(final[0], final[1])
            sp.dma_start(out.rearrange("(t u) s d -> (u s) t d", u=2), m.X[:, :, :]).then_inc(stored, 16)
            sp.wait_ge(stored, 16)

        @block.gpsimd
        def _(pool):
            pool.memset(m.ident[:, :], 0.0).then_inc(consts, 1)
            pool.memset(m.nhalf[:, :], -0.5).then_inc(consts, 1)
            pool.memset(m.hmask[:, :], 1.0).then_inc(consts, 1)
            pool.memset(m.vmask[:, :, :], 0.0).then_inc(consts, 1)
            pool.wait_ge(consts, 4)
            pool.affine_select(out=m.ident[:, :], in_=m.ident[:, :], compare_op=ALU.not_equal, fill=1.0,
                               base=0, pattern=[[-1, P]], channel_multiplier=1).then_inc(consts, 1)
            dh = D // H
            pool.affine_select(out=m.hmask[:, :], in_=m.hmask[:, :], compare_op=ALU.is_ge, fill=0.0,
                               base=0, pattern=[[-dh, H]], channel_multiplier=1).then_inc(consts, 1)
            pool.wait_ge(consts, 6)
            pool.affine_select(out=m.hmask[:, :], in_=m.hmask[:, :], compare_op=ALU.is_ge, fill=0.0,
                               base=dh - 1, pattern=[[dh, H]], channel_multiplier=-1).then_inc(consts, 1)
            for u in range(2):
                pool.wait_ge(consts, 7 + u)
                pool.memset(m.vmask[u * S:(u + 1) * S, u::2, :], 1.0).then_inc(consts, 1)
            pool.wait_ge(consts, 9)
            pool.iota(m.rev[:, :], pattern=[[-1, 16]], base=16, channel_multiplier=0,
                      allow_small_or_imprecise_dtypes=True).then_inc(consts, 1)
            for tm, E in ((tmask16, 16), (tmask8, 8)):
                pool.memset(tm[:, :], 1.0).then_inc(consts, 1)
            pool.wait_ge(consts, 12)
            for tm, E in ((tmask16, 16), (tmask8, 8)):
                pool.affine_select(out=tm[:, :], in_=tm[:, :], compare_op=ALU.is_ge, fill=0.0,
                                   base=0, pattern=[[-E, P // E]], channel_multiplier=1).then_inc(consts, 1)
            pool.wait_ge(consts, 14)
            for tm, E in ((tmask16, 16), (tmask8, 8)):
                pool.affine_select(out=tm[:, :], in_=tm[:, :], compare_op=ALU.is_ge, fill=0.0,
                                   base=E - 1, pattern=[[E, P // E]], channel_multiplier=-1).then_inc(consts, 1)
            pool.memset(m.ones[:, :], 1.0).then_inc(consts, 1)
            pool.memset(m.round[:, :], ROUND).then_inc(consts, 1)
            pool.wait_ge(consts, 18)
            pool.wait_ge(loaded, NLOAD[0])
            for L in layers:
                L.gpsimd(pool)

        @block.tensor
        def _(pe):
            pe.wait_ge(loaded, NLOAD[0])
            pe.wait_ge(consts, 18)
            for g in range(NG):
                if g >= 2:
                    pe.wait_ge(turned, g - 1)
                for i in range(4):
                    tr = pe.transpose(m.banks[g % 2][:, i * P:(i + 1) * P], ctx_raw[:, 4 * g + i, :], m.ident[:, :])
                tr.then_inc(turned_ps, 1)
            nrow = row[0]
            pe.transpose(m.banks[2][:, 0:nrow], rows[0:nrow, :], m.ident[0:nrow, 0:nrow]).then_inc(turned_ps, 1)
            for k in range(4):
                tr = pe.transpose(m.banks[3][:, k * P:(k + 1) * P], w3_raw[:, k, :], m.ident[:, :])
            tr.then_inc(turned_ps, 1)
            pe.wait_ge(mask_set, 1)
            pe.transpose(m.banks[5][:, 0:NT], rows_f[:, :], m.ident[0:NT, 0:NT]).then_inc(mask_ps, 1)
            QW.tensor(pe)
            for L in layers:
                L.tensor(pe)

        @block.scalar
        def _(act):
            act.wait_ge(loaded, NLOAD[0])
            act.activation(gate[:, :], gate_raw, ACT.Tanh).then_inc(gate_ready, 1)
            for g in range(NG):
                act.wait_ge(turned_ps, g + 1)
                act.activation(m.ctxT[:, g * GW:(g + 1) * GW], m.banks[g % 2], ACT.Copy).then_inc(turned, 1)
            act.wait_ge(turned_ps, PRE)
            act.activation(cols[:, 0:row[0]], m.banks[2][:, 0:row[0]], ACT.Copy).then_inc(turned, 1)
            act.activation(w3_sb[:, :, :].rearrange("p k f -> p (k f)"), m.banks[3], ACT.Copy).then_inc(turned, 1)
            QW.scalar(act)
            for L in layers:
                L.scalar(act)

        @block.vector
        def _(dve):
            dve.wait_ge(loaded, NLOAD[0])
            dve.tensor_copy(rows_f[:, :], mask_rows[:, :]).then_inc(mask_set, 1)
            dve.wait_ge(mask_ps, 1)
            dve.tensor_copy(rows_c[:, :], m.banks[5][:, 0:NT]).then_inc(mask_turned, 1)
            dve.wait_ge(mask_turned, 1)
            dve.tensor_tensor(valid[:, :, :], mask_keys[:, :, :],
                              rows_c[:, :].rearrange("p (t o) -> p t o", o=1).broadcast_to([P, NT, S]),
                              ALU.mult).then_inc(mask_turned, 1)
            dve.wait_ge(mask_turned, 2)
            dve.tensor_reduce(m.rowvalid[:, :], valid[:, :, :], AX, ALU.max).then_inc(mask_set, 1)
            dve.tensor_scalar(m.maskbias[:, :, :], valid[:, :, :], -NEG, NEG, ALU.mult, ALU.add).then_inc(mask_set, 1)
            QW.vector(dve)
            for L in layers:
                L.vector(dve)


_INS = [
    "x", "ctx_1024", "mask_BxS2_bf1", "mask_BxSxS2_bk0", "L0_xattn_Wq", "L0_xattn_bq", "L0_xattn_Wk",
    "L0_xattn_bk", "L0_xattn_Wv", "L0_xattn_bv", "L0_xattn_Wo", "L0_xattn_bo", "L0_ffn_w1", "L0_ffn_b1",
    "L0_ffn_w2", "L0_ffn_b2", "L1_xattn_ln_gamma", "L1_xattn_ln_beta", "L1_xattn_w_q", "L1_xattn_w_kv",
    "L1_xattn_w_out", "L1_xattn_b_out", "L1_xattn_gate", "L1_ffn_router_w", "L1_ffn_router_b", "L1_ffn_shared_w1",
    "L1_ffn_shared_b1", "L1_ffn_shared_w2", "L1_ffn_shared_b2", "L1_ffn_routed_w1", "L1_ffn_routed_b1",
    "L1_ffn_routed_w2", "L1_ffn_routed_b2", "L2_xattn_Wg", "L2_xattn_bg", "L2_xattn_W1", "L2_xattn_b1",
    "L2_xattn_W2", "L2_xattn_b2", "L2_ffn_w_router", "L2_ffn_w_gate", "L2_ffn_w_up", "L2_ffn_w_down",
    "L3_xattn_Wq", "L3_xattn_Wk", "L3_xattn_Wv", "L3_xattn_Wo", "L3_ffn_w_gate", "L3_ffn_w_up", "L3_ffn_w_down",
]


def kernel(**inputs):
    import numpy as np
    from concourse import bacc
    from concourse.bass_utils import run_bass_kernel_spmd

    nc = bacc.Bacc("TRN2", target_bir_lowering=False, num_devices=1)
    arrays, ins = {}, {}
    for name in _INS:
        a = np.ascontiguousarray(inputs[name])
        arrays[f"in_{name}"] = a
        ins[name] = nc.dram_tensor(f"in_{name}", a.shape, mybir.dt.from_np(a.dtype), kind="ExternalInput").ap()
    out = nc.dram_tensor("out", (B, S, D), F32, kind="ExternalOutput").ap()
    build(nc, ins, out)
    r = run_bass_kernel_spmd(nc, [arrays], core_ids=[0])
    return r.results[0]["out"]
```

```python
from contextlib import ExitStack

import concourse.bass as bass
from concourse import mybir

ALU = mybir.AluOpType
ACT = mybir.ActivationFunctionType
F32 = mybir.dt.float32
U8 = mybir.dt.uint8
AX = mybir.AxisListType.X

P = 128
B, S, D = 32, 64, 128
TOK = B * S
NT = TOK // P
GT = 4
NG = NT // GT
GW = GT * P
H = 16
HP = H // 2
EPS = 1e-5
NEG = -1.0e30
ROUND = 1.5 * 2.0 ** 23


def live(t):
    return not isinstance(t, int) or 0 <= t < NT


def past(t, k):
    return not isinstance(t, int) or t >= k


def before_end(t, k):
    return not isinstance(t, int) or t < NT - k


def pipeline(eng, step, lo, hi, end):
    for n in range(lo):
        step(n, n % 2)
    with eng.Fori(lo, hi - 1, 2) as i:
        step(i, lo % 2)
        step(i + 1, (lo + 1) % 2)
    for n in range(hi, end):
        step(n, n % 2)


class Layer:

    def __init__(self):
        self.tensor = self.vector = self.scalar = self.gpsimd = self.sync = None
        self.done = None


def tile_of(x, t):
    return x[:, bass.ds(t, 1), :].rearrange("p a d -> p (a d)")


def columns(x, t, n):
    return x[:, bass.ds(t * n, n)]


def apart(eng, m):
    eng.sem_inc(m.passed, 1)


class Signal:

    def __init__(self, sem, base):
        self.sem, self.base = sem, base

    def __call__(self, n):
        return self.sem, self.base + n


class Shared:

    def __init__(self, nc, ctx):
        self.nc, self.ctx, self.counted = nc, ctx, {}

    def sb(self, name, shape, dt=F32):
        return self.ctx.enter_context(self.nc.sbuf_tensor(name, shape, dt))

    def ps(self, name, shape, dt=F32):
        return self.ctx.enter_context(self.nc.psum_tensor(name, shape, dt))

    def sem(self, name):
        return self.ctx.enter_context(self.nc.semaphore(name))

    def counted_semaphore(self, name, total):
        sem, base = self.counted.get(name) or (self.sem(name), 0)
        self.counted[name] = (sem, base + total)
        return Signal(sem, base)


class Norm:

    def __init__(self, sh, sb, tag, m, kind="norm"):
        self.st, self.mv = sb(f"{tag}_stats", [P, 2, 6]), sb(f"{tag}_meanvar", [P, 2, 2])
        self.ve, self.rs = sb(f"{tag}_vareps", [P, 2, 1]), sb(f"{tag}_rstd", [P, 2, 1])
        self.stats_chain = sh.counted_semaphore(f"{kind}_stats_chain", 2 * NT)
        self.var_ready = sh.counted_semaphore(f"{kind}_var_ready", NT)
        self.rstd_ready = sh.counted_semaphore(f"{kind}_rstd_ready", NT)
        self.nhalf, self.passed = m.nhalf, m.passed

    def stats(self, dve, x, t, p):
        if past(t, 2):
            dve.wait_ge(*self.rstd_ready(t - 1))
        dve.bn_stats(self.st[:, p, :], x).then_inc(self.stats_chain.sem, 1)
        dve.wait_ge(*self.stats_chain(2 * t + 1))
        apart(dve, self)
        dve.bn_aggr(self.mv[:, p, :], self.st[:, p, :]).then_inc(self.stats_chain.sem, 1)
        dve.wait_ge(*self.stats_chain(2 * t + 2))
        dve.tensor_scalar(self.ve[:, p, :], self.mv[:, p, 1:2], EPS, None, ALU.add).then_inc(self.var_ready.sem, 1)

    def rstd(self, pool, t, p, applied):
        pool.wait_ge(*self.var_ready(t + 1))
        if past(t, 2):
            pool.wait_ge(*applied(t - 1))
        pool.tensor_tensor(self.rs[:, p, :], self.ve[:, p, :], self.nhalf[:, :], ALU.pow).then_inc(self.rstd_ready.sem, 1)

    def apply(self, dve, out, x, t, p):
        dve.wait_ge(*self.rstd_ready(t + 1))
        return dve.tensor_scalar(out, x, self.mv[:, p, 0:1], self.rs[:, p, 0:1], ALU.subtract, ALU.mult)


class NormAll:

    def __init__(self, sh, m):
        self.seen = sh.counted_semaphore("all_stats", 2 * NT)
        self.var_ready = sh.counted_semaphore("all_var_ready", NG)
        self.rstd_ready = sh.counted_semaphore("all_rstd_ready", NG)
        self.xn_ready = sh.counted_semaphore("all_xn_ready", NG)
        self.xnT_ps = sh.counted_semaphore("all_xnT_in_psum", NG)
        self.xnT_ready = sh.counted_semaphore("all_xnT_ready", NG)
        self.m = m
        self.bank = m.banks[0]

    def stats(self, dve, g):
        m = self.m
        for i in range(GT):
            t = g * GT + i
            dve.bn_stats(m.stats[:, t, :], m.X[:, t, :]).then_inc(self.seen.sem, 1)
        dve.wait_ge(*self.seen(2 * g * GT + GT))
        for i in range(GT):
            t = g * GT + i
            dve.bn_aggr(m.meanvar[:, t, :], m.stats[:, t, :]).then_inc(self.seen.sem, 1)
        dve.wait_ge(*self.seen(2 * g * GT + 2 * GT))
        ts = slice(g * GT, (g + 1) * GT)
        dve.tensor_scalar(m.vareps[:, ts], m.meanvar[:, ts, 1], EPS, None, ALU.add).then_inc(self.var_ready.sem, 1)

    def rstd(self, pool, g):
        m = self.m
        ts = slice(g * GT, (g + 1) * GT)
        pool.wait_ge(*self.var_ready(g + 1))
        pool.tensor_tensor(m.rstd[:, ts], m.vareps[:, ts], m.nhalf[:, :].broadcast_to([P, GT]),
                           ALU.pow).then_inc(self.rstd_ready.sem, 1)

    def apply(self, dve, g):
        m = self.m
        dve.wait_ge(*self.rstd_ready(g + 1))
        for i in range(GT):
            t = g * GT + i
            ap = dve.tensor_scalar(m.xn[:, t, :], m.X[:, t, :], m.meanvar[:, t, 0:1], m.rstd[:, t:t + 1],
                                   ALU.subtract, ALU.mult)
        ap.then_inc(self.xn_ready.sem, 1)

    def turn(self, pe, g):
        pe.wait_ge(*self.xn_ready(g + 1))
        if g:
            pe.wait_ge(*self.xnT_ready(g))
        for i in range(GT):
            tr = pe.transpose(self.bank[:, i * P:(i + 1) * P], self.m.xn[:, g * GT + i, :], self.m.ident[:, :])
        tr.then_inc(self.xnT_ps.sem, 1)

    def evacuate(self, act, g):
        act.wait_ge(*self.xnT_ps(g + 1))
        act.activation(self.m.XNT[:, g * GW:(g + 1) * GW], self.bank, ACT.Copy).then_inc(self.xnT_ready.sem, 1)


def small_head_attention(sh, m, tag, start, w, bias, masked):
    nc = sh.nc
    dh = D // H
    scale = float(dh) ** -0.5
    L = Layer()
    with ExitStack() as scope:
        def sb(name, shape, dt=F32):
            return scope.enter_context(nc.sbuf_tensor(f"{tag}_{name}", shape, dt))

        norm = Norm(sh, sb, f"{tag}_ln", m)
        xn = sb("xn", [P, 2, P])
        xnT = sb("xnT", [P, 2, P])
        qT = sb("qT", [P, 2, P])
        kT = sb("kT", [P, 2, P])
        ctx2 = sb("ctx2", [P, 2, 2, 2, S])
        kexp = sb("kexp", [P, 2, 2, H, S])
        prob = sb("prob", [P, 2, H, S])
        probT = sb("probT", [P, 2, HP, P])
        vbd = sb("vbd", [P, 2, 2, H, dh + 1])
        mx = sb("mx", [P, 2, H])
        rc = sb("rc", [P, 2, H])
        on = sb("on", [P, 2, P])
        oT = sb("oT", [P, 2, P])
        tmp = sb("tmp", [P, 2, P])

    J0, J1 = m.banks[0], m.banks[1]
    pS, pP, pO, J2 = m.wide[0], m.wide[1], m.banks[6], m.banks[7]
    sv = pS.rearrange("p a (h k) -> p (a h) k", k=S)

    signal = sh.counted_semaphore
    MC = RC = 2 if masked else 1
    vones = signal("vones_set", 5)
    xn_ready, xnT_ready, xnT_ps = signal("xn_ready", NT), signal("xnT_ready", NT), signal("xnT_in_psum", NT)
    q_ps, q_ready = signal("q_in_psum", NT), signal("q_ready", NT)
    k_ps, k_ready, kexp_ready = signal("k_in_psum", NT), signal("k_ready", NT), signal("kexp_ready", NT)
    v_ps, v_ready, ctx2_ready = signal("v_in_psum", NT), signal("v_ready", NT), signal("ctx2_ready", NT)
    scores_ready, max_chain, sub_ready = signal("scores_ready", NT), signal("max_chain", MC * NT), signal("sub_ready", NT)
    prob_ready, probT_ps, probT_ready = signal("prob_ready", NT), signal("probT_in_psum", 2 * NT), signal("probT_ready", 2 * NT)
    o_ps, rc_chain, on_ready = signal("o_in_psum", NT), signal("rc_chain", RC * NT), signal("on_ready", NT)
    oT_ps, oT_ready, out_ps, tmp_ready = signal("oT_in_psum", NT), signal("oT_ready", NT), signal("out_in_psum", NT), signal("tmp_ready", NT)
    x_done = signal("x_done", NT)
    L.done = x_done(NT)
    LO, HI, END = 7, NT - 1, NT + 5

    def tensor(pe):
        m.begin(pe, start)

        def turn_x(t, p):
            pe.wait_ge(*xn_ready(t + 1))
            if past(t, 1):
                pe.wait_ge(*q_ready(t))
            else:
                pe.wait_ge(*k_ready(1))
            pe.transpose(J0[:, 0:P], xn[:, p, :], m.ident[:, :]).then_inc(xnT_ps.sem, 1)

        def scores(t, p):
            pe.wait_ge(*q_ready(t + 1))
            pe.wait_ge(*kexp_ready(t + 1))
            if past(t, 1):
                pe.wait_ge(*sub_ready(t))
            for half in range(2):
                for b in range(2):
                    rhs = kexp[:, p, b, half * HP:(half + 1) * HP, :].rearrange("p h k -> p (h k)")
                    mm = pe.matmul(pS[b * S:(b + 1) * S, half, :], qT[:, p, b * S:(b + 1) * S], rhs,
                                   start=True, stop=True)
            mm.then_inc(scores_ready.sem, 1)

        def keys(t, p):
            if past(t, 1):
                pe.wait_ge(*xnT_ready(t))
            pe.matmul(J0[:, 0:P], w["k"], columns(m.ctxT, t, P), start=True, stop=True).then_inc(k_ps.sem, 1)

        def values(t, p):
            pe.wait_ge(*ctx2_ready(t + 1))
            if past(t, 1):
                pe.wait_ge(*v_ready(t))
            for b in range(2):
                mm = pe.matmul(J1[:, b * P:(b + 1) * P], ctx2[:, p, b].rearrange("p u s -> p (u s)"), w["v"],
                               start=True, stop=True)
            mm.then_inc(v_ps.sem, 1)

        def turn_probs(t, p):
            pe.wait_ge(*prob_ready(t + 1))
            if past(t, 1):
                pe.wait_ge(*probT_ready(2 * t))
            for c in range(HP):
                tr = pe.transpose(pP[:, c // 4, c % 4 * P:c % 4 * P + P],
                                  prob[:, p, 2 * c:2 * c + 2, :].rearrange("p h k -> p (h k)"), m.ident[:, :])
                if c % 4 == 3:
                    tr.then_inc(probT_ps.sem, 1)

        def turn_out(t, p):
            pe.wait_ge(*on_ready(t + 1))
            if past(t, 1):
                pe.wait_ge(*tmp_ready(t))
            pe.transpose(J2[:, 0:P], on[:, p, :], m.ident[:, :]).then_inc(oT_ps.sem, 1)

        def queries(t, p, last=False):
            pe.wait_ge(*xnT_ready(t + 1))
            if not last:
                pe.wait_ge(*k_ready(t + 2))
            pe.matmul(J0[:, 0:P], w["q"], xnT[:, p, :], start=True, stop=True).then_inc(q_ps.sem, 1)

        def weigh_values(t, p):
            pe.wait_ge(*probT_ready(2 * t + 2))
            pe.wait_ge(*v_ready(t + 1))
            if past(t, 1):
                pe.wait_ge(*on_ready(t))
            for c in range(HP):
                for b in range(2):
                    mm = pe.matmul(pO[b * S:(b + 1) * S, c * 18:c * 18 + 18], probT[:, p, c, b * S:(b + 1) * S],
                                   vbd[:, p, b, 2 * c:2 * c + 2, :].rearrange("p h d -> p (h d)"),
                                   start=True, stop=True)
            mm.then_inc(o_ps.sem, 1)

        def project(t, p):
            pe.wait_ge(*oT_ready(t + 1))
            pe.matmul(J2[:, P:2 * P], oT[:, p, :], w["o"], start=True, stop=True).then_inc(out_ps.sem, 1)

        def step(n, p):
            q = 1 - p
            if live(n - 1):
                turn_x(n - 1, q)
            if live(n - 2):
                scores(n - 2, p)
            if live(n):
                keys(n, p)
            if live(n - 2):
                values(n - 2, p)
            if live(n - 3):
                turn_probs(n - 3, q)
            if live(n - 4):
                turn_out(n - 4, p)
            if live(n - 1):
                queries(n - 1, q, not live(n))
            if live(n - 3):
                weigh_values(n - 3, q)
            if live(n - 4):
                project(n - 4, p)

        pipeline(pe, step, LO, HI, END)

    def scalar(act):
        m.begin(act, start)

        def evac(dst, src, ready, n, done, bias=None):
            act.wait_ge(*ready(n))
            if bias is None:
                act.activation(dst, src, ACT.Copy).then_inc(done.sem, 1)
            else:
                act.activation(dst, src, ACT.Identity, bias=bias).then_inc(done.sem, 1)

        def step(n, p):
            q = 1 - p
            if live(n - 1):
                t = n - 1
                if past(t, 2):
                    act.wait_ge(*q_ps(t - 1))
                evac(xnT[:, q, :], J0[:, 0:P], xnT_ps, t + 1, xnT_ready)
            if live(n):
                t = n
                if past(t, 2):
                    act.wait_ge(*kexp_ready(t - 1))
                evac(kT[:, p, :], J0[:, 0:P], k_ps, t + 1, k_ready, bias["k"])
            if live(n - 3):
                t = n - 3
                if past(t, 2):
                    act.wait_ge(*o_ps(t - 1))
                for half in range(2):
                    evac(probT[:, q, 4 * half:4 * half + 4, :].rearrange("p c q -> p (c q)"), pP[:, half, :],
                         probT_ps, 2 * t + half + 1, probT_ready)
            if live(n - 4):
                t = n - 4
                if past(t, 2):
                    act.wait_ge(*out_ps(t - 1))
                evac(oT[:, p, :], J2[:, 0:P], oT_ps, t + 1, oT_ready, bias["v"])
            if live(n - 1):
                t = n - 1
                if past(t, 2):
                    act.wait_ge(*scores_ready(t - 1))
                evac(qT[:, q, :], J0[:, 0:P], q_ps, t + 1, q_ready, bias["q"])
            if live(n - 2):
                act.wait_ge(*sub_ready(n - 1))
                pr = prob[:, p].rearrange("p h k -> p (h k)")
                act.activation(pr, pr, ACT.Exp, scale=scale).then_inc(prob_ready.sem, 1)

        pipeline(act, step, LO, HI, END)

    def gpsimd(pool):
        m.begin(pool, start)
        pool.memset(vbd[:, :, :, :, :].rearrange("p a b h d -> p (a b h d)"), 0.0).then_inc(vones.sem, 1)
        for u in range(2):
            for a in range(2):
                pool.wait_ge(*vones(1 + 2 * u + a))
                pool.memset(vbd[u * S:(u + 1) * S, a, :, u::2, dh:dh + 1], 1.0).then_inc(vones.sem, 1)
        pool.wait_ge(*vones(5))

        def context(t, p):
            if past(t, 2):
                pool.wait_ge(*v_ps(t - 1))
            src = columns(m.ctxT, t, P).rearrange("p (b s) -> p b s", b=2)
            for u in range(2):
                cp = pool.tensor_copy(ctx2[:, p, :, u, :], src)
            cp.then_inc(ctx2_ready.sem, 1)

        def step(n, p):
            if live(n + 1):
                norm.rstd(pool, n + 1, 1 - p, xn_ready)
            if live(n - 1):
                context(n - 1, 1 - p)
            if live(n):
                t = n
                pool.wait_ge(*k_ready(t + 1))
                if past(t, 2):
                    pool.wait_ge(*scores_ready(t - 1))
                for b in range(2):
                    kk = kT[:, p, b * S:(b + 1) * S].rearrange("p (o k) -> p o k", o=1)
                    ke = pool.tensor_tensor(kexp[:, p, b], kk.broadcast_to([P, H, S]),
                                            m.hmask[:, :].rearrange("p (h o) -> p h o", o=1).broadcast_to([P, H, S]),
                                            ALU.mult)
                ke.then_inc(kexp_ready.sem, 1)

        norm.rstd(pool, 0, 0, xn_ready)
        pipeline(pool, step, LO, HI, END)

    def vector(dve):
        m.begin(dve, start)
        dve.wait_ge(*vones(5))

        def step(n, p):
            q = 1 - p
            if live(n - 5):
                t = n - 5
                dve.wait_ge(*out_ps(t + 1))
                xt = tile_of(m.X, t)
                if bias["o"] is None:
                    dve.tensor_copy(tmp[:, q, :], J2[:, P:2 * P]).then_inc(tmp_ready.sem, 1)
                else:
                    dve.tensor_tensor(tmp[:, q, :], J2[:, P:2 * P], bias["o"], ALU.add).then_inc(tmp_ready.sem, 1)
                dve.wait_ge(*tmp_ready(t + 1))
                dve.tensor_tensor(xt, xt, tmp[:, q, :], ALU.add).then_inc(x_done.sem, 1)
            if live(n - 4):
                t = n - 4
                dve.wait_ge(*o_ps(t + 1))
                ov = pO[:, 0:H * (dh + 1)].rearrange("p (h e) -> p h e", e=dh + 1)
                dve.reciprocal(rc[:, p, :], ov[:, :, dh]).then_inc(rc_chain.sem, 1)
                dve.wait_ge(*rc_chain(RC * t + 1))
                if masked:
                    dve.tensor_scalar(rc[:, p, :], rc[:, p, :], m.rowvalid[:, bass.ds(t, 1)], None,
                                      ALU.mult).then_inc(rc_chain.sem, 1)
                    dve.wait_ge(*rc_chain(RC * t + 2))
                if past(t, 2):
                    dve.wait_ge(*oT_ps(t - 1))
                dve.tensor_tensor(on[:, p, :].rearrange("p (h d) -> p h d", d=dh), ov[:, :, 0:dh],
                                  rc[:, p, :].rearrange("p (h o) -> p h o", o=1).broadcast_to([P, H, dh]),
                                  ALU.mult).then_inc(on_ready.sem, 1)
            if live(n):
                if past(n, 2):
                    dve.wait_ge(*xnT_ps(n - 1))
                norm.apply(dve, xn[:, p, :], tile_of(m.X, n), n, p).then_inc(xn_ready.sem, 1)
            if live(n + 1):
                norm.stats(dve, tile_of(m.X, n + 1), n + 1, q)
            if live(n - 2):
                t = n - 2
                dve.wait_ge(*scores_ready(t + 1))
                if past(t, 2):
                    dve.wait_ge(*probT_ps(2 * t - 2))
                mxb = mx[:, p, :].rearrange("p (h o) -> p h o", o=1).broadcast_to([P, H, S])
                src, c = sv, 0
                if masked:
                    mb = m.maskbias[:, bass.ds(t, 1), :].broadcast_to([P, H, S])
                    dve.tensor_tensor(prob[:, p], sv, mb, ALU.add).then_inc(max_chain.sem, 1)
                    dve.wait_ge(*max_chain(MC * t + 1))
                    src, c = prob[:, p], 1
                dve.tensor_reduce(mx[:, p, :], src, AX, ALU.max).then_inc(max_chain.sem, 1)
                dve.wait_ge(*max_chain(MC * t + c + 1))
                dve.tensor_tensor(prob[:, p], src, mxb, ALU.subtract).then_inc(sub_ready.sem, 1)
                dve.wait_ge(*v_ps(t + 1))
                if past(t, 2):
                    dve.wait_ge(*o_ps(t - 1))
                for b in range(2):
                    vv = dve.tensor_tensor(vbd[:, p, b, :, 0:dh],
                                           J1[:, b * P:(b + 1) * P].rearrange("p (h d) -> p h d", d=dh),
                                           m.vmask[:, :, 0:dh], ALU.mult)
                vv.then_inc(v_ready.sem, 1)

        norm.stats(dve, tile_of(m.X, 0), 0, 0)
        pipeline(dve, step, LO, HI, END)

    L.tensor, L.scalar, L.gpsimd, L.vector = tensor, scalar, gpsimd, vector
    return L


def wide_head_attention(sh, m, tag, start, w):
    nc = sh.nc
    dh = 64
    scale = float(dh) ** -0.5
    L = Layer()
    with ExitStack() as scope:
        def sb(name, shape, dt=F32):
            return scope.enter_context(nc.sbuf_tensor(f"{tag}_{name}", shape, dt))

        outer = Norm(sh, sb, f"{tag}_outer", m)
        inner = Norm(sh, sb, f"{tag}_inner", m, "inner_norm")
        x1 = sb("x1", [P, 2, P])
        xn = sb("xn", [P, 2, P])
        xnT = sb("xnT", [P, 2, P])
        qT = sb("qT", [P, 2, HP, P])
        kbd = sb("kbd", [P, 2, 2, HP, 2, S])
        ctx1 = sb("ctx1", [P, 2, P])
        vbd = sb("vbd", [P, 2, 2, HP, 2, dh])
        prob = sb("prob", [P, 2, H, S])
        probT = sb("probT", [P, 2, HP, P])
        mx = sb("mx", [P, 2, H])
        sm = sb("sm", [P, 2, H])
        rc = sb("rc", [P, 2, H])
        on = sb("on", [P, 2, H * dh])
        oT = sb("oT", [P, 2, HP, P])
        tmp = sb("tmp", [P, 2, P])

    J0, J1 = m.banks[0], m.banks[1]
    pS, pP, pO = m.wide[0], m.wide[1], m.wide[2]
    sv = pS.rearrange("p a (h k) -> p (a h) k", k=S)
    ov = pO.rearrange("p a (h k) -> p (a h) k", k=dh)

    signal = sh.counted_semaphore
    zeros = signal("blocks_zeroed", 2)
    x1_ready, xn_ready, xnT_ready, xnT_ps = signal("x1_ready", NT), signal("xn_ready", NT), signal("xnT_ready", NT), signal("xnT_in_psum", NT)
    q_ps, q_ready = signal("q_in_psum", 2 * NT), signal("q_ready", 2 * NT)
    k_ps, k_ready = signal("k_in_psum", 2 * NT), signal("k_ready", 4 * NT)
    v_ps, v_ready, ctx1_ready = signal("v_in_psum", 2 * NT), signal("v_ready", 4 * NT), signal("ctx1_ready", NT)
    scores_ready, mx_ready, sub_ready = signal("scores_ready", NT), signal("mx_ready", NT), signal("sub_ready", NT)
    prob_ready, probT_ps, probT_ready = signal("prob_ready", NT), signal("probT_in_psum", 2 * NT), signal("probT_ready", 2 * NT)
    o_ps, sm_ready, rc_ready, on_ready = signal("o_in_psum", NT), signal("sm_ready", NT), signal("rc_ready", NT), signal("on_ready", NT)
    oT_ps, oT_ready, out_ps, tmp_ready = signal("oT_in_psum", 2 * NT), signal("oT_ready", 2 * NT), signal("out_in_psum", NT), signal("tmp_ready", NT)
    x_done = signal("x_done", NT)
    L.done = x_done(NT)
    LO, HI, END = 7, NT - 1, NT + 4

    def tensor(pe):
        m.begin(pe, start)

        def keys(t, p):
            for j in range(2):
                if past(t, 1):
                    pe.wait_ge(*q_ready(2 * t - 1 + j))
                for c in range(4):
                    cc = 4 * j + c
                    mm = pe.matmul((J1, J0)[j][:, c * P:(c + 1) * P], w["k"][:, cc * P:(cc + 1) * P],
                                   columns(m.ctxT, t, P), start=True, stop=True)
                mm.then_inc(k_ps.sem, 1)

        def values(t, p):
            pe.wait_ge(*ctx1_ready(t + 1))
            wv = w["v"].rearrange("p (c u d) -> p c u d", u=2, d=dh)
            for b in range(2):
                if before_end(t, 2):
                    pe.wait_ge(*k_ready(4 * t + 2 * b + 10))
                elif before_end(t, 1):
                    pe.wait_ge(*q_ready(2 * t + 3 + b))
                else:
                    pe.wait_ge(*v_ready(4 * t - 2 + 2 * b))
                for u in range(2):
                    mm = pe.matmul((J1, J0)[b][u * S:(u + 1) * S, :], ctx1[:, p, b * S:(b + 1) * S], wv[:, :, u, :],
                                   start=True, stop=True)
                mm.then_inc(v_ps.sem, 1)

        def turn_x(t, p):
            pe.wait_ge(*xn_ready(t + 1))
            if past(t, 2):
                pe.wait_ge(*v_ready(4 * t - 4))
            else:
                pe.wait_ge(*k_ready(4 * t + 4))
            pe.transpose(J0[:, 0:P], xn[:, p, :], m.ident[:, :]).then_inc(xnT_ps.sem, 1)

        def queries(t, p):
            pe.wait_ge(*xnT_ready(t + 1))
            for j in range(2):
                if j == 0:
                    if past(t, 2):
                        pe.wait_ge(*v_ready(4 * t - 6))
                    else:
                        pe.wait_ge(*k_ready(4 * t + 2))
                for c in range(4):
                    cc = 4 * j + c
                    mm = pe.matmul((J1, J0)[j][:, c * P:(c + 1) * P], w["q"][:, cc * P:(cc + 1) * P], xnT[:, p, :],
                                   start=True, stop=True)
                mm.then_inc(q_ps.sem, 1)

        def scores(t, p):
            pe.wait_ge(*q_ready(2 * t + 2))
            pe.wait_ge(*k_ready(4 * t + 4))
            if past(t, 1):
                pe.wait_ge(*sub_ready(t))
            for c in range(HP):
                for b in range(2):
                    mm = pe.matmul(pS[b * S:(b + 1) * S, c // 4, c % 4 * P:c % 4 * P + P],
                                   qT[:, p, c, b * S:(b + 1) * S],
                                   kbd[:, p, b, c].rearrange("p u k -> p (u k)"), start=True, stop=True)
            mm.then_inc(scores_ready.sem, 1)

        def turn_probs(t, p):
            pe.wait_ge(*prob_ready(t + 1))
            if past(t, 2):
                pe.wait_ge(*tmp_ready(t - 1))
            elif past(t, 1):
                pe.wait_ge(*probT_ready(2 * t))
            for c in range(HP):
                tr = pe.transpose(pP[:, c // 4, c % 4 * P:c % 4 * P + P],
                                  prob[:, p, 2 * c:2 * c + 2, :].rearrange("p h k -> p (h k)"), m.ident[:, :])
                if c % 4 == 3:
                    tr.then_inc(probT_ps.sem, 1)

        def weigh_values(t, p):
            pe.wait_ge(*probT_ready(2 * t + 2))
            pe.wait_ge(*v_ready(4 * t + 4))
            if past(t, 1):
                pe.wait_ge(*on_ready(t))
            for c in range(HP):
                for b in range(2):
                    mm = pe.matmul(pO[b * S:(b + 1) * S, c // 4, c % 4 * P:c % 4 * P + P],
                                   probT[:, p, c, b * S:(b + 1) * S],
                                   vbd[:, p, b, c].rearrange("p u d -> p (u d)"), start=True, stop=True)
            mm.then_inc(o_ps.sem, 1)

        def turn_out(t, p):
            pe.wait_ge(*on_ready(t + 1))
            if before_end(t, 1):
                pe.wait_ge(*probT_ready(2 * t + 4))
            else:
                pe.wait_ge(*tmp_ready(t))
            for c in range(HP):
                tr = pe.transpose(pP[:, c // 4, c % 4 * P:c % 4 * P + P], on[:, p, c * P:(c + 1) * P], m.ident[:, :])
                if c % 4 == 3:
                    tr.then_inc(oT_ps.sem, 1)

        def project(t, p):
            pe.wait_ge(*oT_ready(2 * t + 2))
            for c in range(HP):
                mm = pe.matmul(pP[:, 0, 0:P], oT[:, p, c, :], w["o"][:, c, :], start=(c == 0), stop=(c == HP - 1))
            mm.then_inc(out_ps.sem, 1)

        def step(n, p):
            q = 1 - p
            if live(n - 2):
                scores(n - 2, p)
            if live(n - 1):
                turn_x(n - 1, q)
            if live(n - 3):
                turn_probs(n - 3, q)
            if live(n - 1):
                queries(n - 1, q)
            if live(n - 4):
                turn_out(n - 4, p)
            if live(n):
                keys(n, p)
            if live(n - 3):
                weigh_values(n - 3, q)
            if live(n - 4):
                project(n - 4, p)
            if live(n - 2):
                values(n - 2, p)

        pipeline(pe, step, LO, HI, END)

    def scalar(act):
        m.begin(act, start)
        act.wait_ge(*zeros(2))

        def step(n, p):
            q = 1 - p
            if live(n - 1):
                t = n - 1
                act.wait_ge(*xnT_ps(t + 1))
                if past(t, 2):
                    act.wait_ge(*q_ps(2 * t - 2))
                act.activation(xnT[:, q, :], J0[:, 0:P], ACT.Identity, bias=w["beta"],
                               scale=w["gamma"]).then_inc(xnT_ready.sem, 1)
            if live(n - 3):
                t = n - 3
                if past(t, 2):
                    act.wait_ge(*o_ps(t - 1))
                for half in range(2):
                    act.wait_ge(*probT_ps(2 * t + half + 1))
                    act.activation(probT[:, q, 4 * half:4 * half + 4, :].rearrange("p c q -> p (c q)"),
                                   pP[:, half, :], ACT.Copy).then_inc(probT_ready.sem, 1)
            if live(n - 1):
                t = n - 1
                if past(t, 2):
                    act.wait_ge(*scores_ready(t - 1))
                for j in range(2):
                    act.wait_ge(*q_ps(2 * t + j + 1))
                    act.activation(qT[:, q, 4 * j:4 * j + 4, :].rearrange("p c q -> p (c q)"), (J1, J0)[j],
                                   ACT.Copy).then_inc(q_ready.sem, 1)
            if live(n - 4):
                t = n - 4
                if past(t, 2):
                    act.wait_ge(*out_ps(t - 1))
                for j in range(2):
                    act.wait_ge(*oT_ps(2 * t + j + 1))
                    act.activation(oT[:, p, 4 * j:4 * j + 4, :].rearrange("p c q -> p (c q)"), pP[:, j, :],
                                   ACT.Copy).then_inc(oT_ready.sem, 1)
            if live(n):
                t = n
                if past(t, 2):
                    act.wait_ge(*scores_ready(t - 1))
                for j in range(2):
                    act.wait_ge(*k_ps(2 * t + j + 1))
                    for u in range(2):
                        src = (J1, J0)[j][u * S:(u + 1) * S, :].rearrange("p (c b k) -> p b c k", b=2, k=S)
                        act.activation(kbd[u * S:(u + 1) * S, p, :, 4 * j:4 * j + 4, u, :], src,
                                       ACT.Copy).then_inc(k_ready.sem, 1)
            if live(n - 2):
                act.wait_ge(*sub_ready(n - 1))
                pr = prob[:, p].rearrange("p h k -> p (h k)")
                act.activation(pr, pr, ACT.Exp, scale=scale).then_inc(prob_ready.sem, 1)

        pipeline(act, step, LO, HI, END)

    def gpsimd(pool):
        m.begin(pool, start)
        pool.memset(kbd[:, :, :, :, :, :].rearrange("p a b c u k -> p (a b c u k)"), 0.0).then_inc(zeros.sem, 1)
        pool.memset(vbd[:, :, :, :, :, :].rearrange("p a b c u k -> p (a b c u k)"), 0.0).then_inc(zeros.sem, 1)

        def context(t, p):
            if past(t, 2):
                pool.wait_ge(*v_ps(2 * t - 2))
            pool.tensor_copy(ctx1[:, p, :], columns(m.ctxT, t, P)).then_inc(ctx1_ready.sem, 1)

        def step(n, p):
            if live(n):
                inner.rstd(pool, n, p, xn_ready)
            if live(n + 1):
                outer.rstd(pool, n + 1, 1 - p, x1_ready)
            if live(n - 1):
                context(n - 1, 1 - p)

        outer.rstd(pool, 0, 0, x1_ready)
        pipeline(pool, step, LO, HI, END)

    def vector(dve):
        m.begin(dve, start)
        dve.wait_ge(*zeros(2))

        def step(n, p):
            q = 1 - p
            if live(n):
                outer.apply(dve, x1[:, p, :], tile_of(m.X, n), n, p).then_inc(x1_ready.sem, 1)
                dve.wait_ge(*x1_ready(n + 1))
                inner.stats(dve, x1[:, p, :], n, p)
            if live(n - 2):
                t = n - 2
                dve.wait_ge(*scores_ready(t + 1))
                if past(t, 2):
                    dve.wait_ge(*probT_ps(2 * t - 2))
                dve.tensor_reduce(mx[:, p, :], sv, AX, ALU.max).then_inc(mx_ready.sem, 1)
                dve.wait_ge(*mx_ready(t + 1))
                dve.tensor_tensor(prob[:, p], sv,
                                  mx[:, p, :].rearrange("p (h o) -> p h o", o=1).broadcast_to([P, H, S]),
                                  ALU.subtract).then_inc(sub_ready.sem, 1)
            if live(n):
                if past(n, 2):
                    dve.wait_ge(*xnT_ps(n - 1))
                inner.apply(dve, xn[:, p, :], x1[:, p, :], n, p).then_inc(xn_ready.sem, 1)
            if live(n + 1):
                outer.stats(dve, tile_of(m.X, n + 1), n + 1, q)
            if live(n - 3):
                t = n - 3
                dve.wait_ge(*prob_ready(t + 1))
                dve.tensor_reduce(sm[:, q, :], prob[:, q], AX, ALU.add).then_inc(sm_ready.sem, 1)
                dve.wait_ge(*sm_ready(t + 1))
                dve.reciprocal(rc[:, q, :], sm[:, q, :]).then_inc(rc_ready.sem, 1)
                dve.wait_ge(*rc_ready(t + 1))
                dve.wait_ge(*o_ps(t + 1))
                if past(t, 2):
                    dve.wait_ge(*oT_ps(2 * t - 2))
                dve.tensor_tensor(on[:, q, :].rearrange("p (h d) -> p h d", d=dh), ov,
                                  rc[:, q, :].rearrange("p (h o) -> p h o", o=1).broadcast_to([P, H, dh]),
                                  ALU.mult).then_inc(on_ready.sem, 1)
            if live(n - 4):
                t = n - 4
                dve.wait_ge(*out_ps(t + 1))
                xt = tile_of(m.X, t)
                dve.tensor_tensor(tmp[:, p, :], pP[:, 0, 0:P], w["bo"], ALU.add).then_inc(tmp_ready.sem, 1)
                dve.wait_ge(*tmp_ready(t + 1))
                dve.scalar_tensor_tensor(out=xt, in0=tmp[:, p, :], scalar=w["gate"], in1=xt, op0=ALU.mult,
                                         op1=ALU.add).then_inc(x_done.sem, 1)
            if live(n - 2):
                t = n - 2
                if past(t, 2):
                    dve.wait_ge(*o_ps(t - 1))
                for b in range(2):
                    dve.wait_ge(*v_ps(2 * t + b + 1))
                    for u in range(2):
                        src = (J1, J0)[b][u * S:(u + 1) * S, :].rearrange("p (c d) -> p c d", d=dh)
                        dve.tensor_copy(vbd[u * S:(u + 1) * S, p, b, :, u, :], src).then_inc(v_ready.sem, 1)

        outer.stats(dve, tile_of(m.X, 0), 0, 0)
        pipeline(dve, step, LO, HI, END)

    L.tensor, L.scalar, L.gpsimd, L.vector = tensor, scalar, gpsimd, vector
    return L


def experts(sh, m, tag, start, spec):
    nc = sh.nc
    E, C, gated, router, ER = spec["E"], spec["C"], spec.get("gated"), spec.get("router"), spec.get("ER", 0)
    L = Layer()
    if gated:
        raw, = m.weight_buffers[tag]
    else:
        w1, w2 = m.weight_buffers[tag]
    with ExitStack() as scope:
        def sb(name, shape, dt=F32):
            return scope.enter_context(nc.sbuf_tensor(f"{tag}_{name}", shape, dt))

        if gated:
            w1, w2 = sb("w1", [P, 2, 2 * C * P]), sb("w2", [P, 2, C, D])
        h = sb("h", [P, 2, C, GW])
        if gated:
            sg = sb("sg", [P, 2, GW])
        if router:
            LG = sb("logits", [P, NT, ER])
            gates = sb("gates", [P, NT, E])
            A, Bt, Ct, O1, O2 = (sb(f"work{i}", [P, NT, ER]) for i in range(5))
            m1, m2, rm, ws, wa, wb = (sb(f"row{i}", [P, NT]) for i in range(6))
        if router and spec.get("b2"):
            R = P // E
            gT = sb("gT", [P, E * NT // P, P])
            b2sel = sb("b2sel", [P, R, D])

    J0, J1 = m.banks[0], m.banks[1]
    norm = NormAll(sh, m)
    xn, XNT, xn_ready, xnT_ready = m.xn, m.XNT, norm.xn_ready, norm.xnT_ready
    early, after = spec.get("early"), spec.get("then_norm")
    ring = m.banks[2:6]
    Y = [m.banks[6], m.banks[7]]

    signal = sh.counted_semaphore
    b2 = bool(router and spec.get("b2"))
    EXPS = (2 if spec["whole"] else 1) if router else 0
    LINKS = (17 if E > ER else 16) if router else 0
    ND = 5 if gated else 2
    units = NG * E
    lg_ps, lg_ready = signal("logits_in_psum", NG if router else 0), signal("logits_ready", 1 if router else 0)
    x_plus = signal("x_plus_norm", 1 if spec.get("residual") else 0)
    g_chain, exp_in, exp_out, gates_ready = signal("gates_chain", LINKS), signal("exp_in", EXPS), signal("exp_out", EXPS), signal("gates_ready", 1 if router else 0)
    gT_ps, gT_ready, b2_ps, b2_added, sel_ready = (signal("gT_in_psum", 1 if b2 else 0), signal("gT_ready", 1 if b2 else 0), signal("b2_in_psum", NG if b2 else 0),
                                                   signal("b2_added", NG if b2 else 0 if router else 1), signal("b2sel_ready", R if b2 else 0))
    w_loaded = [signal("w_loaded_even", ND * 16 * ((E + 1) // 2)), signal("w_loaded_odd", ND * 16 * (E // 2))]
    w_turned_ps, w_turned, zeroed = signal("w_turned_ps", 3 * E if gated else 0), signal("w_turned", 3 * E if gated else 0), signal("raw_zeroed", 1 if gated else 0)
    a_ps, s_ready, h_ready, y_ps, combined = (signal("hidden_in_psum", units * C), signal("silu_ready", units * C if gated else 0), signal("h_ready", units * C),
                                              signal("y_in_psum", units), signal("combined", units))
    L.done = combined(units)
    L.norm = norm
    weights_here, m.weights_here = m.weights_here, [s(ND * 16 * n) for s, n in zip(w_loaded, ((E + 1) // 2, E // 2)) if n]

    def over_experts(eng, one, middle):
        if E == 1:
            one(0, 0)
            return
        one(0, 0)
        one(1, 1)
        with eng.Fori(2, E - 3, 2) as e:
            one(e, 0)
            one(e + 1, 1)
        middle()
        one(E - 2, 0)
        one(E - 1, 1)

    def order(first, second, between=None):
        first(0)
        for g in range(1, NG):
            first(g)
            second(g - 1)
            if between:
                between(g - 1)
        second(NG - 1)
        if between:
            between(NG - 1)

    def has(e, k):
        return not isinstance(e, int) or e >= k

    def has_next(e):
        return not isinstance(e, int) or e < E - 1

    def loads(e, p):
        return ND * 8 * (e - p) + ND * 16

    def sync(sp):
        for s, v in weights_here:
            sp.wait_ge(s, v)
        if gated:
            sp.wait_ge(*zeroed(1))

        def one(e, p):
            if has(e, 2):
                if gated:
                    sp.wait_ge(*w_turned_ps(3 * e - 3))
                else:
                    sp.wait_ge(*y_ps(NG * e - NG))
            if gated:
                for k in range(2):
                    src = spec["weights"][k][bass.ds(e, 1)].rearrange("o i h -> (o i) h")
                    sp.dma_start(raw[:, p, k, 0:2 * P].rearrange("p (c h) -> p c h", h=P),
                                 src[0:2 * P, :].rearrange("(c p) h -> p c h", p=P)).then_inc(w_loaded[p].sem, 16)
                    sp.dma_start(raw[0:96, p, k, 2 * P:3 * P], src[2 * P:352, :]).then_inc(w_loaded[p].sem, 16)
                sp.dma_start(raw[:, p, 2, 0:352], spec["weights"][2][bass.ds(e, 1)].rearrange("o h i -> (o h) i")
                             ).then_inc(w_loaded[p].sem, 16)
            else:
                s1, s2, ee = spec["weights"](e)
                sp.dma_start(w1[:, p, :], s1[bass.ds(ee, 1)].rearrange("o d f -> (o d) f")).then_inc(w_loaded[p].sem, 16)
                sp.dma_start(w2[:, p, :, :], s2[bass.ds(ee, 1)].rearrange("o (c p) d -> p (o c) d", p=P)
                             ).then_inc(w_loaded[p].sem, 16)

        over_experts(sp, one, lambda: None)

    def tensor(pe):
        def route(g):
            of = m.ctxT if router == "ctx" else XNT
            if router == "x":
                pe.wait_ge(*xnT_ready(g + 1))
            for t in range(g * GT, (g + 1) * GT):
                mm = pe.matmul(J1[:, t * ER:(t + 1) * ER], of[:, t * P:(t + 1) * P], spec["wr"], start=True, stop=True)
            mm.then_inc(lg_ps.sem, 1)

        if early:
            norm.turn(pe, 2)
        m.begin(pe, start)
        if router == "ctx":
            for g in range(NG):
                route(g)
        for g in range(3 if early else 0, NG):
            norm.turn(pe, g)
            if router == "x" and g:
                for k in range(0 if g == 3 and early else g - 1, g):
                    route(k)
        if router == "x":
            route(NG - 1)

        def turn_weights(e, p):
            pe.wait_ge(*w_loaded[p](loads(e, p)))
            for k in range(3):
                if has(e, 1) or k == 2:
                    pe.wait_ge(*w_turned(3 * e + k - (1 if k == 2 else 2) if k != 2 else 3 * e + 1))
                elif k == 0:
                    pe.wait_ge(*xnT_ready(NG))
                else:
                    pe.wait_ge(*lg_ready(1))
                for c in range(C):
                    tr = pe.transpose((J0, J1, J0)[k][:, c * P:(c + 1) * P], raw[:, p, k, c * P:(c + 1) * P],
                                      m.ident[:, :])
                tr.then_inc(w_turned_ps.sem, 1)

        if gated:
            turn_weights(0, 0)

        def one(e, p):
            if gated:
                pe.wait_ge(*w_turned(3 * e + 3))
            else:
                pe.wait_ge(*w_loaded[p](loads(e, p)))

            def first(g):
                x = XNT[:, g * GW:(g + 1) * GW]
                if not has(e, 1):
                    pe.wait_ge(*xnT_ready(g + 1))
                for c in range(C):
                    k = C * NG * e + C * g + c
                    if gated:
                        if has(e, 1) or C * g + c >= 2:
                            pe.wait_ge(*h_ready(k - 1))
                        b = (C * g + c) % 2 * 2
                        pe.matmul(ring[b], w1[:, p, c * P:(c + 1) * P], x, start=True, stop=True)
                        pe.matmul(ring[b + 1], w1[:, p, (C + c) * P:(C + c + 1) * P], x, start=True,
                                  stop=True).then_inc(a_ps.sem, 1)
                    else:
                        if has(e, 1) or C * g + c >= 4:
                            pe.wait_ge(*h_ready(k - 3))
                        pe.matmul(ring[(C * g + c) % 4], w1[:, p, c * P:(c + 1) * P], x, start=True,
                                  stop=True).then_inc(a_ps.sem, 1)
                if gated and g == 1 and has_next(e):
                    turn_weights(e + 1, 1 - p)

            def second(g):
                u = NG * e + g
                for c in range(C):
                    pe.wait_ge(*h_ready(C * u + c + 1))
                    if c == 0 and (has(e, 1) or g >= 2):
                        pe.wait_ge(*combined(u - 1))
                    for i in range(GT):
                        mm = pe.matmul(Y[g % 2][:, i * P:(i + 1) * P], h[:, g % 2, c, i * P:(i + 1) * P],
                                       w2[:, p, c, :], start=(c == 0 and i == 0), stop=(c == C - 1),
                                       skip_group_check=True)
                mm.then_inc(y_ps.sem, 1)

            def next_norm(g):
                if g >= 2:
                    m.norm_after[tag].turn(pe, g - 2)

            order(first, second, next_norm if after and isinstance(e, int) and e == E - 1 else None)

        def middle():
            if not (router and spec.get("b2")):
                return
            pe.wait_ge(*gates_ready(1))
            pe.wait_ge(*sel_ready(R))
            gv = gates[:, :, :].rearrange("p t e -> p (t e)")
            for j in range(E * NT // P):
                tr = pe.transpose(J0[:, j * P:(j + 1) * P], gv[:, j * P:(j + 1) * P], m.ident[:, :])
            tr.then_inc(gT_ps.sem, 1)
            pe.wait_ge(*gT_ready(1))
            for g in range(NG):
                if g >= 1:
                    pe.wait_ge(*b2_added(g))
                lo = g * GT % R
                pe.matmul(J1[:, :], gT[:, g * GT // R, :], b2sel[:, lo:lo + GT, :].rearrange("p t d -> p (t d)"),
                          start=True, stop=True).then_inc(b2_ps.sem, 1)

        over_experts(pe, one, middle)

    def scalar(act):
        for g in range(NG):
            norm.evacuate(act, g)
        m.begin(act, start)
        if router:
            act.wait_ge(*exp_in(1))
            act.activation(wb[:, :], wb[:, :], ACT.Exp).then_inc(exp_out.sem, 1)
            if spec["whole"]:
                act.wait_ge(*exp_in(2))
                act.activation(A[:, :, :], A[:, :, :], ACT.Exp).then_inc(exp_out.sem, 1)

        def turned(e, p):
            for k in range(3):
                act.wait_ge(*w_turned_ps(3 * e + k + 1))
                if has(e, 2) and k == 0:
                    act.wait_ge(*y_ps(NG * e - NG))
                dst = w2[:, p].rearrange("p c d -> p (c d)") if k == 2 else w1[:, p, k * C * P:(k + 1) * C * P]
                act.activation(dst, (J0, J1, J0)[k][:, 0:C * P], ACT.Copy).then_inc(w_turned.sem, 1)

        if gated:
            turned(0, 0)

        def one(e, p):
            if not gated:
                act.wait_ge(*w_loaded[p](loads(e, p)))

            def first(g):
                u = NG * e + g
                for c in range(C):
                    k = C * u + c
                    act.wait_ge(*a_ps(k + 1))
                    if gated:
                        if has(e, 1) or C * g + c >= 2:
                            act.wait_ge(*h_ready(k - 1))
                        b = (C * g + c) % 2
                        act.activation(sg[:, b, :], ring[2 * b], ACT.Silu).then_inc(s_ready.sem, 1)
                    else:
                        if c == 0 and (has(e, 1) or g >= 2):
                            act.wait_ge(*y_ps(u - 1))
                        apart(act, m)
                        act.activation(h[:, g % 2, c, :], ring[(C * g + c) % 4], spec["func"],
                                       bias=spec["b1"][:, bass.ds(e * C + c, 1)]).then_inc(h_ready.sem, 1)
                if gated and g == 1 and has_next(e):
                    turned(e + 1, 1 - p)

            order(first, lambda g: None)

        def middle():
            if router and spec.get("b2"):
                act.wait_ge(*gT_ps(1))
                act.activation(gT[:, :, :].rearrange("p j q -> p (j q)"), J0[:, 0:E * NT // P * P],
                               ACT.Copy).then_inc(gT_ready.sem, 1)

        over_experts(act, one, middle)

    def gpsimd(pool):
        if gated:
            pool.memset(raw[:, :, :, :].rearrange("p a k f -> p (a k f)"), 0.0).then_inc(zeroed.sem, 1)
        for g in range(NG):
            norm.rstd(pool, g)
        m.begin(pool, start)
        if spec.get("residual"):
            pool.wait_ge(*xn_ready(NG))
            pool.tensor_tensor(m.X[:, :, :], m.X[:, :, :], xn[:, :, :], ALU.add).then_inc(x_plus.sem, 1)
        if not router:
            pool.wait_ge(*xn_ready(NG))
            pool.tensor_tensor(m.X[:, :, :], m.X[:, :, :],
                               spec["bo"].rearrange("p (o d) -> p o d", o=1).broadcast_to([P, NT, D]),
                               ALU.add).then_inc(b2_added.sem, 1)
        if router and spec.get("b2"):
            for t in range(R):
                pool.tensor_scalar(b2sel[:, t, :], spec["b2rep"][:, :], spec["tmask"][:, t:t + 1], None,
                                   ALU.mult).then_inc(sel_ready.sem, 1)

    def vector(dve):
        m.begin(dve, start)

        for g in range(0 if not early else NG, NG):
            norm.stats(dve, g)
            if g:
                norm.apply(dve, g - 1)
        norm.apply(dve, NG - 1)
        links = [0]

        def link(ins):
            ins.then_inc(g_chain.sem, 1)
            links[0] += 1
            dve.wait_ge(*g_chain(links[0]))

        def wide(r):
            return r[:, :].rearrange("p (t o) -> p t o", o=1).broadcast_to([P, NT, ER])

        def take_best(logits, best, onehot):
            link(dve.tensor_reduce(best[:, :], logits[:, :, :], AX, ALU.max))
            link(dve.tensor_tensor(Bt[:, :, :], logits[:, :, :], wide(best), ALU.is_ge))
            rev = m.rev[:, 16 - ER:16].rearrange("p (o e) -> p o e", o=1).broadcast_to([P, NT, ER])
            link(dve.tensor_tensor(Bt[:, :, :], Bt[:, :, :], rev, ALU.mult))
            link(dve.tensor_reduce(rm[:, :], Bt[:, :, :], AX, ALU.max))
            link(dve.tensor_tensor(onehot[:, :, :], Bt[:, :, :], wide(rm), ALU.is_equal))

        dve.wait_ge(*xn_ready(NG))
        if router:
            dve.wait_ge(*lg_ps(NG))
            lg = J1[:, 0:NT * ER].rearrange("p (t e) -> p t e", e=ER)
            if spec.get("br") is None:
                dve.tensor_copy(LG[:, :, :], lg).then_inc(lg_ready.sem, 1)
            else:
                dve.tensor_tensor(LG[:, :, :], lg, spec["br"].rearrange("p (o e) -> p o e", o=1).broadcast_to([P, NT, ER]),
                                  ALU.add).then_inc(lg_ready.sem, 1)
            dve.wait_ge(*lg_ready(1))
            take_best(LG, m1, O1)
            link(dve.scalar_tensor_tensor(out=Ct[:, :, :].rearrange("p t e -> p (t e)"),
                                          in0=O1[:, :, :].rearrange("p t e -> p (t e)"), scalar=NEG,
                                          in1=LG[:, :, :].rearrange("p t e -> p (t e)"), op0=ALU.mult, op1=ALU.add))
            take_best(Ct, m2, O2)
            dve.tensor_tensor(wb[:, :], m2[:, :], m1[:, :], ALU.subtract).then_inc(exp_in.sem, 1)
            if spec["whole"]:
                dve.tensor_tensor(A[:, :, :], LG[:, :, :], wide(m1), ALU.subtract).then_inc(exp_in.sem, 1)
                dve.wait_ge(*exp_out(2))
                link(dve.tensor_reduce(ws[:, :], A[:, :, :], AX, ALU.add))
            else:
                dve.wait_ge(*exp_out(1))
                link(dve.tensor_scalar(ws[:, :], wb[:, :], 1.0, None, ALU.add))
            link(dve.reciprocal(wa[:, :], ws[:, :]))
            link(dve.tensor_tensor(wb[:, :], wb[:, :], wa[:, :], ALU.mult))
            link(dve.tensor_tensor(O1[:, :, :], O1[:, :, :], wide(wa), ALU.mult))
            link(dve.tensor_tensor(O2[:, :, :], O2[:, :, :], wide(wb), ALU.mult))
            if E > ER:
                link(dve.memset(gates[:, :, ER:E], 1.0))
            dve.tensor_tensor(gates[:, :, 0:ER], O1[:, :, :], O2[:, :, :], ALU.add).then_inc(gates_ready.sem, 1)
            dve.wait_ge(*gates_ready(1))
            assert links[0] == LINKS
            if spec.get("residual"):
                dve.wait_ge(*x_plus(1))
        else:
            dve.wait_ge(*b2_added(1))

        def one(e, p):
            def first(g):
                if not gated:
                    return
                u = NG * e + g
                for c in range(C):
                    dve.wait_ge(*s_ready(C * u + c + 1))
                    if c == 0 and (has(e, 1) or g >= 2):
                        dve.wait_ge(*y_ps(u - 1))
                    b = (C * g + c) % 2
                    dve.tensor_tensor(h[:, g % 2, c, :], sg[:, b, :], ring[2 * b + 1], ALU.mult).then_inc(h_ready.sem, 1)

            def second(g):
                u = NG * e + g
                dve.wait_ge(*y_ps(u + 1))
                if has(e, 1):
                    dve.wait_ge(*combined(u - NG + 1))
                if not router:
                    xg = m.X[:, g * GT:(g + 1) * GT, :].rearrange("p t d -> p (t d)")
                    dve.tensor_tensor(xg, xg, Y[g % 2], ALU.add).then_inc(combined.sem, 1)
                    return
                for i in range(GT):
                    t = g * GT + i
                    st = dve.scalar_tensor_tensor(out=m.X[:, t, :], in0=Y[g % 2][:, i * P:(i + 1) * P],
                                                  scalar=gates[:, t, bass.ds(e, 1)], in1=m.X[:, t, :],
                                                  op0=ALU.mult, op1=ALU.add)
                st.then_inc(combined.sem, 1)

            def next_norm(g):
                dve.wait_ge(*combined(NG * e + g + 1))
                m.norm_after[tag].stats(dve, g)
                if g:
                    m.norm_after[tag].apply(dve, g - 1)

            order(first, second, next_norm if after and isinstance(e, int) and e == E - 1 else None)

        def middle():
            if router and spec.get("b2"):
                dve.wait_ge(*combined(NG * (E - 2)))
                for g in range(NG):
                    dve.wait_ge(*b2_ps(g + 1))
                    xg = m.X[:, g * GT:(g + 1) * GT, :].rearrange("p t d -> p (t d)")
                    dve.tensor_tensor(xg, xg, J1[:, :], ALU.add).then_inc(b2_added.sem, 1)
                dve.wait_ge(*b2_added(NG))

        over_experts(dve, one, middle)

    L.tensor, L.scalar, L.gpsimd, L.vector, L.sync = tensor, scalar, gpsimd, vector, sync
    return L


def quantised_ffn(sh, m, tag, start, w):
    nc = sh.nc
    C = 3
    K = C * NG
    QMAX = 32767.0
    L = Layer()
    with ExitStack() as scope:
        def sb(name, shape, dt=F32):
            return scope.enter_context(nc.sbuf_tensor(f"{tag}_{name}", shape, dt))

        G, U, SG = (sb(name, [P, K, GW]) for name in ("gate", "up", "sig"))
        am = sb("amax", [P, 5, 2 * K])
        a1, b1 = sb("amax_rows", [P, 5]), sb("amax_all", [P, 5])
        scale, inv = sb("scale", [P, 5]), sb("inv", [P, 5])
        us = sb("up_times_gate_scale", [P, 1])

    J0, J1 = m.banks[0], m.banks[1]
    norm = NormAll(sh, m)
    xn, XNT, xn_ready, xnT_ready = m.xn, m.XNT, norm.xn_ready, norm.xnT_ready
    signal = sh.counted_semaphore
    xmax = signal("x_max", 1)
    rows_max, turned, one_max, spread_ps = signal("rows_max", 5), signal("rows_turned", 5), signal("one_max", 5), signal("max_spread", 5)
    scale_set, inv_set, us_set = signal("scale_set", 5), signal("inv_set", 5), signal("us_set", 1)
    x_a, x_q = signal("x_scaled", NG), signal("x_quantised", NG)
    gu_ps, gu_here, gu_max = signal("gate_up_in_psum", 2 * K), signal("gate_up_here", 2 * K), signal("gate_up_max", 2 * K)
    g_a, g_q, sig, sig_a, sig_q = (signal("gate_scaled", K), signal("gate_quantised", K), signal("sigmoid", K), signal("sigmoid_scaled", K),
                                   signal("sigmoid_quantised", K))
    gs, gs_max = signal("gated", K), signal("gated_max", K)
    gs_a, u_a, u_q, o_here, o_max = (signal("gated_scaled", K), signal("up_scaled", K), signal("up_quantised", K), signal("o_here", K),
                                     signal("o_max", K))
    o_a, o_q, y_ps, x_done = signal("o_scaled", K), signal("o_quantised", K), signal("y_in_psum", NG), signal("x_done", NG)
    X_, G_, U_, S_, O_ = range(5)
    L.done = x_done(NG)

    def piece(x, k):
        return x[:, bass.ds(k, 1), :].rearrange("p o f -> p (o f)")

    def passes(eng, step, n, lag):
        for i in range(lag):
            step(i)
        with eng.Fori(lag, n) as i:
            step(i)
        for i in range(n, n + lag):
            step(i)

    def on(k):
        return not isinstance(k, int) or 0 <= k < K

    def quantise(dve, x, r, by=None):
        s = scale[:, r:r + 1] if by is None else by
        return dve.tensor_scalar(x, x, ROUND, s, ALU.subtract, ALU.mult)

    def tensor(pe):
        m.begin(pe, start)

        for g in range(NG):
            norm.turn(pe, g)
        pe.wait_ge(*xnT_ready(NG))

        def spread_max(r):
            pe.wait_ge(*rows_max(r + 1))
            pe.transpose(J0[0:1, 0:P], a1[:, r:r + 1], m.ident[:, :]).then_inc(turned.sem, 1)
            pe.wait_ge(*one_max(r + 1))
            pe.matmul(J1[:, 0:1], m.ones[0:1, :], b1[0:1, r:r + 1], start=True, stop=True).then_inc(spread_ps.sem, 1)

        spread_max(X_)

        def gate_up(g):
            pe.wait_ge(*x_q(g + 1))
            for j in range(2 * C):
                if not isinstance(g, int) or g >= 1:
                    pe.wait_ge(*gu_here(2 * C * g - 2 * C + j + 1))
                pe.matmul(m.banks[2 + j], w["gu"][:, j * P:(j + 1) * P], columns(XNT, g, GW), start=True,
                          stop=True).then_inc(gu_ps.sem, 1)

        gate_up(0)
        with pe.Fori(1, NG) as g:
            gate_up(g)
        for r in (G_, U_, S_, O_):
            spread_max(r)
        for g in range(NG):
            for c in range(C):
                pe.wait_ge(*o_q(C * g + c + 1))
                if c == 0 and g >= 2:
                    pe.wait_ge(*x_done(g - 1))
                for i in range(GT):
                    mm = pe.matmul(m.banks[2 + g % 2][:, i * P:(i + 1) * P], G[:, C * g + c, i * P:(i + 1) * P],
                                   w["d"][:, c * P:(c + 1) * P], start=(c == 0 and i == 0), stop=(c == C - 1),
                                   skip_group_check=True)
            mm.then_inc(y_ps.sem, 1)

    def scalar(act):
        m.begin(act, start)

        for g in range(NG):
            norm.evacuate(act, g)

        def gate_up(g):
            for j in range(2 * C):
                act.wait_ge(*gu_ps(2 * C * g + j + 1))
                apart(act, m)
                act.activation(piece((G, U)[j // C], C * g + j % C), m.banks[2 + j], ACT.Copy).then_inc(gu_here.sem, 1)

        with act.Fori(0, NG) as g:
            gate_up(g)

        def scaled(x, r, done):
            act.activation(x, x, ACT.Identity, bias=m.round[:, 0:1], scale=inv[:, r:r + 1]).then_inc(done.sem, 1)

        act.wait_ge(*inv_set(G_ + 1))
        act.wait_ge(*gu_here(2 * K))

        def gate_pass(n):
            if on(n):
                scaled(piece(G, n), G_, g_a)
            if on(n - 1):
                act.wait_ge(*g_q(n))
                apart(act, m)
                act.activation(piece(SG, n - 1), piece(G, n - 1), ACT.Sigmoid).then_inc(sig.sem, 1)
            if on(n - 2):
                act.wait_ge(*sig(n - 1))
                apart(act, m)
                act.activation(piece(SG, n - 2), piece(SG, n - 2), ACT.Identity, bias=m.round[:, 0:1],
                               scale=65536.0).then_inc(sig_a.sem, 1)

        passes(act, gate_pass, K, 2)
        act.wait_ge(*inv_set(U_ + 1))
        with act.Fori(0, K) as k:
            scaled(piece(U, k), U_, u_a)
        act.wait_ge(*inv_set(S_ + 1))
        with act.Fori(0, K) as k:
            scaled(piece(G, k), S_, gs_a)
        act.wait_ge(*inv_set(O_ + 1))
        with act.Fori(0, K) as k:
            scaled(piece(G, k), O_, o_a)

    def gpsimd(pool):
        m.begin(pool, start)

        for g in range(NG):
            norm.rstd(pool, g)

    def vector(dve):
        m.begin(dve, start)

        for g in range(NG):
            norm.stats(dve, g)
            if g:
                norm.apply(dve, g - 1)
        norm.apply(dve, NG - 1)
        dve.wait_ge(*xn_ready(NG))
        dve.tensor_reduce(am[:, X_, 0:1], xn[:, :, :].rearrange("p t d -> p (t d)"), AX, ALU.max,
                          apply_absolute_value=True).then_inc(xmax.sem, 1)

        def find_scale(r, src, seen, count):
            dve.wait_ge(*seen(count))
            dve.tensor_reduce(a1[:, r:r + 1], src, AX, ALU.max).then_inc(rows_max.sem, 1)
            dve.wait_ge(*turned(r + 1))
            dve.tensor_reduce(b1[0:1, r:r + 1], J0[0:1, 0:P], AX, ALU.max).then_inc(one_max.sem, 1)
            dve.wait_ge(*spread_ps(r + 1))
            dve.tensor_scalar(scale[:, r:r + 1], J1[:, 0:1], 1.0 / QMAX, 1e-12, ALU.mult, ALU.max).then_inc(scale_set.sem, 1)
            dve.wait_ge(*scale_set(r + 1))
            dve.reciprocal(inv[:, r:r + 1], scale[:, r:r + 1]).then_inc(inv_set.sem, 1)
            dve.wait_ge(*inv_set(r + 1))

        find_scale(X_, am[:, X_, 0:1], xmax, 1)
        dve.wait_ge(*xnT_ready(NG))

        def quantise_x(n):
            if isinstance(n, int) and n >= NG:
                pass
            else:
                dve.tensor_scalar(columns(XNT, n, GW), columns(XNT, n, GW), inv[:, X_:X_ + 1], ROUND, ALU.mult,
                                  ALU.add).then_inc(x_a.sem, 1)
            if not isinstance(n, int) or n >= 1:
                dve.wait_ge(*x_a(n))
                quantise(dve, columns(XNT, n - 1, GW), X_).then_inc(x_q.sem, 1)

        passes(dve, quantise_x, NG, 1)

        def greatest(g):
            for j in range(2 * C):
                dve.wait_ge(*gu_here(2 * C * g + j + 1))
                dve.tensor_reduce(am[:, (G_, U_)[j // C], bass.ds(C * g + j % C, 1)],
                                  piece((G, U)[j // C], C * g + j % C), AX, ALU.max,
                                  apply_absolute_value=True).then_inc(gu_max.sem, 1)

        with dve.Fori(0, NG) as g:
            greatest(g)
        find_scale(G_, am[:, G_, 0:K], gu_max, 2 * K)
        find_scale(U_, am[:, U_, 0:K], gu_max, 2 * K)

        def gate_pass(n):
            if on(n):
                dve.wait_ge(*g_a(n + 1))
                quantise(dve, piece(G, n), G_).then_inc(g_q.sem, 1)
            if on(n - 2):
                k = n - 2
                dve.wait_ge(*sig_a(k + 1))
                dve.tensor_scalar(piece(SG, k), piece(SG, k), ROUND, 65535.0, ALU.subtract, ALU.min).then_inc(sig_q.sem, 1)
            if on(n - 3):
                k = n - 3
                dve.wait_ge(*sig_q(k + 1))
                dve.scalar_tensor_tensor(out=piece(G, k), in0=piece(SG, k), scalar=1.0 / 65536.0, in1=piece(G, k),
                                         op0=ALU.mult, op1=ALU.mult).then_inc(gs.sem, 1)
            if on(n - 4):
                k = n - 4
                dve.wait_ge(*gs(k + 1))
                dve.tensor_reduce(am[:, S_, bass.ds(k, 1)], piece(G, k), AX, ALU.max,
                                  apply_absolute_value=True).then_inc(gs_max.sem, 1)

        passes(dve, gate_pass, K, 4)
        find_scale(S_, am[:, S_, 0:K], gs_max, K)
        dve.tensor_tensor(us[:, :], scale[:, U_:U_ + 1], scale[:, S_:S_ + 1], ALU.mult).then_inc(us_set.sem, 1)
        dve.wait_ge(*us_set(1))

        def o_pass(n):
            if on(n):
                dve.wait_ge(*u_a(n + 1))
                quantise(dve, piece(U, n), U_, us[:, 0:1]).then_inc(u_q.sem, 1)
            if on(n - 1):
                k = n - 1
                dve.wait_ge(*u_q(k + 1))
                dve.wait_ge(*gs_a(k + 1))
                dve.scalar_tensor_tensor(out=piece(G, k), in0=piece(G, k), scalar=ROUND, in1=piece(U, k),
                                         op0=ALU.subtract, op1=ALU.mult).then_inc(o_here.sem, 1)
            if on(n - 2):
                k = n - 2
                dve.wait_ge(*o_here(k + 1))
                dve.tensor_reduce(am[:, O_, bass.ds(k, 1)], piece(G, k), AX, ALU.max,
                                  apply_absolute_value=True).then_inc(o_max.sem, 1)

        passes(dve, o_pass, K, 2)
        find_scale(O_, am[:, O_, 0:K], o_max, K)
        with dve.Fori(0, K) as k:
            dve.wait_ge(*o_a(k + 1))
            quantise(dve, piece(G, k), O_).then_inc(o_q.sem, 1)
        for g in range(NG):
            dve.wait_ge(*y_ps(g + 1))
            xg = m.X[:, g * GT:(g + 1) * GT, :].rearrange("p t d -> p (t d)")
            dve.tensor_tensor(xg, xg, m.banks[2 + g % 2], ALU.add).then_inc(x_done.sem, 1)

    L.tensor, L.scalar, L.gpsimd, L.vector = tensor, scalar, gpsimd, vector
    return L


def block_quantised_weights(sh, m, ins, load, loaded, count):
    C, NB = 3, 12
    raw, q = sh.sb("qw_raw", [P, 3, C * P]), sh.sb("qw_rounded", [P, 3, C * P])
    s, rs = sh.sb("qw_scale", [P, 3, NB]), sh.sb("qw_inverse", [P, 3, NB])
    gu, d = sh.sb("qw_gate_up", [P, 2 * C * P]), sh.sb("qw_down", [P, C * P])
    for k, name in enumerate(("gate", "up")):
        load(raw[:, k, :].rearrange("p (c h) -> p c h", h=P), ins[f"L3_ffn_w_{name}"].rearrange("(c p) h -> p c h", p=P))
    load(raw[:, 2, :], ins["L3_ffn_w_down"])
    chain = sh.sem("qw_chain")
    turned_ps, turned = sh.sem("qw_turned_ps"), sh.sem("qw_turned")
    flat = lambda x: x[:, :, :].rearrange("p k f -> p (k f)")
    blocks = lambda x: flat(x).rearrange("p (n b) -> p n b", b=32)
    spread = lambda x: flat(x).rearrange("p (n o) -> p n o", o=1).broadcast_to([P, 3 * NB, 32])

    def vector(dve):
        dve.wait_ge(loaded, count())
        dve.tensor_reduce(flat(s), blocks(raw), AX, ALU.max, apply_absolute_value=True).then_inc(chain, 1)
        dve.wait_ge(chain, 1)
        dve.tensor_scalar(flat(s), flat(s), 1.0 / 7.0, 1e-12, ALU.mult, ALU.max).then_inc(chain, 1)
        dve.wait_ge(chain, 2)
        dve.reciprocal(flat(rs), flat(s)).then_inc(chain, 1)
        dve.wait_ge(chain, 3)
        dve.tensor_tensor(blocks(q), blocks(raw), spread(rs), ALU.mult).then_inc(chain, 1)
        dve.wait_ge(chain, 4)
        dve.tensor_scalar(flat(q), flat(q), ROUND, ROUND, ALU.add, ALU.subtract).then_inc(chain, 1)
        dve.wait_ge(chain, 5)
        dve.tensor_scalar(flat(q), flat(q), 7.0, -8.0, ALU.min, ALU.max).then_inc(chain, 1)
        dve.wait_ge(chain, 6)
        dve.tensor_tensor(blocks(q), blocks(q), spread(s), ALU.mult).then_inc(chain, 1)

    def tensor(pe):
        pe.wait_ge(chain, 7)
        for k in range(3):
            if k >= 1:
                pe.wait_ge(turned, k)
            for c in range(C):
                tr = pe.transpose(m.banks[4][:, c * P:(c + 1) * P], q[:, k, c * P:(c + 1) * P], m.ident[:, :])
            tr.then_inc(turned_ps, 1)

    def scalar(act):
        for k in range(3):
            act.wait_ge(turned_ps, k + 1)
            dst = d[:, :] if k == 2 else gu[:, k * C * P:(k + 1) * C * P]
            act.activation(dst, m.banks[4][:, 0:C * P], ACT.Copy).then_inc(turned, 1)

    L = Layer()
    L.tensor, L.scalar, L.vector, L.done = tensor, scalar, vector, (turned, 3)
    return L, {"gu": gu, "d": d}


def build(nc, ins, out, which=tuple(range(8))):
    ctx = ExitStack()
    with ctx:
        sh = Shared(nc, ctx)
        sb, sem = sh.sb, sh.sem

        class M:
            pass

        m = M()
        m.X = sb("X", [P, NT, D])
        m.ctxT = sb("ctxT", [P, TOK])
        m.xn = sb("xn", [P, NT, P])
        m.XNT = sb("XNT", [P, TOK])
        m.stats, m.meanvar = sb("stats", [P, NT, 6]), sb("meanvar", [P, NT, 2])
        m.vareps, m.rstd = sb("vareps", [P, NT]), sb("rstd", [P, NT])
        m.ident = sb("ident", [P, P])
        m.nhalf = sb("nhalf", [P, 1])
        m.hmask = sb("hmask", [P, H])
        m.vmask = sb("vmask", [P, H, S])
        m.maskbias = sb("maskbias", [P, NT, S])
        m.rowvalid = sb("rowvalid", [P, NT])
        ctx_raw = sb("ctx_raw", [P, NT, D])
        psum = sh.ps("psum", [P, 8, 512])
        m.banks = [psum[:, i, :] for i in range(8)]
        m.wide = [psum[:, 2:4, :], psum[:, 4:6, :], psum[:, 6:8, :]]

        loaded, consts, turned_ps, turned = sem("loaded"), sem("consts"), sem("turned_ps"), sem("turned")
        m.passed = sem("passed")
        NLOAD = [0]
        NCONST = [0]
        loads = []

        def load(dst, src):
            loads.append((dst, src))
            NLOAD[0] += 16

        load(ctx_raw[:, :, :], ins["ctx_1024"].rearrange("(t u) s d -> (u s) t d", u=2))
        load(m.X[:, :, :], ins["x"].rearrange("(t u) s d -> (u s) t d", u=2))

        rows, cols = sb("rows", [P, P]), sb("cols", [P, P])
        row = [0]

        def columns_of(src):
            n = src.shape[0]
            load(rows[row[0]:row[0] + n, :], src)
            row[0] += n
            return cols[:, row[0] - n:row[0]]

        def column(src):
            return columns_of(src.rearrange("(o p) -> o p", o=1))

        def spread(name, src):
            c = sb(name, [P, src.shape[0]])
            load(c[:, :], src.rearrange("(o n) -> o n", o=1).partition_broadcast(P))
            return c[:, :]

        def matrix(name, src):
            c = sb(name, [P, src.shape[1]])
            load(c[:, :], src)
            return c[:, :]

        w0 = {k: matrix(f"L0w{k}", ins[f"L0_xattn_W{k}"]) for k in "qkvo"}
        b0 = {k: column(ins[f"L0_xattn_b{k}"]) for k in "qkv"}
        b0["o"] = spread("L0bo", ins["L0_xattn_bo"])
        w1 = {"q": matrix("L1wq", ins["L1_xattn_w_q"]), "k": matrix("L1wk", ins["L1_xattn_w_kv"][:, 0:1024]),
              "v": matrix("L1wv", ins["L1_xattn_w_kv"][:, 1024:2048]),
              "gamma": column(ins["L1_xattn_ln_gamma"]), "beta": column(ins["L1_xattn_ln_beta"]),
              "bo": spread("L1bo", ins["L1_xattn_b_out"])}
        w1o = sb("L1wo", [P, HP, D])
        load(w1o[:, :, :], ins["L1_xattn_w_out"].rearrange("(c p) d -> p c d", p=P))
        w1["o"] = w1o
        gate_raw, gate = spread("L1gate_raw", ins["L1_xattn_gate"]), sb("L1gate", [P, 1])
        w1["gate"] = gate[:, 0:1]
        gate_ready = sem("gate_ready")
        b2 = {}
        for name, E, parts in (("L1", 16, [("L1_ffn_routed_b2", 14), ("L1_ffn_shared_b2", 2)]),
                               ("L2", 8, [("L2_xattn_b2", 8)])):
            b2[name] = sb(f"{name}b2rep", [P, D])
            for r in range(P // E):
                at = r * E
                for src, k in parts:
                    load(b2[name][at:at + k, :], ins[src])
                    at += k
        f0b2 = spread("F0b2", ins["L0_ffn_b2"])
        wr1, br1 = matrix("L1wr", ins["L1_ffn_router_w"]), spread("L1br", ins["L1_ffn_router_b"])
        wr2, br2 = matrix("L2wr", ins["L2_xattn_Wg"]), spread("L2br", ins["L2_xattn_bg"])
        wr3 = columns_of(ins["L2_ffn_w_router"])
        b1_0 = columns_of(ins["L0_ffn_b1"].rearrange("(c p) -> c p", p=P))
        b1_1 = columns_of(ins["L1_ffn_routed_b1"])
        columns_of(ins["L1_ffn_shared_b1"])
        b1_1 = cols[:, row[0] - 16:row[0]]
        b1_2 = columns_of(ins["L2_xattn_b1"].rearrange("e (c p) -> (e c) p", p=P))
        m.rev = sb("rev", [P, 16])
        tmask16, tmask8 = sb("tmask16", [P, 8]), sb("tmask8", [P, 16])
        mask_rows, mask_keys = sb("mask_rows", [NT, P], U8), sb("mask_keys", [P, NT, S], U8)
        load(mask_rows[:, :], ins["mask_BxS2_bf1"].rearrange("(t u) s -> t (u s)", u=2))
        load(mask_keys[:, :, :], ins["mask_BxSxS2_bk0"].rearrange("(t u) s k -> (u s) t k", u=2))
        rows_f, rows_c, valid = sb("rows_f", [NT, P]), sb("rows_c", [P, NT]), sb("valid", [P, NT, S])
        mask_set, mask_ps, mask_turned = sem("mask_set"), sem("mask_ps"), sem("mask_turned")
        w3_raw, w3_sb = sb("L3w_raw", [P, 4, P]), sb("L3w", [P, 4, P])
        for k, c in enumerate("qkvo"):
            load(w3_raw[:, k, :], ins[f"L3_xattn_W{c}"])
        w3 = {c: w3_sb[:, k, :] for k, c in enumerate("qkvo")}
        m.ones, m.round = sb("ones", [P, P]), sb("round", [P, 1])
        QW, qw = block_quantised_weights(sh, m, ins, load, loaded, lambda: NLOAD[0])
        PRE = NT // 4
        m.setup = None

        def begin(eng, start):
            for s, v in start:
                eng.wait_ge(s, v)

        m.begin = begin
        m.weights_here = []
        m.weight_buffers = {tag: (sb(f"{tag}_w1", [P, 2, C * P]), sb(f"{tag}_w2", [P, 2, C, D]))
                            for tag, C in (("F0", 4), ("E1", 1), ("E2", 4))}
        m.weight_buffers["E3"] = (sb("E3_raw", [P, 2, 3, 3 * P]),)
        m.norm_after = {}
        PRE += 2
        start0 = [(loaded, NLOAD[0]), (consts, 18), (turned, PRE)]

        makers = {
            0: lambda st: small_head_attention(sh, m, "A0", st, w0, b0, False),
            2: lambda st: wide_head_attention(sh, m, "A1", st + [(gate_ready, 1)], w1),
        }
        makers[1] = lambda st: experts(sh, m, "F0", st, dict(
            E=1, C=4, func=ACT.Gelu, bo=f0b2,
            weights=lambda e: (ins["L0_ffn_w1"].rearrange("(o d) f -> o d f", o=1),
                               ins["L0_ffn_w2"].rearrange("(o d) f -> o d f", o=1),
                               e), b1=b1_0))

        def weights1(e):
            if isinstance(e, int) and e >= 14:
                return ins["L1_ffn_shared_w1"], ins["L1_ffn_shared_w2"], e - 14
            return ins["L1_ffn_routed_w1"], ins["L1_ffn_routed_w2"], e

        makers[3] = lambda st: experts(sh, m, "E1", st, dict(
            then_norm=4 in which,
            E=16, C=1, func=ACT.Gelu, router="x", ER=14, wr=wr1, br=br1, whole=True, residual=True, b2=True,
            b2rep=b2["L1"], tmask=tmask16, b1=b1_1, weights=weights1))
        makers[4] = lambda st: experts(sh, m, "E2", st, dict(
            then_norm=5 in which, early=3 in which,
            E=8, C=4, func=ACT.Relu, router="ctx", ER=8, wr=wr2, br=br2, whole=False, b2=True,
            b2rep=b2["L2"], tmask=tmask8, b1=b1_2,
            weights=lambda e: (ins["L2_xattn_W1"], ins["L2_xattn_W2"], e)))
        makers[5] = lambda st: experts(sh, m, "E3", st, dict(
            early=4 in which,
            E=8, C=3, gated=True, router="x", ER=8, wr=wr3, br=None, whole=False,
            weights=(ins["L2_ffn_w_gate"], ins["L2_ffn_w_up"], ins["L2_ffn_w_down"])))
        makers[6] = lambda st: small_head_attention(sh, m, "A3", st + [(mask_set, 3)], w3, dict.fromkeys("qkvo"), True)
        makers[7] = lambda st: quantised_ffn(sh, m, "Q3", st + [QW.done], qw)
        early_norm = {3: "E1", 4: "E2"}
        layers, st = [], start0
        for k in which:
            layers.append(makers[k](st))
            if k - 1 in early_norm and k - 1 in which:
                m.norm_after[early_norm[k - 1]] = layers[-1].norm
            st = [layers[-1].done]
        final = layers[-1].done

        stored = sem("stored")
        block = ctx.enter_context(nc.Block())

        @block.sync
        def _(sp):
            for dst, src in loads:
                sp.dma_start(dst, src).then_inc(loaded, 16)
            for L in layers:
                if L.sync:
                    L.sync(sp)
            sp.wait_ge(final[0], final[1])
            sp.dma_start(out.rearrange("(t u) s d -> (u s) t d", u=2), m.X[:, :, :]).then_inc(stored, 16)
            sp.wait_ge(stored, 16)

        @block.gpsimd
        def _(pool):
            pool.memset(m.ident[:, :], 0.0).then_inc(consts, 1)
            pool.memset(m.nhalf[:, :], -0.5).then_inc(consts, 1)
            pool.memset(m.hmask[:, :], 1.0).then_inc(consts, 1)
            pool.memset(m.vmask[:, :, :], 0.0).then_inc(consts, 1)
            pool.wait_ge(consts, 4)
            pool.affine_select(out=m.ident[:, :], in_=m.ident[:, :], compare_op=ALU.not_equal, fill=1.0,
                               base=0, pattern=[[-1, P]], channel_multiplier=1).then_inc(consts, 1)
            dh = D // H
            pool.affine_select(out=m.hmask[:, :], in_=m.hmask[:, :], compare_op=ALU.is_ge, fill=0.0,
                               base=0, pattern=[[-dh, H]], channel_multiplier=1).then_inc(consts, 1)
            pool.wait_ge(consts, 6)
            pool.affine_select(out=m.hmask[:, :], in_=m.hmask[:, :], compare_op=ALU.is_ge, fill=0.0,
                               base=dh - 1, pattern=[[dh, H]], channel_multiplier=-1).then_inc(consts, 1)
            for u in range(2):
                pool.wait_ge(consts, 7 + u)
                pool.memset(m.vmask[u * S:(u + 1) * S, u::2, :], 1.0).then_inc(consts, 1)
            pool.wait_ge(consts, 9)
            pool.iota(m.rev[:, :], pattern=[[-1, 16]], base=16, channel_multiplier=0,
                      allow_small_or_imprecise_dtypes=True).then_inc(consts, 1)
            for tm, E in ((tmask16, 16), (tmask8, 8)):
                pool.memset(tm[:, :], 1.0).then_inc(consts, 1)
            pool.wait_ge(consts, 12)
            for tm, E in ((tmask16, 16), (tmask8, 8)):
                pool.affine_select(out=tm[:, :], in_=tm[:, :], compare_op=ALU.is_ge, fill=0.0,
                                   base=0, pattern=[[-E, P // E]], channel_multiplier=1).then_inc(consts, 1)
            pool.wait_ge(consts, 14)
            for tm, E in ((tmask16, 16), (tmask8, 8)):
                pool.affine_select(out=tm[:, :], in_=tm[:, :], compare_op=ALU.is_ge, fill=0.0,
                                   base=E - 1, pattern=[[E, P // E]], channel_multiplier=-1).then_inc(consts, 1)
            pool.memset(m.ones[:, :], 1.0).then_inc(consts, 1)
            pool.memset(m.round[:, :], ROUND).then_inc(consts, 1)
            pool.wait_ge(consts, 18)
            pool.wait_ge(loaded, NLOAD[0])
            for L in layers:
                L.gpsimd(pool)

        @block.tensor
        def _(pe):
            pe.wait_ge(loaded, NLOAD[0])
            pe.wait_ge(consts, 18)
            for g in range(NG):
                if g >= 2:
                    pe.wait_ge(turned, g - 1)
                for i in range(4):
                    tr = pe.transpose(m.banks[g % 2][:, i * P:(i + 1) * P], ctx_raw[:, 4 * g + i, :], m.ident[:, :])
                tr.then_inc(turned_ps, 1)
            nrow = row[0]
            pe.transpose(m.banks[2][:, 0:nrow], rows[0:nrow, :], m.ident[0:nrow, 0:nrow]).then_inc(turned_ps, 1)
            for k in range(4):
                tr = pe.transpose(m.banks[3][:, k * P:(k + 1) * P], w3_raw[:, k, :], m.ident[:, :])
            tr.then_inc(turned_ps, 1)
            pe.wait_ge(mask_set, 1)
            pe.transpose(m.banks[5][:, 0:NT], rows_f[:, :], m.ident[0:NT, 0:NT]).then_inc(mask_ps, 1)
            QW.tensor(pe)
            for L in layers:
                L.tensor(pe)

        @block.scalar
        def _(act):
            act.wait_ge(loaded, NLOAD[0])
            act.activation(gate[:, :], gate_raw, ACT.Tanh).then_inc(gate_ready, 1)
            for g in range(NG):
                act.wait_ge(turned_ps, g + 1)
                act.activation(m.ctxT[:, g * GW:(g + 1) * GW], m.banks[g % 2], ACT.Copy).then_inc(turned, 1)
            act.wait_ge(turned_ps, PRE)
            act.activation(cols[:, 0:row[0]], m.banks[2][:, 0:row[0]], ACT.Copy).then_inc(turned, 1)
            act.activation(w3_sb[:, :, :].rearrange("p k f -> p (k f)"), m.banks[3], ACT.Copy).then_inc(turned, 1)
            QW.scalar(act)
            for L in layers:
                L.scalar(act)

        @block.vector
        def _(dve):
            dve.wait_ge(loaded, NLOAD[0])
            dve.tensor_copy(rows_f[:, :], mask_rows[:, :]).then_inc(mask_set, 1)
            dve.wait_ge(mask_ps, 1)
            dve.tensor_copy(rows_c[:, :], m.banks[5][:, 0:NT]).then_inc(mask_turned, 1)
            dve.wait_ge(mask_turned, 1)
            dve.tensor_tensor(valid[:, :, :], mask_keys[:, :, :],
                              rows_c[:, :].rearrange("p (t o) -> p t o", o=1).broadcast_to([P, NT, S]),
                              ALU.mult).then_inc(mask_turned, 1)
            dve.wait_ge(mask_turned, 2)
            dve.tensor_reduce(m.rowvalid[:, :], valid[:, :, :], AX, ALU.max).then_inc(mask_set, 1)
            dve.tensor_scalar(m.maskbias[:, :, :], valid[:, :, :], -NEG, NEG, ALU.mult, ALU.add).then_inc(mask_set, 1)
            QW.vector(dve)
            for L in layers:
                L.vector(dve)


_INS = [
    "x", "ctx_1024", "mask_BxS2_bf1", "mask_BxSxS2_bk0", "L0_xattn_Wq", "L0_xattn_bq", "L0_xattn_Wk",
    "L0_xattn_bk", "L0_xattn_Wv", "L0_xattn_bv", "L0_xattn_Wo", "L0_xattn_bo", "L0_ffn_w1", "L0_ffn_b1",
    "L0_ffn_w2", "L0_ffn_b2", "L1_xattn_ln_gamma", "L1_xattn_ln_beta", "L1_xattn_w_q", "L1_xattn_w_kv",
    "L1_xattn_w_out", "L1_xattn_b_out", "L1_xattn_gate", "L1_ffn_router_w", "L1_ffn_router_b", "L1_ffn_shared_w1",
    "L1_ffn_shared_b1", "L1_ffn_shared_w2", "L1_ffn_shared_b2", "L1_ffn_routed_w1", "L1_ffn_routed_b1",
    "L1_ffn_routed_w2", "L1_ffn_routed_b2", "L2_xattn_Wg", "L2_xattn_bg", "L2_xattn_W1", "L2_xattn_b1",
    "L2_xattn_W2", "L2_xattn_b2", "L2_ffn_w_router", "L2_ffn_w_gate", "L2_ffn_w_up", "L2_ffn_w_down",
    "L3_xattn_Wq", "L3_xattn_Wk", "L3_xattn_Wv", "L3_xattn_Wo", "L3_ffn_w_gate", "L3_ffn_w_up", "L3_ffn_w_down",
]


def kernel(**inputs):
    import numpy as np
    from concourse import bacc
    from concourse.bass_utils import run_bass_kernel_spmd

    nc = bacc.Bacc("TRN2", target_bir_lowering=False, num_devices=1)
    arrays, ins = {}, {}
    for name in _INS:
        a = np.ascontiguousarray(inputs[name])
        arrays[f"in_{name}"] = a
        ins[name] = nc.dram_tensor(f"in_{name}", a.shape, mybir.dt.from_np(a.dtype), kind="ExternalInput").ap()
    out = nc.dram_tensor("out", (B, S, D), F32, kind="ExternalOutput").ap()
    build(nc, ins, out)
    r = run_bass_kernel_spmd(nc, [arrays], core_ids=[0])
    return r.results[0]["out"]
```

```python
from contextlib import ExitStack

import concourse.bass as bass
from concourse import mybir

ALU = mybir.AluOpType
ACT = mybir.ActivationFunctionType
F32 = mybir.dt.float32
F32R = mybir.dt.float32r
U8 = mybir.dt.uint8
AX = mybir.AxisListType.X

P = 128
B, S, D = 32, 64, 128
TOK = B * S
NT = TOK // P
GT = 4
NG = NT // GT
GW = GT * P
H = 16
HP = H // 2
EPS = 1e-5
NEG = -1.0e30
ROUND = 1.5 * 2.0 ** 23


def live(t):
    return not isinstance(t, int) or 0 <= t < NT


def past(t, k):
    return not isinstance(t, int) or t >= k


def before_end(t, k):
    return not isinstance(t, int) or t < NT - k


def pipeline(eng, step, lo, hi, end):
    for n in range(lo):
        step(n, n % 2)
    with eng.Fori(lo, hi - 1, 2) as i:
        step(i, lo % 2)
        step(i + 1, (lo + 1) % 2)
    for n in range(hi, end):
        step(n, n % 2)


class Layer:

    def __init__(self):
        self.tensor = self.vector = self.scalar = self.gpsimd = self.sync = None
        self.done = None


def tile_of(x, t):
    return x[:, bass.ds(t, 1), :].rearrange("p a d -> p (a d)")


def columns(x, t, n):
    return x[:, bass.ds(t * n, n)]


def apart(eng, m):
    eng.sem_inc(m.passed, 1)


class Signal:

    def __init__(self, sem, base):
        self.sem, self.base = sem, base

    def __call__(self, n):
        return self.sem, self.base + n


class Shared:

    def __init__(self, nc, ctx):
        self.nc, self.ctx, self.counted = nc, ctx, {}

    def sb(self, name, shape, dt=F32):
        return self.ctx.enter_context(self.nc.sbuf_tensor(name, shape, dt))

    def ps(self, name, shape, dt=F32):
        return self.ctx.enter_context(self.nc.psum_tensor(name, shape, dt))

    def sem(self, name):
        return self.ctx.enter_context(self.nc.semaphore(name))

    def counted_semaphore(self, name, total):
        sem, base = self.counted.get(name) or (self.sem(name), 0)
        self.counted[name] = (sem, base + total)
        return Signal(sem, base)


class Norm:

    def __init__(self, sh, sb, tag, m, kind="norm"):
        self.st, self.mv = sb(f"{tag}_stats", [P, 2, 6]), sb(f"{tag}_meanvar", [P, 2, 2])
        self.ve, self.rs = sb(f"{tag}_vareps", [P, 2, 1]), sb(f"{tag}_rstd", [P, 2, 1])
        self.stats_chain = sh.counted_semaphore(f"{kind}_stats_chain", 2 * NT)
        self.var_ready = sh.counted_semaphore(f"{kind}_var_ready", NT)
        self.rstd_ready = sh.counted_semaphore(f"{kind}_rstd_ready", NT)
        self.nhalf, self.passed = m.nhalf, m.passed

    def stats(self, dve, x, t, p):
        if past(t, 2):
            dve.wait_ge(*self.rstd_ready(t - 1))
        dve.bn_stats(self.st[:, p, :], x).then_inc(self.stats_chain.sem, 1)
        dve.wait_ge(*self.stats_chain(2 * t + 1))
        apart(dve, self)
        dve.bn_aggr(self.mv[:, p, :], self.st[:, p, :]).then_inc(self.stats_chain.sem, 1)
        dve.wait_ge(*self.stats_chain(2 * t + 2))
        dve.tensor_scalar(self.ve[:, p, :], self.mv[:, p, 1:2], EPS, None, ALU.add).then_inc(self.var_ready.sem, 1)

    def rstd(self, pool, t, p, applied):
        pool.wait_ge(*self.var_ready(t + 1))
        if past(t, 2):
            pool.wait_ge(*applied(t - 1))
        pool.tensor_tensor(self.rs[:, p, :], self.ve[:, p, :], self.nhalf[:, :], ALU.pow).then_inc(self.rstd_ready.sem, 1)

    def apply(self, dve, out, x, t, p):
        dve.wait_ge(*self.rstd_ready(t + 1))
        return dve.tensor_scalar(out, x, self.mv[:, p, 0:1], self.rs[:, p, 0:1], ALU.subtract, ALU.mult)


class NormAll:

    def __init__(self, sh, m, split):
        self.seen = sh.counted_semaphore("all_stats", NT)
        self.aggregated = sh.counted_semaphore("all_aggregated", NT)
        self.var_ready = sh.counted_semaphore("all_var_ready", NG)
        self.rstd_ready = sh.counted_semaphore("all_rstd_ready", NG)
        self.xn_ready = sh.counted_semaphore("all_xn_ready", NG)
        self.xnT_ps = sh.counted_semaphore("all_xnT_in_psum", NG)
        self.xnT_ready = sh.counted_semaphore("all_xnT_ready", NG)
        self.split_ready = sh.counted_semaphore("all_xnT_split", NG if split else 0)
        self.m, self.split = m, split
        self.bank = m.banks[0]
        self.route = None

    def tile_stats(self, dve, t):
        out = self.m.stats[:, bass.ds(t, 1), :].rearrange("p o s -> p (o s)")
        dve.bn_stats(out, tile_of(self.m.X, t)).then_inc(self.seen.sem, 1)

    def stats(self, dve, g, seen=False):
        m = self.m
        ts = slice(g * GT, (g + 1) * GT)
        if not seen:
            for t in range(g * GT, (g + 1) * GT):
                self.tile_stats(dve, t)
        dve.wait_ge(*self.seen(g * GT + GT))
        for t in range(g * GT, (g + 1) * GT):
            dve.bn_aggr(m.meanvar[:, t, :], m.stats[:, t, :]).then_inc(self.aggregated.sem, 1)
        dve.wait_ge(*self.aggregated(g * GT + GT))
        dve.tensor_scalar(m.vareps[:, ts], m.meanvar[:, ts, 1], EPS, None, ALU.add).then_inc(self.var_ready.sem, 1)

    def rstd(self, pool, g):
        m = self.m
        ts = slice(g * GT, (g + 1) * GT)
        pool.wait_ge(*self.var_ready(g + 1))
        pool.tensor_tensor(m.rstd[:, ts], m.vareps[:, ts], m.nhalf[:, :].broadcast_to([P, GT]),
                           ALU.pow).then_inc(self.rstd_ready.sem, 1)

    def apply(self, dve, g):
        m = self.m
        dve.wait_ge(*self.rstd_ready(g + 1))
        for i in range(GT):
            t = g * GT + i
            ap = dve.tensor_scalar(m.xn[:, t, :], m.X[:, t, :], m.meanvar[:, t, 0:1], m.rstd[:, t:t + 1],
                                   ALU.subtract, ALU.mult)
        ap.then_inc(self.xn_ready.sem, 1)

    def turn(self, pe, g):
        pe.wait_ge(*self.xn_ready(g + 1))
        if g:
            pe.wait_ge(*self.xnT_ready(g))
        for i in range(GT):
            tr = pe.transpose(self.bank[:, i * P:(i + 1) * P], self.m.xn[:, g * GT + i, :], self.m.ident[:, :])
        tr.then_inc(self.xnT_ps.sem, 1)

    def evacuate(self, act, g):
        act.wait_ge(*self.xnT_ps(g + 1))
        cols = slice(g * GW, (g + 1) * GW)
        if self.split:
            act.activation(self.split[0][:, cols], self.bank, ACT.Copy)
        act.activation(self.m.XNT[:, cols], self.bank, ACT.Copy).then_inc(self.xnT_ready.sem, 1)

    def low_part(self, pool, g):
        pool.wait_ge(*self.xnT_ready(g + 1))
        cols = slice(g * GW, (g + 1) * GW)
        hi, lo = self.split
        pool.tensor_tensor(lo[:, cols], self.m.XNT[:, cols], hi[:, cols], ALU.subtract).then_inc(self.split_ready.sem, 1)


def small_head_attention(sh, m, tag, start, w, bias, masked, early=False):
    nc = sh.nc
    dh = D // H
    scale = float(dh) ** -0.5
    L = Layer()
    with ExitStack() as scope:
        def sb(name, shape, dt=F32):
            return scope.enter_context(nc.sbuf_tensor(f"{tag}_{name}", shape, dt))

        norm = NormAll(sh, m, None) if early else Norm(sh, sb, f"{tag}_ln", m)
        if not early:
            xn = sb("xn", [P, 2, P])
        if not early:
            xnT = sb("xnT", [P, 2, P])
        qT = sb("qT", [P, 2, P])
        kT = sb("kT", [P, 2, P])
        ctx2 = sb("ctx2", [P, 2, 2, 2, S])
        kexp = sb("kexp", [P, 2, 2, H, S])
        vbd = sb("vbd", [P, 2, 2, H, dh + 1])
        prob = sb("prob", [P, 2, H, S])
        probT = sb("probT", [P, 2, HP, P])
        mx = sb("mx", [P, 2, H])
        rc = sb("rc", [P, 2, H])
        on = sb("on", [P, 2, P])
        oT = sb("oT", [P, 2, P])
        tmp = sb("tmp", [P, 2, P])

    J0, J1 = m.banks[0], m.banks[1]
    pS, pP, pO, J2 = m.wide[0], m.wide[1], m.banks[6], m.banks[7]
    sv = pS.rearrange("p a (h k) -> p (a h) k", k=S)

    signal = sh.counted_semaphore
    MC = RC = 2 if masked else 1
    vones = signal("vones_set", 5)
    if not early:
        xn_ready, xnT_ready, xnT_ps = signal("xn_ready", NT), signal("xnT_ready", NT), signal("xnT_in_psum", NT)
    L.norm = norm
    q_ps, q_ready = signal("q_in_psum", NT), signal("q_ready", NT)
    k_ps, k_ready, kexp_ready = signal("k_in_psum", NT), signal("k_ready", NT), signal("kexp_ready", NT)
    v_ps, v_ready, ctx2_ready = signal("v_in_psum", NT), signal("v_ready", NT), signal("ctx2_ready", NT)
    scores_ready, max_chain, sub_ready = signal("scores_ready", NT), signal("max_chain", MC * NT), signal("sub_ready", NT)
    prob_ready, probT_ps, probT_ready = signal("prob_ready", NT), signal("probT_in_psum", 2 * NT), signal("probT_ready", 2 * NT)
    o_ps, rc_chain, on_ready = signal("o_in_psum", NT), signal("rc_chain", RC * NT), signal("on_ready", NT)
    oT_ps, oT_ready, out_ps, tmp_ready = signal("oT_in_psum", NT), signal("oT_ready", NT), signal("out_in_psum", NT), signal("tmp_ready", NT if bias["o"] is not None else 0)
    x_done = signal("x_done", NT)
    out_read = x_done if bias["o"] is None else tmp_ready
    L.done = x_done(NT)
    LO, HI, END = 7, NT - 1, NT + 6

    def tensor(pe):
        if early:
            norm.turn(pe, 2)
        m.begin(pe, start)
        if early:
            norm.turn(pe, 3)
            pe.wait_ge(*norm.xnT_ready(NG))

        def turn_x(t, p):
            pe.wait_ge(*xn_ready(t + 1))
            if past(t, 1):
                pe.wait_ge(*q_ready(t))
            else:
                pe.wait_ge(*k_ready(1))
            pe.transpose(J0[:, 0:P], xn[:, p, :], m.ident[:, :]).then_inc(xnT_ps.sem, 1)

        def scores(t, p):
            pe.wait_ge(*q_ready(t + 1))
            pe.wait_ge(*kexp_ready(t + 1))
            if past(t, 1):
                if masked:
                    pe.wait_ge(*max_chain(MC * t - 1))
                else:
                    pe.wait_ge(*sub_ready(t))
            for half in range(2):
                for b in range(2):
                    rhs = kexp[:, p, b, half * HP:(half + 1) * HP, :].rearrange("p h k -> p (h k)")
                    mm = pe.matmul(pS[b * S:(b + 1) * S, half, :], qT[:, p, b * S:(b + 1) * S], rhs,
                                   start=True, stop=True)
            mm.then_inc(scores_ready.sem, 1)

        def keys(t, p):
            if not early and past(t, 1):
                pe.wait_ge(*xnT_ready(t))
            elif past(t, 2):
                pe.wait_ge(*q_ready(t - 1))
            elif past(t, 1):
                pe.wait_ge(*k_ready(t))
            pe.matmul(J0[:, 0:P], w["k"], columns(m.ctxT, t, P), start=True, stop=True).then_inc(k_ps.sem, 1)

        def values(t, p):
            pe.wait_ge(*ctx2_ready(t + 1))
            if past(t, 1):
                pe.wait_ge(*v_ready(t))
            for b in range(2):
                mm = pe.matmul(J1[:, b * P:(b + 1) * P], ctx2[:, p, b].rearrange("p u s -> p (u s)"), w["v"],
                               start=True, stop=True)
            mm.then_inc(v_ps.sem, 1)

        def turn_probs(t, p):
            pe.wait_ge(*prob_ready(t + 1))
            if past(t, 1):
                pe.wait_ge(*probT_ready(2 * t))
            for c in range(HP):
                tr = pe.transpose(pP[:, c // 4, c % 4 * P:c % 4 * P + P],
                                  prob[:, p, 2 * c:2 * c + 2, :].rearrange("p h k -> p (h k)"), m.ident[:, :])
                if c % 4 == 3:
                    tr.then_inc(probT_ps.sem, 1)

        def turn_out(t, p):
            pe.wait_ge(*on_ready(t + 1))
            if past(t, 1):
                pe.wait_ge(*out_read(t))
            pe.transpose(J2[:, 0:P], on[:, p, :], m.ident[:, :]).then_inc(oT_ps.sem, 1)

        def queries(t, p, last=False):
            if not early:
                pe.wait_ge(*xnT_ready(t + 1))
            if not last:
                pe.wait_ge(*k_ready(t + 2))
            x = columns(m.XNT, t, P) if early else xnT[:, p, :]
            pe.matmul(J0[:, 0:P], w["q"], x, start=True, stop=True).then_inc(q_ps.sem, 1)

        def weigh_values(t, p):
            pe.wait_ge(*probT_ready(2 * t + 2))
            pe.wait_ge(*v_ready(t + 1))
            if past(t, 1):
                pe.wait_ge(*on_ready(t))
            for c in range(HP):
                for b in range(2):
                    mm = pe.matmul(pO[b * S:(b + 1) * S, c * 18:c * 18 + 18], probT[:, p, c, b * S:(b + 1) * S],
                                   vbd[:, p, b, 2 * c:2 * c + 2, :].rearrange("p h d -> p (h d)"),
                                   start=True, stop=True)
            mm.then_inc(o_ps.sem, 1)

        def project(t, p):
            pe.wait_ge(*oT_ready(t + 1))
            pe.matmul(J2[:, P:2 * P], oT[:, p, :], w["o"], start=True, stop=True).then_inc(out_ps.sem, 1)

        def step(n, p):
            q = 1 - p
            if not early and live(n - 1):
                turn_x(n - 1, q)
            if live(n - 2):
                scores(n - 2, p)
            if live(n):
                keys(n, p)
            if live(n - 3):
                turn_probs(n - 3, q)
            if live(n - 2):
                values(n - 2, p)
            if live(n - 4):
                turn_out(n - 4, p)
            if live(n - 1):
                queries(n - 1, q, not live(n))
            if live(n - 3):
                weigh_values(n - 3, q)
            if live(n - 4):
                project(n - 4, p)

        pipeline(pe, step, LO, HI, END)

    def scalar(act):
        if early:
            for g in range(NG):
                norm.evacuate(act, g)
        m.begin(act, start)

        def evac(dst, src, ready, n, done, bias=None):
            act.wait_ge(*ready(n))
            if bias is None:
                act.activation(dst, src, ACT.Copy).then_inc(done.sem, 1)
            else:
                act.activation(dst, src, ACT.Identity, bias=bias).then_inc(done.sem, 1)

        def context(t, p):
            if past(t, 2):
                act.wait_ge(*v_ps(t - 1))
            apart(act, m)
            act.activation(ctx2[:, p, :, :, :],
                           columns(m.ctxT, t, P).rearrange("p (b o s) -> p b o s", b=2, o=1).broadcast_to([P, 2, 2, S]),
                           ACT.Copy).then_inc(ctx2_ready.sem, 1)

        def step(n, p):
            q = 1 - p
            if not early and live(n - 1):
                t = n - 1
                if past(t, 2):
                    act.wait_ge(*q_ps(t - 1))
                evac(xnT[:, q, :], J0[:, 0:P], xnT_ps, t + 1, xnT_ready)
            if live(n):
                t = n
                if past(t, 2):
                    act.wait_ge(*kexp_ready(t - 1))
                evac(kT[:, p, :], J0[:, 0:P], k_ps, t + 1, k_ready, bias["k"])
            if live(n - 3):
                t = n - 3
                if past(t, 2):
                    act.wait_ge(*o_ps(t - 1))
                for half in range(2):
                    evac(probT[:, q, 4 * half:4 * half + 4, :].rearrange("p c q -> p (c q)"), pP[:, half, :],
                         probT_ps, 2 * t + half + 1, probT_ready)
            if live(n - 4):
                t = n - 4
                if past(t, 2):
                    act.wait_ge(*out_ps(t - 1))
                evac(oT[:, p, :], J2[:, 0:P], oT_ps, t + 1, oT_ready, bias["v"])
            if live(n - 1):
                t = n - 1
                if past(t, 2):
                    act.wait_ge(*scores_ready(t - 1))
                evac(qT[:, q, :], J0[:, 0:P], q_ps, t + 1, q_ready, bias["q"])
            if live(n - 2):
                act.wait_ge(*sub_ready(n - 1))
                pr = prob[:, p].rearrange("p h k -> p (h k)")
                act.activation(pr, pr, ACT.Exp, scale=scale).then_inc(prob_ready.sem, 1)
            if live(n - 1):
                context(n - 1, q)

        pipeline(act, step, LO, HI, END)

    def gpsimd(pool):
        if early:
            for g in range(NG):
                norm.rstd(pool, g)
        m.begin(pool, start)
        pool.memset(vbd[:, :, :, :, :].rearrange("p a b h d -> p (a b h d)"), 0.0).then_inc(vones.sem, 1)
        for u in range(2):
            for a in range(2):
                pool.wait_ge(*vones(1 + 2 * u + a))
                pool.memset(vbd[u * S:(u + 1) * S, a, :, u::2, dh:dh + 1], 1.0).then_inc(vones.sem, 1)
        pool.wait_ge(*vones(5))

        def step(n, p):
            if not early and live(n + 1):
                norm.rstd(pool, n + 1, 1 - p, xn_ready)
            if live(n):
                t = n
                pool.wait_ge(*k_ready(t + 1))
                if past(t, 2):
                    pool.wait_ge(*scores_ready(t - 1))
                for b in range(2):
                    kk = kT[:, p, b * S:(b + 1) * S].rearrange("p (o k) -> p o k", o=1)
                    ke = pool.tensor_tensor(kexp[:, p, b], kk.broadcast_to([P, H, S]),
                                            m.hmask[:, :].rearrange("p (h o) -> p h o", o=1).broadcast_to([P, H, S]),
                                            ALU.mult)
                ke.then_inc(kexp_ready.sem, 1)

        if not early:
            norm.rstd(pool, 0, 0, xn_ready)
        pipeline(pool, step, LO, HI, END)

    def vector(dve):
        if early:
            norm.apply(dve, NG - 1)
        m.begin(dve, start)
        dve.wait_ge(*vones(5))

        def step(n, p):
            q = 1 - p
            if live(n - 5):
                t = n - 5
                dve.wait_ge(*out_ps(t + 1))
                xt = tile_of(m.X, t)
                if bias["o"] is None:
                    dve.tensor_tensor(xt, xt, J2[:, P:2 * P], ALU.add).then_inc(x_done.sem, 1)
                else:
                    dve.tensor_tensor(tmp[:, q, :], J2[:, P:2 * P], bias["o"], ALU.add).then_inc(tmp_ready.sem, 1)
                    dve.wait_ge(*tmp_ready(t + 1))
                    dve.tensor_tensor(xt, xt, tmp[:, q, :], ALU.add).then_inc(x_done.sem, 1)
            if live(n - 6) and tag in m.stats_after:
                dve.wait_ge(*x_done(n - 5))
                m.stats_after[tag].tile_stats(dve, n - 6)
            if live(n - 4):
                t = n - 4
                dve.wait_ge(*o_ps(t + 1))
                ov = pO[:, 0:H * (dh + 1)].rearrange("p (h e) -> p h e", e=dh + 1)
                dve.reciprocal(rc[:, p, :], ov[:, :, dh]).then_inc(rc_chain.sem, 1)
                dve.wait_ge(*rc_chain(RC * t + 1))
                if masked:
                    dve.tensor_scalar(rc[:, p, :], rc[:, p, :], m.rowvalid[:, bass.ds(t, 1)], None,
                                      ALU.mult).then_inc(rc_chain.sem, 1)
                    dve.wait_ge(*rc_chain(RC * t + 2))
                if past(t, 2):
                    dve.wait_ge(*oT_ps(t - 1))
                dve.tensor_tensor(on[:, p, :].rearrange("p (h d) -> p h d", d=dh), ov[:, :, 0:dh],
                                  rc[:, p, :].rearrange("p (h o) -> p h o", o=1).broadcast_to([P, H, dh]),
                                  ALU.mult).then_inc(on_ready.sem, 1)
            if live(n - 2):
                t = n - 2
                dve.wait_ge(*scores_ready(t + 1))
                if past(t, 2):
                    dve.wait_ge(*probT_ps(2 * t - 2))
                mxb = mx[:, p, :].rearrange("p (h o) -> p h o", o=1).broadcast_to([P, H, S])
                src, c = sv, 0
                if masked:
                    mb = m.maskbias[:, bass.ds(t, 1), :].broadcast_to([P, H, S])
                    dve.tensor_tensor(prob[:, p], sv, mb, ALU.add).then_inc(max_chain.sem, 1)
                    dve.wait_ge(*max_chain(MC * t + 1))
                    src, c = prob[:, p], 1
                dve.tensor_reduce(mx[:, p, :], src, AX, ALU.max).then_inc(max_chain.sem, 1)
                dve.wait_ge(*max_chain(MC * t + c + 1))
                dve.tensor_tensor(prob[:, p], src, mxb, ALU.subtract).then_inc(sub_ready.sem, 1)
            if not early and live(n):
                if past(n, 2):
                    dve.wait_ge(*xnT_ps(n - 1))
                norm.apply(dve, xn[:, p, :], tile_of(m.X, n), n, p).then_inc(xn_ready.sem, 1)
            if not early and live(n + 1):
                norm.stats(dve, tile_of(m.X, n + 1), n + 1, q)
            if live(n - 2):
                t = n - 2
                dve.wait_ge(*v_ps(t + 1))
                if past(t, 2):
                    dve.wait_ge(*o_ps(t - 1))
                for b in range(2):
                    vv = dve.tensor_tensor(vbd[:, p, b, :, 0:dh],
                                           J1[:, b * P:(b + 1) * P].rearrange("p (h d) -> p h d", d=dh),
                                           m.vmask[:, :, 0:dh], ALU.mult)
                vv.then_inc(v_ready.sem, 1)

        if not early:
            norm.stats(dve, tile_of(m.X, 0), 0, 0)
        pipeline(dve, step, LO, HI, END)

    L.tensor, L.scalar, L.gpsimd, L.vector = tensor, scalar, gpsimd, vector
    return L


def wide_head_attention(sh, m, tag, start, w):
    nc = sh.nc
    dh = 64
    scale = float(dh) ** -0.5
    L = Layer()
    with ExitStack() as scope:
        def sb(name, shape, dt=F32):
            return scope.enter_context(nc.sbuf_tensor(f"{tag}_{name}", shape, dt))

        outer = Norm(sh, sb, f"{tag}_outer", m)
        inner = Norm(sh, sb, f"{tag}_inner", m, "inner_norm")
        x1 = sb("x1", [P, 2, P])
        xn = sb("xn", [P, 2, P])
        xnT = sb("xnT", [P, 2, P])
        qT = sb("qT", [P, 2, HP, P])
        ctx1 = sb("ctx1", [P, 2, P])
        prob = sb("prob", [P, 2, H, S])
        probT = sb("probT", [P, 2, HP, P])
        mx = sb("mx", [P, 2, H])
        sm = sb("sm", [P, 2, H])
        rc = sb("rc", [P, 2, H])
        on = sb("on", [P, 2, H * dh])
        oT = sb("oT", [P, 2, HP, P])
        tmp = sb("tmp", [P, 2, P])

    kbd, vbd = m.blocks
    J0, J1 = m.banks[0], m.banks[1]
    pS, pP, pO = m.wide[0], m.wide[1], m.wide[2]
    sv = pS.rearrange("p a (h k) -> p (a h) k", k=S)
    ov = pO.rearrange("p a (h k) -> p (a h) k", k=dh)

    signal = sh.counted_semaphore
    zeros = signal("blocks_zeroed", 2)
    x1_ready, xn_ready, xnT_ready, xnT_ps = signal("x1_ready", NT), signal("xn_ready", NT), signal("xnT_ready", NT), signal("xnT_in_psum", NT)
    q_ps, q_ready = signal("q_in_psum", 2 * NT), signal("q_ready", 2 * NT)
    k_ps, k_ready = signal("k_in_psum", 2 * NT), signal("k_ready", 4 * NT)
    v_ps, v_ready, ctx1_ready = signal("v_in_psum", 2 * NT), signal("v_ready", 4 * NT), signal("ctx1_ready", NT)
    scores_ready, mx_ready, sub_ready = signal("scores_ready", NT), signal("mx_ready", NT), signal("sub_ready", NT)
    prob_ready, probT_ps, probT_ready = signal("prob_ready", NT), signal("probT_in_psum", 2 * NT), signal("probT_ready", 2 * NT)
    o_ps, sm_ready, rc_ready, on_ready = signal("o_in_psum", NT), signal("sm_ready", NT), signal("rc_ready", NT), signal("on_ready", NT)
    oT_ps, oT_ready, out_ps, tmp_ready = signal("oT_in_psum", 2 * NT), signal("oT_ready", 2 * NT), signal("out_in_psum", NT), signal("tmp_ready", NT)
    x_done = signal("x_done", NT)
    L.done = x_done(NT)
    LO, HI, END = 7, NT - 1, NT + 5

    def tensor(pe):
        m.begin(pe, start)

        def keys(t, p):
            for j in range(2):
                if past(t, 1):
                    pe.wait_ge(*q_ready(2 * t - 1 + j))
                for c in range(4):
                    cc = 4 * j + c
                    mm = pe.matmul((J1, J0)[j][:, c * P:(c + 1) * P], w["k"][:, cc * P:(cc + 1) * P],
                                   columns(m.ctxT, t, P), start=True, stop=True)
                mm.then_inc(k_ps.sem, 1)

        def values(t, p):
            pe.wait_ge(*ctx1_ready(t + 1))
            wv = w["v"].rearrange("p (c u d) -> p c u d", u=2, d=dh)
            for b in range(2):
                if before_end(t, 2):
                    pe.wait_ge(*k_ready(4 * t + 2 * b + 10))
                elif before_end(t, 1):
                    pe.wait_ge(*q_ready(2 * t + 3 + b))
                else:
                    pe.wait_ge(*v_ready(4 * t - 2 + 2 * b))
                for u in range(2):
                    mm = pe.matmul((J1, J0)[b][u * S:(u + 1) * S, :], ctx1[:, p, b * S:(b + 1) * S], wv[:, :, u, :],
                                   start=True, stop=True)
                mm.then_inc(v_ps.sem, 1)

        def turn_x(t, p):
            pe.wait_ge(*xn_ready(t + 1))
            if past(t, 2):
                pe.wait_ge(*v_ready(4 * t - 4))
            else:
                pe.wait_ge(*k_ready(4 * t + 4))
            pe.transpose(J0[:, 0:P], xn[:, p, :], m.ident[:, :]).then_inc(xnT_ps.sem, 1)

        def queries(t, p):
            pe.wait_ge(*xnT_ready(t + 1))
            for j in range(2):
                if j == 0:
                    if past(t, 2):
                        pe.wait_ge(*v_ready(4 * t - 6))
                    else:
                        pe.wait_ge(*k_ready(4 * t + 2))
                for c in range(4):
                    cc = 4 * j + c
                    mm = pe.matmul((J1, J0)[j][:, c * P:(c + 1) * P], w["q"][:, cc * P:(cc + 1) * P], xnT[:, p, :],
                                   start=True, stop=True)
                mm.then_inc(q_ps.sem, 1)

        def scores(t, p):
            pe.wait_ge(*q_ready(2 * t + 2))
            pe.wait_ge(*k_ready(4 * t + 4))
            if past(t, 1):
                pe.wait_ge(*sub_ready(t))
            for c in range(HP):
                for b in range(2):
                    mm = pe.matmul(pS[b * S:(b + 1) * S, c // 4, c % 4 * P:c % 4 * P + P],
                                   qT[:, p, c, b * S:(b + 1) * S],
                                   kbd[:, p, b, c].rearrange("p u k -> p (u k)"), start=True, stop=True)
            mm.then_inc(scores_ready.sem, 1)

        def turn_probs(t, p):
            pe.wait_ge(*prob_ready(t + 1))
            if past(t, 2):
                pe.wait_ge(*tmp_ready(t - 1))
            elif past(t, 1):
                pe.wait_ge(*probT_ready(2 * t))
            for c in range(HP):
                tr = pe.transpose(pP[:, c // 4, c % 4 * P:c % 4 * P + P],
                                  prob[:, p, 2 * c:2 * c + 2, :].rearrange("p h k -> p (h k)"), m.ident[:, :])
                if c % 4 == 3:
                    tr.then_inc(probT_ps.sem, 1)

        def weigh_values(t, p):
            pe.wait_ge(*probT_ready(2 * t + 2))
            pe.wait_ge(*v_ready(4 * t + 4))
            if past(t, 1):
                pe.wait_ge(*on_ready(t))
            for c in range(HP):
                for b in range(2):
                    mm = pe.matmul(pO[b * S:(b + 1) * S, c // 4, c % 4 * P:c % 4 * P + P],
                                   probT[:, p, c, b * S:(b + 1) * S],
                                   vbd[:, p, b, c].rearrange("p u d -> p (u d)"), start=True, stop=True)
            mm.then_inc(o_ps.sem, 1)

        def turn_out(t, p):
            pe.wait_ge(*on_ready(t + 1))
            if before_end(t, 1):
                pe.wait_ge(*probT_ready(2 * t + 4))
            else:
                pe.wait_ge(*tmp_ready(t))
            for c in range(HP):
                tr = pe.transpose(pP[:, c // 4, c % 4 * P:c % 4 * P + P], on[:, p, c * P:(c + 1) * P], m.ident[:, :])
                if c % 4 == 3:
                    tr.then_inc(oT_ps.sem, 1)

        def project(t, p):
            pe.wait_ge(*oT_ready(2 * t + 2))
            for c in range(HP):
                mm = pe.matmul(pP[:, 0, 0:P], oT[:, p, c, :], w["o"][:, c, :], start=(c == 0), stop=(c == HP - 1))
            mm.then_inc(out_ps.sem, 1)

        def step(n, p):
            q = 1 - p
            if live(n - 2):
                scores(n - 2, p)
            if live(n - 1):
                turn_x(n - 1, q)
            if live(n - 3):
                turn_probs(n - 3, q)
            if live(n - 1):
                queries(n - 1, q)
            if live(n - 4):
                turn_out(n - 4, p)
            if live(n):
                keys(n, p)
            if live(n - 3):
                weigh_values(n - 3, q)
            if live(n - 4):
                project(n - 4, p)
            if live(n - 2):
                values(n - 2, p)

        pipeline(pe, step, LO, HI, END)

    def scalar(act):
        m.begin(act, start)
        act.wait_ge(*zeros(2))

        def step(n, p):
            q = 1 - p
            if live(n - 1):
                t = n - 1
                act.wait_ge(*xnT_ps(t + 1))
                if past(t, 2):
                    act.wait_ge(*q_ps(2 * t - 2))
                act.activation(xnT[:, q, :], J0[:, 0:P], ACT.Identity, bias=w["beta"],
                               scale=w["gamma"]).then_inc(xnT_ready.sem, 1)
            if live(n - 3):
                t = n - 3
                if past(t, 2):
                    act.wait_ge(*o_ps(t - 1))
                for half in range(2):
                    act.wait_ge(*probT_ps(2 * t + half + 1))
                    act.activation(probT[:, q, 4 * half:4 * half + 4, :].rearrange("p c q -> p (c q)"),
                                   pP[:, half, :], ACT.Copy).then_inc(probT_ready.sem, 1)
            if live(n - 1):
                t = n - 1
                if past(t, 2):
                    act.wait_ge(*scores_ready(t - 1))
                for j in range(2):
                    act.wait_ge(*q_ps(2 * t + j + 1))
                    act.activation(qT[:, q, 4 * j:4 * j + 4, :].rearrange("p c q -> p (c q)"), (J1, J0)[j],
                                   ACT.Copy).then_inc(q_ready.sem, 1)
            if live(n - 4):
                t = n - 4
                if past(t, 2):
                    act.wait_ge(*out_ps(t - 1))
                for j in range(2):
                    act.wait_ge(*oT_ps(2 * t + j + 1))
                    act.activation(oT[:, p, 4 * j:4 * j + 4, :].rearrange("p c q -> p (c q)"), pP[:, j, :],
                                   ACT.Copy).then_inc(oT_ready.sem, 1)
            if live(n):
                t = n
                if past(t, 2):
                    act.wait_ge(*scores_ready(t - 1))
                for j in range(2):
                    act.wait_ge(*k_ps(2 * t + j + 1))
                    for u in range(2):
                        src = (J1, J0)[j][u * S:(u + 1) * S, :].rearrange("p (c b k) -> p b c k", b=2, k=S)
                        act.activation(kbd[u * S:(u + 1) * S, p, :, 4 * j:4 * j + 4, u, :], src,
                                       ACT.Copy).then_inc(k_ready.sem, 1)
            if live(n - 2):
                act.wait_ge(*sub_ready(n - 1))
                pr = prob[:, p].rearrange("p h k -> p (h k)")
                act.activation(pr, pr, ACT.Exp, scale=scale).then_inc(prob_ready.sem, 1)

        pipeline(act, step, LO, HI, END)

    def gpsimd(pool):
        for x in (kbd, vbd):
            pool.memset(x[:, :, :, :, :, :].rearrange("p a b c u k -> p (a b c u k)"), 0.0).then_inc(zeros.sem, 1)
        m.begin(pool, start)

        def context(t, p):
            if past(t, 2):
                pool.wait_ge(*v_ps(2 * t - 2))
            pool.tensor_copy(ctx1[:, p, :], columns(m.ctxT, t, P)).then_inc(ctx1_ready.sem, 1)

        def step(n, p):
            if live(n):
                inner.rstd(pool, n, p, xn_ready)
            if live(n + 1):
                outer.rstd(pool, n + 1, 1 - p, x1_ready)
            if live(n - 1):
                context(n - 1, 1 - p)

        outer.rstd(pool, 0, 0, x1_ready)
        pipeline(pool, step, LO, HI, END)

    def vector(dve):
        m.begin(dve, start)
        dve.wait_ge(*zeros(2))

        def step(n, p):
            q = 1 - p
            if live(n):
                outer.apply(dve, x1[:, p, :], tile_of(m.X, n), n, p).then_inc(x1_ready.sem, 1)
                dve.wait_ge(*x1_ready(n + 1))
                inner.stats(dve, x1[:, p, :], n, p)
            if live(n - 2):
                t = n - 2
                dve.wait_ge(*scores_ready(t + 1))
                if past(t, 2):
                    dve.wait_ge(*probT_ps(2 * t - 2))
                dve.tensor_reduce(mx[:, p, :], sv, AX, ALU.max).then_inc(mx_ready.sem, 1)
                dve.wait_ge(*mx_ready(t + 1))
                dve.tensor_tensor(prob[:, p], sv,
                                  mx[:, p, :].rearrange("p (h o) -> p h o", o=1).broadcast_to([P, H, S]),
                                  ALU.subtract).then_inc(sub_ready.sem, 1)
            if live(n):
                if past(n, 2):
                    dve.wait_ge(*xnT_ps(n - 1))
                inner.apply(dve, xn[:, p, :], x1[:, p, :], n, p).then_inc(xn_ready.sem, 1)
            if live(n + 1):
                outer.stats(dve, tile_of(m.X, n + 1), n + 1, q)
            if live(n - 3):
                t = n - 3
                dve.wait_ge(*prob_ready(t + 1))
                dve.tensor_reduce(sm[:, q, :], prob[:, q], AX, ALU.add).then_inc(sm_ready.sem, 1)
                dve.wait_ge(*sm_ready(t + 1))
                dve.reciprocal(rc[:, q, :], sm[:, q, :]).then_inc(rc_ready.sem, 1)
                dve.wait_ge(*rc_ready(t + 1))
                dve.wait_ge(*o_ps(t + 1))
                if past(t, 2):
                    dve.wait_ge(*oT_ps(2 * t - 2))
                dve.tensor_tensor(on[:, q, :].rearrange("p (h d) -> p h d", d=dh), ov,
                                  rc[:, q, :].rearrange("p (h o) -> p h o", o=1).broadcast_to([P, H, dh]),
                                  ALU.mult).then_inc(on_ready.sem, 1)
            if live(n - 4):
                t = n - 4
                dve.wait_ge(*out_ps(t + 1))
                xt = tile_of(m.X, t)
                dve.tensor_tensor(tmp[:, p, :], pP[:, 0, 0:P], w["bo"], ALU.add).then_inc(tmp_ready.sem, 1)
                dve.wait_ge(*tmp_ready(t + 1))
                dve.scalar_tensor_tensor(out=xt, in0=tmp[:, p, :], scalar=w["gate"], in1=xt, op0=ALU.mult,
                                         op1=ALU.add).then_inc(x_done.sem, 1)
            if live(n - 5) and tag in m.stats_after:
                dve.wait_ge(*x_done(n - 4))
                m.stats_after[tag].tile_stats(dve, n - 5)
            if live(n - 2):
                t = n - 2
                if past(t, 2):
                    dve.wait_ge(*o_ps(t - 1))
                for b in range(2):
                    dve.wait_ge(*v_ps(2 * t + b + 1))
                    for u in range(2):
                        src = (J1, J0)[b][u * S:(u + 1) * S, :].rearrange("p (c d) -> p c d", d=dh)
                        dve.tensor_copy(vbd[u * S:(u + 1) * S, p, b, :, u, :], src).then_inc(v_ready.sem, 1)

        outer.stats(dve, tile_of(m.X, 0), 0, 0)
        pipeline(dve, step, LO, HI, END)

    L.tensor, L.scalar, L.gpsimd, L.vector = tensor, scalar, gpsimd, vector
    return L


def experts(sh, m, tag, start, spec):
    nc = sh.nc
    E, C, gated, router, ER = spec["E"], spec["C"], spec.get("gated"), spec.get("router"), spec.get("ER", 0)
    L = Layer()
    if gated:
        raw, = m.weight_buffers[tag]
    else:
        w1, w2 = m.weight_buffers[tag]
    with ExitStack() as scope:
        def sb(name, shape, dt=F32):
            return scope.enter_context(nc.sbuf_tensor(f"{tag}_{name}", shape, dt))

        XH, XL = (sb(name, [P, TOK], F32R) for name in ("XH", "XL"))
        WH, WL = (sb(name, [P, 2, 6 * P], F32R) for name in ("WH", "WL"))
        if gated:
            w1, w2 = sb("w1", [P, 2, 2 * C * P]), sb("w2", [P, 2, C, D])
        h = sb("h", [P, 2, C, GW])
        if gated:
            sg = sb("sg", [P, 2, GW])
        if router:
            LG = sb("logits", [P, NT, ER])
            gates = sb("gates", [P, NT, E])
            A, Bt, Ct, O1, O2 = (sb(f"work{i}", [P, NT, ER]) for i in range(5))
            m1, m2, rm, ws, wa, wb = (sb(f"row{i}", [P, NT]) for i in range(6))
        if router and spec.get("b2"):
            R = P // E
            gT = sb("gT", [P, E * NT // P, P])
            b2sel = sb("b2sel", [P, R, D])

    J0, J1 = m.banks[0], m.banks[1]
    norm = NormAll(sh, m, (XH, XL))
    xn, XNT, xn_ready, xnT_ready = m.xn, m.XNT, norm.xn_ready, norm.xnT_ready
    early, after = spec.get("early"), spec.get("then_norm")
    ring = m.banks[2:6]
    pair = [m.banks[2:4], m.banks[4:6], [J0, J1]]
    Y = [m.banks[6], m.banks[7]]

    signal = sh.counted_semaphore
    b2 = bool(router and spec.get("b2"))
    EXPS = (2 if spec["whole"] else 1) if router else 0
    LINKS = (17 if E > ER else 16) if router else 0
    ND = 5 if gated else 2
    units = NG * E
    lg_ps, lg_ready = signal("logits_in_psum", NG if router else 0), signal("logits_ready", 1 if router else 0)
    x_plus = signal("x_plus_norm", 1 if spec.get("residual") else 0)
    g_chain, exp_in, exp_out, gates_ready = signal("gates_chain", LINKS), signal("exp_in", EXPS), signal("exp_out", EXPS), signal("gates_ready", 1 if router else 0)
    gT_ps, gT_ready, b2_ps, b2_added, sel_ready = (signal("gT_in_psum", 1 if b2 else 0), signal("gT_ready", 1 if b2 else 0), signal("b2_in_psum", NG if b2 else 0),
                                                   signal("b2_added", NG if b2 else 0 if router else 1), signal("b2sel_ready", R if b2 else 0))
    w_loaded = [signal("w_loaded_even", ND * 16 * ((E + 1) // 2)), signal("w_loaded_odd", ND * 16 * (E // 2))]
    w_turned_ps, w_turned, zeroed = signal("w_turned_ps", 3 * E if gated else 0), signal("w_turned", 3 * E if gated else 0), signal("raw_zeroed", 1 if gated else 0)
    a_ps, s_ready, h_ready, y_ps, combined = (signal("hidden_in_psum", units * C), signal("silu_ready", units * C if gated else 0), signal("h_ready", units * C),
                                              signal("y_in_psum", units), signal("combined", units))
    L.done = combined(units)
    L.norm = norm
    hi_ready, w_split = signal("w_high_ready", E), signal("w_split", E)
    split_free, m.split_free = m.split_free, [a_ps(units * C)]
    weights_here, m.weights_here = m.weights_here, [s(ND * 16 * n) for s, n in zip(w_loaded, ((E + 1) // 2, E // 2)) if n]

    def over_experts(eng, one, middle, late=lambda: None):
        if E == 1:
            one(0, 0)
            return
        one(0, 0)
        one(1, 1)
        with eng.Fori(2, E - 3, 2) as e:
            one(e, 0)
            one(e + 1, 1)
        middle()
        one(E - 2, 0)
        late()
        one(E - 1, 1)

    def order(e, p, first, second, between=None):
        first(0)
        if has(e, 1):
            second(e - 1, 1 - p, NG - 1)
        for g in range(1, NG):
            first(g)
            second(e, p, g - 1)
            if between:
                between(g - 1)
        if not has_next(e):
            second(e, p, NG - 1)
            if between:
                between(NG - 1)

    four = router and not gated

    def y_bank(e, g):
        return (Y + [J0, J1])[g] if four and not has(e, 1) else Y[g % 2]

    def y_free(e, g):
        if four and not has(e, 1):
            return 0
        if four and not has(e, 2) and g < 2:
            return g + 1
        return NG * e + g - 1 if has(e, 1) or g >= 2 else 0

    def has(e, k):
        return not isinstance(e, int) or e >= k

    def has_next(e):
        return not isinstance(e, int) or e < E - 1

    def loads(e, p):
        return ND * 8 * (e - p) + ND * 16

    def sync(sp):
        for s, v in weights_here:
            sp.wait_ge(s, v)
        if gated:
            sp.wait_ge(*zeroed(1))

        def one(e, p):
            if has(e, 2):
                if gated:
                    sp.wait_ge(*w_turned_ps(3 * e - 3))
                else:
                    sp.wait_ge(*y_ps(NG * e - NG))
            if gated:
                for k in range(2):
                    src = spec["weights"][k][bass.ds(e, 1)].rearrange("o i h -> (o i) h")
                    sp.dma_start(raw[:, p, k, 0:2 * P].rearrange("p (c h) -> p c h", h=P),
                                 src[0:2 * P, :].rearrange("(c p) h -> p c h", p=P)).then_inc(w_loaded[p].sem, 16)
                    sp.dma_start(raw[0:96, p, k, 2 * P:3 * P], src[2 * P:352, :]).then_inc(w_loaded[p].sem, 16)
                sp.dma_start(raw[:, p, 2, 0:352], spec["weights"][2][bass.ds(e, 1)].rearrange("o h i -> (o h) i")
                             ).then_inc(w_loaded[p].sem, 16)
            else:
                s1, s2, ee = spec["weights"](e)
                sp.dma_start(w1[:, p, :], s1[bass.ds(ee, 1)].rearrange("o d f -> (o d) f")).then_inc(w_loaded[p].sem, 16)
                sp.dma_start(w2[:, p, :, :], s2[bass.ds(ee, 1)].rearrange("o (c p) d -> p (o c) d", p=P)
                             ).then_inc(w_loaded[p].sem, 16)

        over_experts(sp, one, lambda: None)

    def route(pe, g):
        of = m.ctxT if router == "ctx" else XNT
        if router == "x":
            pe.wait_ge(*xnT_ready(g + 1))
        for t in range(g * GT, (g + 1) * GT):
            mm = pe.matmul(J1[:, t * ER:(t + 1) * ER], of[:, t * P:(t + 1) * P], spec["wr"], start=True, stop=True)
        mm.then_inc(lg_ps.sem, 1)

    norm.route = route if early and router == "ctx" else None

    def tensor(pe):
        if norm.route:
            route(pe, 3)
        if early:
            norm.turn(pe, 2)
        m.begin(pe, start)
        if router == "ctx" and not norm.route:
            for g in range(NG):
                route(pe, g)
        for g in range(3 if early else 0, NG):
            norm.turn(pe, g)
            if router == "x" and g:
                for k in range(0 if g == 3 and early else g - 1, g):
                    route(pe, k)
        if router == "x":
            route(pe, NG - 1)

        def turn_weights(e, p):
            pe.wait_ge(*w_loaded[p](loads(e, p)))
            for k in range(3):
                if has(e, 1) or k == 2:
                    pe.wait_ge(*w_turned(3 * e + k - (1 if k == 2 else 2) if k != 2 else 3 * e + 1))
                elif k == 0:
                    pe.wait_ge(*xnT_ready(NG))
                else:
                    pe.wait_ge(*lg_ready(1))
                for c in range(C):
                    tr = pe.transpose((J0, J1, J0)[k][:, c * P:(c + 1) * P], raw[:, p, k, c * P:(c + 1) * P],
                                      m.ident[:, :])
                tr.then_inc(w_turned_ps.sem, 1)

        if gated:
            turn_weights(0, 0)

        def one(e, p):
            if gated:
                pe.wait_ge(*w_turned(3 * e + 3))
            else:
                pe.wait_ge(*w_loaded[p](loads(e, p)))
            pe.wait_ge(*w_split(e + 1))

            def product(out, k, cols):
                ws = slice(k * P, (k + 1) * P)
                pe.matmul(out, WH[:, p, ws], XH[:, cols], start=True, stop=False)
                pe.matmul(out, WH[:, p, ws], XL[:, cols], start=False, stop=False)
                return pe.matmul(out, WL[:, p, ws], XH[:, cols], start=False, stop=True)

            def first(g):
                cols = slice(g * GW, (g + 1) * GW)
                if not has(e, 1):
                    pe.wait_ge(*norm.split_ready(g + 1))
                for c in range(C):
                    k = C * NG * e + C * g + c
                    if gated:
                        if has(e, 1) or g >= 1:
                            pe.wait_ge(*h_ready(k - C + 1))
                        if c == 2 and g == 2 and has_next(e):
                            pe.wait_ge(*w_turned(3 * e + 6))
                        product(pair[c][0], c, cols)
                        product(pair[c][1], C + c, cols).then_inc(a_ps.sem, 1)
                    else:
                        if has(e, 1) or C * g + c >= 4:
                            pe.wait_ge(*h_ready(k - 3))
                        product(ring[(C * g + c) % 4], c, cols).then_inc(a_ps.sem, 1)
            def second(e, p, g):
                u = NG * e + g
                for c in range(C):
                    pe.wait_ge(*h_ready(C * u + c + 1))
                    if c == 0 and (has(e, 1) or y_free(e, g)):
                        pe.wait_ge(*combined(y_free(e, g)))
                    elif c == 0 and four and g == 3:
                        pe.wait_ge(*lg_ready(1))
                    for i in range(GT):
                        mm = pe.matmul(y_bank(e, g)[:, i * P:(i + 1) * P], h[:, g % 2, c, i * P:(i + 1) * P],
                                       w2[:, p, c, :], start=(c == 0 and i == 0), stop=(c == C - 1),
                                       skip_group_check=True)
                mm.then_inc(y_ps.sem, 1)

            def between(g):
                if gated and g == 0 and has_next(e):
                    pe.wait_ge(*h_ready(C * NG * e + 2 * C))
                    turn_weights(e + 1, 1 - p)
                if after and not has_next(e) and g >= 2:
                    if g == 2:
                        pe.wait_ge(*h_ready(C * NG * E))
                    follower = m.norm_after[tag]
                    if follower.route:
                        pe.wait_ge(*b2_added(NG))
                        for k in ((0, 1), (2,))[g - 2]:
                            follower.route(pe, k)
                    follower.turn(pe, g - 2)

            order(e, p, first, second, between)

        def middle():
            if not (router and spec.get("b2")):
                return
            pe.wait_ge(*gates_ready(1))
            pe.wait_ge(*sel_ready(R))
            gv = gates[:, :, :].rearrange("p t e -> p (t e)")
            for j in range(E * NT // P):
                tr = pe.transpose(J0[:, j * P:(j + 1) * P], gv[:, j * P:(j + 1) * P], m.ident[:, :])
            tr.then_inc(gT_ps.sem, 1)
            pe.wait_ge(*gT_ready(1))
            for g in range(NG):
                if g >= 1:
                    pe.wait_ge(*b2_added(g))
                lo = g * GT % R
                pe.matmul(J1[:, :], gT[:, g * GT // R, :], b2sel[:, lo:lo + GT, :].rearrange("p t d -> p (t d)"),
                          start=True, stop=True).then_inc(b2_ps.sem, 1)

        def late():
            if spec.get("late"):
                pe.wait_ge(*b2_added(NG))
                spec["late"].tensor(pe)

        over_experts(pe, one, middle, late)

    def scalar(act):
        for g in range(NG):
            norm.evacuate(act, g)
        m.begin(act, start)

        def gate_exps():
            act.wait_ge(*exp_in(1))
            act.activation(wb[:, :], wb[:, :], ACT.Exp).then_inc(exp_out.sem, 1)
            if spec["whole"]:
                act.wait_ge(*exp_in(2))
                act.activation(A[:, :, :], A[:, :, :], ACT.Exp).then_inc(exp_out.sem, 1)

        def turned(e, p):
            for k in range(3):
                act.wait_ge(*w_turned_ps(3 * e + k + 1))
                if has(e, 2) and k == 0:
                    act.wait_ge(*y_ps(NG * e - NG))
                dst = w2[:, p].rearrange("p c d -> p (c d)") if k == 2 else w1[:, p, k * C * P:(k + 1) * C * P]
                act.activation(dst, (J0, J1, J0)[k][:, 0:C * P], ACT.Copy).then_inc(w_turned.sem, 1)

        if gated:
            turned(0, 0)

        def one(e, p):
            if not gated:
                act.wait_ge(*w_loaded[p](loads(e, p)))

            def first(g):
                u = NG * e + g
                for c in range(C):
                    k = C * u + c
                    act.wait_ge(*a_ps(k + 1))
                    if gated:
                        if has(e, 1) or C * g + c >= 2:
                            act.wait_ge(*h_ready(k - 1))
                        b = (C * g + c) % 2
                        act.activation(sg[:, b, :], pair[c][0], ACT.Silu).then_inc(s_ready.sem, 1)
                    else:
                        if c == 0 and (has(e, 1) or g >= 2):
                            act.wait_ge(*y_ps(u - 1))
                        apart(act, m)
                        act.activation(h[:, g % 2, c, :], ring[(C * g + c) % 4], spec["func"],
                                       bias=spec["b1"][:, bass.ds(e * C + c, 1)]).then_inc(h_ready.sem, 1)
                if gated and g == 1 and has_next(e):
                    turned(e + 1, 1 - p)
                if router and not has(e, 1) and g == 1:
                    gate_exps()

            order(e, p, first, lambda e, p, g: None)

        def middle():
            if router and spec.get("b2"):
                act.wait_ge(*gT_ps(1))
                act.activation(gT[:, :, :].rearrange("p j q -> p (j q)"), J0[:, 0:E * NT // P * P],
                               ACT.Copy).then_inc(gT_ready.sem, 1)

        over_experts(act, one, middle, lambda: spec["late"].scalar(act) if spec.get("late") else None)

    def split(eng, e, p):
        if gated:
            eng.wait_ge(*w_turned(3 * e + 2))
        else:
            eng.wait_ge(*w_loaded[p](loads(e, p)))
        if has(e, 2):
            eng.wait_ge(*a_ps(C * NG * (e - 1)))
        n = (2 if gated else 1) * C * P
        hi, lo = WH[:, p, 0:n], WL[:, p, 0:n]
        apart(eng, m)
        eng.tensor_copy(hi, w1[:, p, 0:n]).then_inc(hi_ready.sem, 1)
        eng.wait_ge(*hi_ready(e + 1))
        eng.tensor_tensor(lo, w1[:, p, 0:n], hi, ALU.subtract).then_inc(w_split.sem, 1)

    def gpsimd(pool):
        if gated:
            pool.memset(raw[:, :, :, :].rearrange("p a k f -> p (a k f)"), 0.0).then_inc(zeroed.sem, 1)

        for g in range(3):
            norm.rstd(pool, g)
        if not early:
            m.begin(pool, start)
        for s, v in split_free:
            pool.wait_ge(s, v)
        if not gated:
            split(pool, 0, 0)
        norm.low_part(pool, 0)
        norm.rstd(pool, 3)
        for g in range(1, NG):
            norm.low_part(pool, g)
        m.begin(pool, start)
        if E > 1:
            split(pool, 1, 1)
        if spec.get("residual"):
            pool.wait_ge(*xn_ready(NG))
            pool.tensor_tensor(m.X[:, :, :], m.X[:, :, :], xn[:, :, :], ALU.add).then_inc(x_plus.sem, 1)
        if not router:
            pool.wait_ge(*xn_ready(NG))
            pool.tensor_tensor(m.X[:, :, :], m.X[:, :, :],
                               spec["bo"].rearrange("p (o d) -> p o d", o=1).broadcast_to([P, NT, D]),
                               ALU.add).then_inc(b2_added.sem, 1)
        if router and spec.get("b2"):
            for t in range(R):
                pool.tensor_scalar(b2sel[:, t, :], spec["b2rep"][:, :], spec["tmask"][:, t:t + 1], None,
                                   ALU.mult).then_inc(sel_ready.sem, 1)
        if E > 1:
            with pool.Fori(2, E - 1, 2) as e:
                split(pool, e, 0)
                split(pool, e + 1, 1)

    def vector(dve):
        m.begin(dve, start)

        for g in range(0 if not early else NG, NG):
            norm.stats(dve, g, spec.get("seen"))
            if g:
                norm.apply(dve, g - 1)
        norm.apply(dve, NG - 1)
        links = [0]

        def link(ins):
            ins.then_inc(g_chain.sem, 1)
            links[0] += 1
            dve.wait_ge(*g_chain(links[0]))

        def wide(r):
            return r[:, :].rearrange("p (t o) -> p t o", o=1).broadcast_to([P, NT, ER])

        def take_best(logits, best, onehot):
            link(dve.tensor_reduce(best[:, :], logits[:, :, :], AX, ALU.max))
            link(dve.tensor_tensor(Bt[:, :, :], logits[:, :, :], wide(best), ALU.is_ge))
            rev = m.rev[:, 16 - ER:16].rearrange("p (o e) -> p o e", o=1).broadcast_to([P, NT, ER])
            link(dve.tensor_tensor(Bt[:, :, :], Bt[:, :, :], rev, ALU.mult))
            link(dve.tensor_reduce(rm[:, :], Bt[:, :, :], AX, ALU.max))
            link(dve.tensor_tensor(onehot[:, :, :], Bt[:, :, :], wide(rm), ALU.is_equal))

        dve.wait_ge(*xn_ready(NG))
        if router:
            dve.wait_ge(*lg_ps(NG))
            lg = J1[:, 0:NT * ER].rearrange("p (t e) -> p t e", e=ER)
            if spec.get("br") is None:
                dve.tensor_copy(LG[:, :, :], lg).then_inc(lg_ready.sem, 1)
            else:
                dve.tensor_tensor(LG[:, :, :], lg, spec["br"].rearrange("p (o e) -> p o e", o=1).broadcast_to([P, NT, ER]),
                                  ALU.add).then_inc(lg_ready.sem, 1)
            dve.wait_ge(*lg_ready(1))
        if gated:
            split(dve, 0, 0)

        def find_gates():
            take_best(LG, m1, O1)
            link(dve.scalar_tensor_tensor(out=Ct[:, :, :].rearrange("p t e -> p (t e)"),
                                          in0=O1[:, :, :].rearrange("p t e -> p (t e)"), scalar=NEG,
                                          in1=LG[:, :, :].rearrange("p t e -> p (t e)"), op0=ALU.mult, op1=ALU.add))
            take_best(Ct, m2, O2)
            dve.tensor_tensor(wb[:, :], m2[:, :], m1[:, :], ALU.subtract).then_inc(exp_in.sem, 1)
            if spec["whole"]:
                dve.tensor_tensor(A[:, :, :], LG[:, :, :], wide(m1), ALU.subtract).then_inc(exp_in.sem, 1)
                dve.wait_ge(*exp_out(2))
                link(dve.tensor_reduce(ws[:, :], A[:, :, :], AX, ALU.add))
            else:
                dve.wait_ge(*exp_out(1))
                link(dve.tensor_scalar(ws[:, :], wb[:, :], 1.0, None, ALU.add))
            link(dve.reciprocal(wa[:, :], ws[:, :]))
            link(dve.tensor_tensor(wb[:, :], wb[:, :], wa[:, :], ALU.mult))
            link(dve.tensor_tensor(O1[:, :, :], O1[:, :, :], wide(wa), ALU.mult))
            link(dve.tensor_tensor(O2[:, :, :], O2[:, :, :], wide(wb), ALU.mult))
            if E > ER:
                link(dve.memset(gates[:, :, ER:E], 1.0))
            dve.tensor_tensor(gates[:, :, 0:ER], O1[:, :, :], O2[:, :, :], ALU.add).then_inc(gates_ready.sem, 1)
            dve.wait_ge(*gates_ready(1))
            assert links[0] == LINKS
            if spec.get("residual"):
                dve.wait_ge(*x_plus(1))

        if not router:
            dve.wait_ge(*b2_added(1))
        elif not gated:
            find_gates()

        def one(e, p):
            def first(g):
                if not gated:
                    return
                u = NG * e + g
                for c in range(C):
                    dve.wait_ge(*s_ready(C * u + c + 1))
                    if c == 0 and (has(e, 1) or g >= 2):
                        dve.wait_ge(*y_ps(u - 1))
                    b = (C * g + c) % 2
                    dve.tensor_tensor(h[:, g % 2, c, :], sg[:, b, :], pair[c][1], ALU.mult).then_inc(h_ready.sem, 1)
                if not has(e, 1) and g == 1:
                    find_gates()

            def second(e, p, g):
                u = NG * e + g
                dve.wait_ge(*y_ps(u + 1))
                if has(e, 1):
                    dve.wait_ge(*combined(u - NG + 1))
                if not router:
                    xg = m.X[:, g * GT:(g + 1) * GT, :].rearrange("p t d -> p (t d)")
                    dve.tensor_tensor(xg, xg, y_bank(e, g), ALU.add).then_inc(combined.sem, 1)
                    return
                for i in range(GT):
                    t = g * GT + i
                    st = dve.scalar_tensor_tensor(out=m.X[:, t, :], in0=y_bank(e, g)[:, i * P:(i + 1) * P],
                                                  scalar=gates[:, t, bass.ds(e, 1)], in1=m.X[:, t, :],
                                                  op0=ALU.mult, op1=ALU.add)
                st.then_inc(combined.sem, 1)

            def next_norm(g):
                dve.wait_ge(*combined(NG * e + g + 1))
                m.norm_after[tag].stats(dve, g)
                if g:
                    m.norm_after[tag].apply(dve, g - 1)

            order(e, p, first, second, next_norm if after and isinstance(e, int) and e == E - 1 else None)

        def middle():
            if router and spec.get("b2"):
                dve.wait_ge(*combined(NG * (E - 2) - 1))
                for g in range(NG):
                    dve.wait_ge(*b2_ps(g + 1))
                    xg = m.X[:, g * GT:(g + 1) * GT, :].rearrange("p t d -> p (t d)")
                    dve.tensor_tensor(xg, xg, J1[:, :], ALU.add).then_inc(b2_added.sem, 1)
                dve.wait_ge(*b2_added(NG))
            if spec.get("late"):
                spec["late"].vector(dve)

        over_experts(dve, one, middle)

    L.tensor, L.scalar, L.gpsimd, L.vector, L.sync = tensor, scalar, gpsimd, vector, sync
    return L


def quantised_ffn(sh, m, tag, start, w):
    nc = sh.nc
    C = 3
    K = C * NG
    QMAX = 32767.0
    L = Layer()
    with ExitStack() as scope:
        def sb(name, shape, dt=F32):
            return scope.enter_context(nc.sbuf_tensor(f"{tag}_{name}", shape, dt))

        G, U, SG = sb("gate", [P, K, GW]), sb("up", [P, K, GW]), m.sig
        am = sb("amax", [P, 5, 2 * K])
        a1, b1 = sb("amax_rows", [P, 5]), sb("amax_all", [P, 5])
        scale, inv = sb("scale", [P, 5]), sb("inv", [P, 5])
        us = sb("up_times_gate_scale", [P, 1])

    J0, J1 = m.banks[0], m.banks[1]
    norm = NormAll(sh, m, None)
    xn, XNT, xn_ready, xnT_ready = m.xn, m.XNT, norm.xn_ready, norm.xnT_ready
    signal = sh.counted_semaphore
    xmax = signal("x_max", 1)
    rows_max, turned, one_max, spread_ps = signal("rows_max", 5), signal("rows_turned", 5), signal("one_max", 5), signal("max_spread", 5)
    scale_set, inv_set, us_set = signal("scale_set", 5), signal("inv_set", 5), signal("us_set", 1)
    x_a, x_q = signal("x_scaled", NG), signal("x_quantised", NG)
    gu_ps, gu_here, gu_max = signal("gate_up_in_psum", 2 * K), signal("gate_up_here", 2 * K), signal("gate_up_max", 2 * K)
    g_a, g_q, sig, sig_a, sig_q = (signal("gate_scaled", K), signal("gate_quantised", K), signal("sigmoid", K), signal("sigmoid_scaled", K),
                                   signal("sigmoid_quantised", K))
    gs, gs_max = signal("gated", K), signal("gated_max", K)
    gs_a, u_a, u_q, o_here, o_max = (signal("gated_scaled", K), signal("up_scaled", K), signal("up_quantised", K), signal("o_here", K),
                                     signal("o_max", K))
    o_a, o_q, y_ps, x_done = signal("o_scaled", K), signal("o_quantised", K), signal("y_in_psum", NG), signal("x_done", NG)
    X_, G_, U_, S_, O_ = range(5)
    L.done = x_done(NG)

    def piece(x, k):
        return x[:, bass.ds(k, 1), :].rearrange("p o f -> p (o f)")

    def passes(eng, step, n, lag):
        for i in range(lag):
            step(i)
        with eng.Fori(lag, n) as i:
            step(i)
        for i in range(n, n + lag):
            step(i)

    def on(k):
        return not isinstance(k, int) or 0 <= k < K

    def quantise(dve, x, r, by=None):
        s = scale[:, r:r + 1] if by is None else by
        return dve.tensor_scalar(x, x, ROUND, s, ALU.subtract, ALU.mult)

    def tensor(pe):
        m.begin(pe, start)

        for g in range(NG):
            norm.turn(pe, g)
        pe.wait_ge(*xnT_ready(NG))

        def spread_max(r):
            pe.wait_ge(*rows_max(r + 1))
            pe.transpose(J0[0:1, 0:P], a1[:, r:r + 1], m.ident[:, :]).then_inc(turned.sem, 1)
            pe.wait_ge(*one_max(r + 1))
            pe.matmul(J1[:, 0:1], m.ones[0:1, :], b1[0:1, r:r + 1], start=True, stop=True).then_inc(spread_ps.sem, 1)

        spread_max(X_)

        def gate_up(g):
            pe.wait_ge(*x_q(g + 1))
            for j in range(2 * C):
                if not isinstance(g, int) or g >= 1:
                    pe.wait_ge(*gu_here(2 * C * g - 2 * C + j + 1))
                pe.matmul(m.banks[2 + j], w["gu"][:, j * P:(j + 1) * P], columns(XNT, g, GW), start=True,
                          stop=True).then_inc(gu_ps.sem, 1)

        gate_up(0)
        with pe.Fori(1, NG) as g:
            gate_up(g)
        for r in (G_, U_, S_, O_):
            spread_max(r)
        for g in range(NG):
            for c in range(C):
                pe.wait_ge(*o_q(C * g + c + 1))
                if c == 0 and g >= 2:
                    pe.wait_ge(*x_done(g - 1))
                for i in range(GT):
                    mm = pe.matmul(m.banks[2 + g % 2][:, i * P:(i + 1) * P], G[:, C * g + c, i * P:(i + 1) * P],
                                   w["d"][:, c * P:(c + 1) * P], start=(c == 0 and i == 0), stop=(c == C - 1),
                                   skip_group_check=True)
            mm.then_inc(y_ps.sem, 1)

    def scalar(act):
        m.begin(act, start)

        for g in range(NG):
            norm.evacuate(act, g)

        def gate_up(g):
            for j in range(2 * C):
                act.wait_ge(*gu_ps(2 * C * g + j + 1))
                apart(act, m)
                act.activation(piece((G, U)[j // C], C * g + j % C), m.banks[2 + j], ACT.Copy).then_inc(gu_here.sem, 1)

        with act.Fori(0, NG) as g:
            gate_up(g)

        def scaled(x, r, done):
            act.activation(x, x, ACT.Identity, bias=m.round[:, 0:1], scale=inv[:, r:r + 1]).then_inc(done.sem, 1)

        act.wait_ge(*inv_set(G_ + 1))
        act.wait_ge(*gu_here(2 * K))

        def gate_pass(n):
            if on(n):
                scaled(piece(G, n), G_, g_a)
            if on(n - 1):
                act.wait_ge(*g_q(n))
                apart(act, m)
                act.activation(piece(SG, n - 1), piece(G, n - 1), ACT.Sigmoid).then_inc(sig.sem, 1)
            if on(n - 2):
                act.wait_ge(*sig(n - 1))
                apart(act, m)
                act.activation(piece(SG, n - 2), piece(SG, n - 2), ACT.Identity, bias=m.round[:, 0:1],
                               scale=65536.0).then_inc(sig_a.sem, 1)

        passes(act, gate_pass, K, 2)
        act.wait_ge(*inv_set(U_ + 1))
        with act.Fori(0, K) as k:
            scaled(piece(U, k), U_, u_a)
        act.wait_ge(*inv_set(S_ + 1))
        with act.Fori(0, K) as k:
            scaled(piece(G, k), S_, gs_a)
        act.wait_ge(*inv_set(O_ + 1))
        with act.Fori(0, K) as k:
            scaled(piece(G, k), O_, o_a)

    def gpsimd(pool):
        m.begin(pool, start)

        for g in range(NG):
            norm.rstd(pool, g)

    def vector(dve):
        m.begin(dve, start)

        for g in range(NG):
            norm.stats(dve, g)
            if g:
                norm.apply(dve, g - 1)
        norm.apply(dve, NG - 1)
        dve.wait_ge(*xn_ready(NG))
        dve.tensor_reduce(am[:, X_, 0:1], xn[:, :, :].rearrange("p t d -> p (t d)"), AX, ALU.max,
                          apply_absolute_value=True).then_inc(xmax.sem, 1)

        def find_scale(r, src, seen, count):
            dve.wait_ge(*seen(count))
            dve.tensor_reduce(a1[:, r:r + 1], src, AX, ALU.max).then_inc(rows_max.sem, 1)
            dve.wait_ge(*turned(r + 1))
            dve.tensor_reduce(b1[0:1, r:r + 1], J0[0:1, 0:P], AX, ALU.max).then_inc(one_max.sem, 1)
            dve.wait_ge(*spread_ps(r + 1))
            dve.tensor_scalar(scale[:, r:r + 1], J1[:, 0:1], 1.0 / QMAX, 1e-12, ALU.mult, ALU.max).then_inc(scale_set.sem, 1)
            dve.wait_ge(*scale_set(r + 1))
            dve.reciprocal(inv[:, r:r + 1], scale[:, r:r + 1]).then_inc(inv_set.sem, 1)
            dve.wait_ge(*inv_set(r + 1))

        find_scale(X_, am[:, X_, 0:1], xmax, 1)
        dve.wait_ge(*xnT_ready(NG))

        def quantise_x(n):
            if isinstance(n, int) and n >= NG:
                pass
            else:
                dve.tensor_scalar(columns(XNT, n, GW), columns(XNT, n, GW), inv[:, X_:X_ + 1], ROUND, ALU.mult,
                                  ALU.add).then_inc(x_a.sem, 1)
            if not isinstance(n, int) or n >= 1:
                dve.wait_ge(*x_a(n))
                quantise(dve, columns(XNT, n - 1, GW), X_).then_inc(x_q.sem, 1)

        passes(dve, quantise_x, NG, 1)

        def greatest(g):
            for j in range(2 * C):
                dve.wait_ge(*gu_here(2 * C * g + j + 1))
                dve.tensor_reduce(am[:, (G_, U_)[j // C], bass.ds(C * g + j % C, 1)],
                                  piece((G, U)[j // C], C * g + j % C), AX, ALU.max,
                                  apply_absolute_value=True).then_inc(gu_max.sem, 1)

        with dve.Fori(0, NG) as g:
            greatest(g)
        find_scale(G_, am[:, G_, 0:K], gu_max, 2 * K)
        find_scale(U_, am[:, U_, 0:K], gu_max, 2 * K)

        def gate_pass(n):
            if on(n):
                dve.wait_ge(*g_a(n + 1))
                quantise(dve, piece(G, n), G_).then_inc(g_q.sem, 1)
            if on(n - 2):
                k = n - 2
                dve.wait_ge(*sig_a(k + 1))
                dve.tensor_scalar(piece(SG, k), piece(SG, k), ROUND, 65535.0, ALU.subtract, ALU.min).then_inc(sig_q.sem, 1)
            if on(n - 3):
                k = n - 3
                dve.wait_ge(*sig_q(k + 1))
                dve.scalar_tensor_tensor(out=piece(G, k), in0=piece(SG, k), scalar=1.0 / 65536.0, in1=piece(G, k),
                                         op0=ALU.mult, op1=ALU.mult).then_inc(gs.sem, 1)
            if on(n - 4):
                k = n - 4
                dve.wait_ge(*gs(k + 1))
                dve.tensor_reduce(am[:, S_, bass.ds(k, 1)], piece(G, k), AX, ALU.max,
                                  apply_absolute_value=True).then_inc(gs_max.sem, 1)

        passes(dve, gate_pass, K, 4)
        find_scale(S_, am[:, S_, 0:K], gs_max, K)
        dve.tensor_tensor(us[:, :], scale[:, U_:U_ + 1], scale[:, S_:S_ + 1], ALU.mult).then_inc(us_set.sem, 1)
        dve.wait_ge(*us_set(1))

        def o_pass(n):
            if on(n):
                dve.wait_ge(*u_a(n + 1))
                quantise(dve, piece(U, n), U_, us[:, 0:1]).then_inc(u_q.sem, 1)
            if on(n - 1):
                k = n - 1
                dve.wait_ge(*u_q(k + 1))
                dve.wait_ge(*gs_a(k + 1))
                dve.scalar_tensor_tensor(out=piece(G, k), in0=piece(G, k), scalar=ROUND, in1=piece(U, k),
                                         op0=ALU.subtract, op1=ALU.mult).then_inc(o_here.sem, 1)
            if on(n - 2):
                k = n - 2
                dve.wait_ge(*o_here(k + 1))
                dve.tensor_reduce(am[:, O_, bass.ds(k, 1)], piece(G, k), AX, ALU.max,
                                  apply_absolute_value=True).then_inc(o_max.sem, 1)

        passes(dve, o_pass, K, 2)
        find_scale(O_, am[:, O_, 0:K], o_max, K)
        with dve.Fori(0, K) as k:
            dve.wait_ge(*o_a(k + 1))
            quantise(dve, piece(G, k), O_).then_inc(o_q.sem, 1)
        for g in range(NG):
            dve.wait_ge(*y_ps(g + 1))
            xg = m.X[:, g * GT:(g + 1) * GT, :].rearrange("p t d -> p (t d)")
            dve.tensor_tensor(xg, xg, m.banks[2 + g % 2], ALU.add).then_inc(x_done.sem, 1)

    L.tensor, L.scalar, L.gpsimd, L.vector = tensor, scalar, gpsimd, vector
    return L


def late_preparation(sh, m, ins, load):
    C, NB = 3, 12
    raw, q = sh.sb("qw_raw", [P, 3, C * P]), sh.sb("qw_rounded", [P, 3, C * P])
    s, rs = sh.sb("qw_scale", [P, 3, NB]), sh.sb("qw_inverse", [P, 3, NB])
    gu, d = sh.sb("qw_gate_up", [P, 2 * C * P]), sh.sb("qw_down", [P, C * P])
    for k, name in enumerate(("gate", "up")):
        load(raw[:, k, :].rearrange("p (c h) -> p c h", h=P), ins[f"L3_ffn_w_{name}"].rearrange("(c p) h -> p c h", p=P))
    load(raw[:, 2, :], ins["L3_ffn_w_down"])
    chain = sh.sem("qw_chain")
    turned_ps, turned = sh.sem("late_turned_ps"), sh.sem("late_turned")
    mask_valid, mask_set = sh.sem("mask_valid"), sh.sem("mask_set")
    w3_raw, w3 = sh.sb("L3w_raw", [P, 4, P]), m.w3
    for k, c in enumerate("qkvo"):
        load(w3_raw[:, k, :], ins[f"L3_xattn_W{c}"])
    flat = lambda x: x[:, :, :].rearrange("p k f -> p (k f)")
    blocks = lambda x: flat(x).rearrange("p (n b) -> p n b", b=32)
    spread = lambda x: flat(x).rearrange("p (n o) -> p n o", o=1).broadcast_to([P, 3 * NB, 32])

    def vector(dve):
        dve.tensor_tensor(m.valid[:, :, :], m.mask_keys[:, :, :],
                          m.mask_rows[:, :].rearrange("p (t o) -> p t o", o=1).broadcast_to([P, NT, S]),
                          ALU.mult).then_inc(mask_valid, 1)
        dve.wait_ge(mask_valid, 1)
        dve.tensor_reduce(m.rowvalid[:, :], m.valid[:, :, :], AX, ALU.max).then_inc(mask_set, 1)
        dve.tensor_scalar(m.maskbias[:, :, :], m.valid[:, :, :], -NEG, NEG, ALU.mult, ALU.add).then_inc(mask_set, 1)
        dve.tensor_reduce(flat(s), blocks(raw), AX, ALU.max, apply_absolute_value=True).then_inc(chain, 1)
        dve.wait_ge(chain, 1)
        dve.tensor_scalar(flat(s), flat(s), 1.0 / 7.0, 1e-12, ALU.mult, ALU.max).then_inc(chain, 1)
        dve.wait_ge(chain, 2)
        dve.reciprocal(flat(rs), flat(s)).then_inc(chain, 1)
        dve.wait_ge(chain, 3)
        dve.tensor_tensor(blocks(q), blocks(raw), spread(rs), ALU.mult).then_inc(chain, 1)
        dve.wait_ge(chain, 4)
        dve.tensor_scalar(flat(q), flat(q), ROUND, ROUND, ALU.add, ALU.subtract).then_inc(chain, 1)
        dve.wait_ge(chain, 5)
        dve.tensor_scalar(flat(q), flat(q), 7.0, -8.0, ALU.min, ALU.max).then_inc(chain, 1)
        dve.wait_ge(chain, 6)
        dve.tensor_tensor(blocks(q), blocks(q), spread(s), ALU.mult).then_inc(chain, 1)

    def tensor(pe):
        for k in range(4):
            tr = pe.transpose(m.banks[0][:, k * P:(k + 1) * P], w3_raw[:, k, :], m.ident[:, :])
        tr.then_inc(turned_ps, 1)
        pe.wait_ge(chain, 7)
        for k in range(3):
            if k >= 1:
                pe.wait_ge(turned, k)
            for c in range(C):
                tr = pe.transpose(m.banks[1 - k % 2][:, c * P:(c + 1) * P], q[:, k, c * P:(c + 1) * P], m.ident[:, :])
            tr.then_inc(turned_ps, 1)
        pe.wait_ge(turned, 4)

    def scalar(act):
        act.wait_ge(turned_ps, 1)
        act.activation(w3[:, :, :].rearrange("p k f -> p (k f)"), m.banks[0], ACT.Copy).then_inc(turned, 1)
        for k in range(3):
            act.wait_ge(turned_ps, k + 2)
            dst = d[:, :] if k == 2 else gu[:, k * C * P:(k + 1) * C * P]
            act.activation(dst, m.banks[1 - k % 2][:, 0:C * P], ACT.Copy).then_inc(turned, 1)

    L = Layer()
    L.tensor, L.scalar, L.vector, L.done = tensor, scalar, vector, (turned, 4)
    return L, {"gu": gu, "d": d}, (mask_set, 2)


def build(nc, ins, out, which=tuple(range(8))):
    ctx = ExitStack()
    with ctx:
        sh = Shared(nc, ctx)
        sb, sem = sh.sb, sh.sem

        class M:
            pass

        m = M()
        m.X = sb("X", [P, NT, D])
        m.ctxT = sb("ctxT", [P, TOK])
        m.xn = sb("xn", [P, NT, P])
        m.XNT = sb("XNT", [P, TOK])
        m.stats, m.meanvar = sb("stats", [P, NT, 6]), sb("meanvar", [P, NT, 2])
        m.vareps, m.rstd = sb("vareps", [P, NT]), sb("rstd", [P, NT])
        m.ident = sb("ident", [P, P])
        m.nhalf = sb("nhalf", [P, 1])
        m.hmask = sb("hmask", [P, H])
        m.vmask = sb("vmask", [P, H, S])
        m.maskbias = sb("maskbias", [P, NT, S])
        m.rowvalid = sb("rowvalid", [P, NT])
        ctx_raw = m.xn
        psum = sh.ps("psum", [P, 8, 512])
        m.banks = [psum[:, i, :] for i in range(8)]
        m.wide = [psum[:, 2:4, :], psum[:, 4:6, :], psum[:, 6:8, :]]

        loaded, consts, turned_ps, turned = sem("loaded"), sem("consts"), sem("turned_ps"), sem("turned")
        m.passed = sem("passed")
        ctx_loaded, x_loaded, first_loaded = sem("ctx_loaded"), sem("x_loaded"), sem("first_loaded")
        loads, first_loads = [], []

        def load(dst, src):
            loads.append((dst, src))

        def load_first(dst, src):
            first_loads.append((dst, src))

        rows, cols = sb("rows", [P, P]), sb("cols", [P, P])
        row = [0]

        rows0, cols0 = sb("rows0", [3, P]), sb("cols0", [P, 3])

        def columns_of(src):
            n = src.shape[0]
            load(rows[row[0]:row[0] + n, :], src)
            row[0] += n
            return cols[:, row[0] - n:row[0]]

        def column(src):
            return columns_of(src.rearrange("(o p) -> o p", o=1))

        def spread(name, src, load=load):
            c = sb(name, [P, src.shape[0]])
            load(c[:, :], src.rearrange("(o n) -> o n", o=1).partition_broadcast(P))
            return c[:, :]

        def matrix(name, src, load=load):
            c = sb(name, [P, src.shape[1]])
            load(c[:, :], src)
            return c[:, :]

        w0, b0 = {}, {}
        for i, k in enumerate("qkv"):
            load_first(rows0[i:i + 1, :], ins[f"L0_xattn_b{k}"].rearrange("(o p) -> o p", o=1))
            b0[k] = cols0[:, i:i + 1]
        for k in "kvqo":
            w0[k] = matrix(f"L0w{k}", ins[f"L0_xattn_W{k}"], load_first)
        b0["o"] = spread("L0bo", ins["L0_xattn_bo"], load_first)
        w1 = {"q": matrix("L1wq", ins["L1_xattn_w_q"]), "k": matrix("L1wk", ins["L1_xattn_w_kv"][:, 0:1024]),
              "v": matrix("L1wv", ins["L1_xattn_w_kv"][:, 1024:2048]),
              "gamma": column(ins["L1_xattn_ln_gamma"]), "beta": column(ins["L1_xattn_ln_beta"]),
              "bo": spread("L1bo", ins["L1_xattn_b_out"])}
        w1o = sb("L1wo", [P, HP, D])
        load(w1o[:, :, :], ins["L1_xattn_w_out"].rearrange("(c p) d -> p c d", p=P))
        w1["o"] = w1o
        gate_raw, gate = spread("L1gate_raw", ins["L1_xattn_gate"], load_first), sb("L1gate", [P, 1])
        w1["gate"] = gate[:, 0:1]
        gate_ready = sem("gate_ready")
        b2 = {}
        for name, E, parts in (("L1", 16, [("L1_ffn_routed_b2", 14), ("L1_ffn_shared_b2", 2)]),
                               ("L2", 8, [("L2_xattn_b2", 8)])):
            b2[name] = sb(f"{name}b2rep", [P, D])
            for r in range(P // E):
                at = r * E
                for src, k in parts:
                    load(b2[name][at:at + k, :], ins[src])
                    at += k
        f0b2 = spread("F0b2", ins["L0_ffn_b2"])
        wr1, br1 = matrix("L1wr", ins["L1_ffn_router_w"]), spread("L1br", ins["L1_ffn_router_b"])
        wr2, br2 = matrix("L2wr", ins["L2_xattn_Wg"]), spread("L2br", ins["L2_xattn_bg"])
        wr3 = columns_of(ins["L2_ffn_w_router"])
        b1_0 = columns_of(ins["L0_ffn_b1"].rearrange("(c p) -> c p", p=P))
        b1_1 = columns_of(ins["L1_ffn_routed_b1"])
        columns_of(ins["L1_ffn_shared_b1"])
        b1_1 = cols[:, row[0] - 16:row[0]]
        b1_2 = columns_of(ins["L2_xattn_b1"].rearrange("e (c p) -> (e c) p", p=P))
        m.rev = sb("rev", [P, 16])
        tmask16, tmask8 = sb("tmask16", [P, 8]), sb("tmask8", [P, 16])
        mask_rows, mask_keys = sb("mask_rows", [NT, P], U8), sb("mask_keys", [P, NT, S], U8)
        load(mask_rows[:, :], ins["mask_BxS2_bf1"].rearrange("(t u) s -> t (u s)", u=2))
        load(mask_keys[:, :, :], ins["mask_BxSxS2_bk0"].rearrange("(t u) s k -> (u s) t k", u=2))
        rows_f, m.mask_rows, m.valid = sb("rows_f", [NT, P]), sb("rows_c", [P, NT]), sb("valid", [P, NT, S])
        m.mask_keys = mask_keys
        rows_set, rows_ps, rows_turned = sem("mask_rows_set"), sem("mask_rows_in_psum"), sem("mask_rows_turned")
        m.w3 = sb("L3w", [P, 4, P])
        w3 = {c: m.w3[:, k, :] for k, c in enumerate("qkvo")}
        m.ones, m.round = sb("ones", [P, P]), sb("round", [P, 1])
        late, qw, masks_set = late_preparation(sh, m, ins, load)
        NLOAD = 16 * len(loads)

        def begin(eng, start):
            for s, v in start:
                eng.wait_ge(s, v)

        m.begin = begin
        m.weights_here = []
        m.split_free = []
        blocks = sb("blocks", [P, 2, 2, 2, HP, 2, S])
        m.blocks = blocks[:, 0], blocks[:, 1]
        m.sig = blocks[:, :, :, :, :, :, :].rearrange("p i a b c u k -> p (i a b c u k)")[:, 0:12 * GW].rearrange(
            "p (k f) -> p k f", f=GW)
        m.weight_buffers = {tag: (sb(f"{tag}_w1", [P, 2, C * P]), sb(f"{tag}_w2", [P, 2, C, D]))
                            for tag, C in (("E1", 1), ("E2", 4))}
        m.weight_buffers["F0"] = m.weight_buffers["E2"]
        m.weight_buffers["E3"] = (sb("E3_raw", [P, 2, 3, 3 * P]),)
        m.norm_after, m.stats_after = {}, {}
        start0 = [(x_loaded, 16), (first_loaded, 16 * len(first_loads)), (consts, 18), (turned, NG + 1)]

        makers = {
            0: lambda st: small_head_attention(sh, m, "A0", st, w0, b0, False),
            2: lambda st: wide_head_attention(sh, m, "A1", st + [(gate_ready, 1)], w1),
        }
        makers[1] = lambda st: experts(sh, m, "F0", st, dict(
            seen=0 in which, E=1, C=4, func=ACT.Gelu, bo=f0b2,
            weights=lambda e: (ins["L0_ffn_w1"].rearrange("(o d) f -> o d f", o=1),
                               ins["L0_ffn_w2"].rearrange("(o d) f -> o d f", o=1),
                               e), b1=b1_0))

        def weights1(e):
            if isinstance(e, int) and e >= 14:
                return ins["L1_ffn_shared_w1"], ins["L1_ffn_shared_w2"], e - 14
            return ins["L1_ffn_routed_w1"], ins["L1_ffn_routed_w2"], e

        makers[3] = lambda st: experts(sh, m, "E1", st, dict(
            then_norm=4 in which, seen=2 in which,
            E=16, C=1, func=ACT.Gelu, router="x", ER=14, wr=wr1, br=br1, whole=True, residual=True, b2=True,
            b2rep=b2["L1"], tmask=tmask16, b1=b1_1, weights=weights1))
        makers[4] = lambda st: experts(sh, m, "E2", st, dict(
            then_norm=5 in which, early=3 in which,
            late=late if late_inside else None,
            E=8, C=4, func=ACT.Relu, router="ctx", ER=8, wr=wr2, br=br2, whole=False, b2=True,
            b2rep=b2["L2"], tmask=tmask8, b1=b1_2,
            weights=lambda e: (ins["L2_xattn_W1"], ins["L2_xattn_W2"], e)))
        makers[5] = lambda st: experts(sh, m, "E3", st, dict(
            then_norm=6 in which, early=4 in which,
            E=8, C=3, gated=True, router="x", ER=8, wr=wr3, br=None, whole=False,
            weights=(ins["L2_ffn_w_gate"], ins["L2_ffn_w_up"], ins["L2_ffn_w_down"])))
        makers[6] = lambda st: small_head_attention(sh, m, "A3", st + [masks_set, late.done], w3, dict.fromkeys("qkvo"), True, early=5 in which)
        makers[7] = lambda st: quantised_ffn(sh, m, "Q3", st + [late.done], qw)
        early_stats = {0: "A0", 2: "A1"}
        early_norm = {3: "E1", 4: "E2", 5: "E3"}
        late_inside = 4 in which
        layers, st = [], start0
        if which[0] != 0:
            layers.append(Layer())
            layers[0].tensor = layers[0].vector = layers[0].scalar = layers[0].gpsimd = lambda eng: None
            layers[0].done = (turned, NG + 1)
            st = st + [(loaded, NLOAD), (turned, NG + 2)]
        for k in which:
            layers.append(makers[k](st))
            if k - 1 in early_norm and k - 1 in which:
                m.norm_after[early_norm[k - 1]] = layers[-1].norm
            if k - 1 in early_stats and k - 1 in which:
                m.stats_after[early_stats[k - 1]] = layers[-1].norm
            st = [layers[-1].done]
            if k == 0:
                st += [(loaded, NLOAD), (turned, NG + 2)]
        final = layers[-1].done

        stored = sem("stored")
        block = ctx.enter_context(nc.Block())

        @block.sync
        def _(sp):
            sp.dma_start(ctx_raw[:, :, :], ins["ctx_1024"].rearrange("(t u) s d -> (u s) t d", u=2)).then_inc(ctx_loaded, 16)
            sp.dma_start(m.X[:, :, :], ins["x"].rearrange("(t u) s d -> (u s) t d", u=2)).then_inc(x_loaded, 16)
            sp.wait_ge(x_loaded, 16)
            sp.wait_ge(first_loaded, 16 * len(first_loads))
            for dst, src in loads:
                sp.dma_start(dst, src).then_inc(loaded, 16)
            for L in layers:
                if L.sync:
                    L.sync(sp)
            sp.wait_ge(final[0], final[1])
            sp.dma_start(out.rearrange("(t u) s d -> (u s) t d", u=2), m.X[:, :, :]).then_inc(stored, 16)
            sp.wait_ge(stored, 16)

        @block.gpsimd
        def _(pool):
            pool.memset(m.ident[:, :], 0.0).then_inc(consts, 1)
            pool.memset(m.nhalf[:, :], -0.5).then_inc(consts, 1)
            pool.memset(m.hmask[:, :], 1.0).then_inc(consts, 1)
            pool.memset(m.vmask[:, :, :], 0.0).then_inc(consts, 1)
            pool.wait_ge(consts, 4)
            pool.affine_select(out=m.ident[:, :], in_=m.ident[:, :], compare_op=ALU.not_equal, fill=1.0,
                               base=0, pattern=[[-1, P]], channel_multiplier=1).then_inc(consts, 1)
            dh = D // H
            pool.affine_select(out=m.hmask[:, :], in_=m.hmask[:, :], compare_op=ALU.is_ge, fill=0.0,
                               base=0, pattern=[[-dh, H]], channel_multiplier=1).then_inc(consts, 1)
            pool.wait_ge(consts, 6)
            pool.affine_select(out=m.hmask[:, :], in_=m.hmask[:, :], compare_op=ALU.is_ge, fill=0.0,
                               base=dh - 1, pattern=[[dh, H]], channel_multiplier=-1).then_inc(consts, 1)
            for u in range(2):
                pool.wait_ge(consts, 7 + u)
                pool.memset(m.vmask[u * S:(u + 1) * S, u::2, :], 1.0).then_inc(consts, 1)
            pool.wait_ge(consts, 9)
            pool.iota(m.rev[:, :], pattern=[[-1, 16]], base=16, channel_multiplier=0,
                      allow_small_or_imprecise_dtypes=True).then_inc(consts, 1)
            for tm, E in ((tmask16, 16), (tmask8, 8)):
                pool.memset(tm[:, :], 1.0).then_inc(consts, 1)
            pool.wait_ge(consts, 12)
            for tm, E in ((tmask16, 16), (tmask8, 8)):
                pool.affine_select(out=tm[:, :], in_=tm[:, :], compare_op=ALU.is_ge, fill=0.0,
                                   base=0, pattern=[[-E, P // E]], channel_multiplier=1).then_inc(consts, 1)
            pool.wait_ge(consts, 14)
            for tm, E in ((tmask16, 16), (tmask8, 8)):
                pool.affine_select(out=tm[:, :], in_=tm[:, :], compare_op=ALU.is_ge, fill=0.0,
                                   base=E - 1, pattern=[[E, P // E]], channel_multiplier=-1).then_inc(consts, 1)
            pool.memset(m.ones[:, :], 1.0).then_inc(consts, 1)
            pool.memset(m.round[:, :], ROUND).then_inc(consts, 1)
            pool.wait_ge(consts, 18)
            layers[0].gpsimd(pool)
            pool.wait_ge(loaded, NLOAD)
            for L in layers[1:]:
                L.gpsimd(pool)

        @block.tensor
        def _(pe):
            pe.wait_ge(ctx_loaded, 16)
            pe.wait_ge(consts, 18)
            for g in range(NG):
                if g >= 2:
                    pe.wait_ge(turned, g - 1)
                for i in range(4):
                    tr = pe.transpose(m.banks[g % 2][:, i * P:(i + 1) * P], ctx_raw[:, 4 * g + i, :], m.ident[:, :])
                tr.then_inc(turned_ps, 1)
            pe.wait_ge(first_loaded, 16 * len(first_loads))
            pe.transpose(m.banks[2][:, 0:3], rows0[:, :], m.ident[0:3, 0:3]).then_inc(turned_ps, 1)
            layers[0].tensor(pe)
            pe.wait_ge(loaded, NLOAD)
            pe.wait_ge(*layers[0].done)
            nrow = row[0]
            pe.transpose(m.banks[2][:, 0:nrow], rows[0:nrow, :], m.ident[0:nrow, 0:nrow]).then_inc(turned_ps, 1)
            pe.wait_ge(rows_set, 1)
            pe.transpose(m.banks[3][:, 0:NT], rows_f[:, :], m.ident[0:NT, 0:NT]).then_inc(rows_ps, 1)
            if not late_inside:
                late.tensor(pe)
            for L in layers[1:]:
                L.tensor(pe)

        @block.scalar
        def _(act):
            for dst, src in first_loads:
                act.dma_start(dst, src).then_inc(first_loaded, 16)
            for g in range(NG):
                act.wait_ge(turned_ps, g + 1)
                act.activation(m.ctxT[:, g * GW:(g + 1) * GW], m.banks[g % 2], ACT.Copy).then_inc(turned, 1)
            act.wait_ge(turned_ps, NG + 1)
            act.activation(cols0[:, :], m.banks[2][:, 0:3], ACT.Copy).then_inc(turned, 1)
            act.wait_ge(first_loaded, 16 * len(first_loads))
            act.activation(gate[:, :], gate_raw, ACT.Tanh).then_inc(gate_ready, 1)
            layers[0].scalar(act)
            act.wait_ge(turned_ps, NG + 2)
            act.activation(cols[:, 0:row[0]], m.banks[2][:, 0:row[0]], ACT.Copy).then_inc(turned, 1)
            if not late_inside:
                late.scalar(act)
            for L in layers[1:]:
                L.scalar(act)

        @block.vector
        def _(dve):
            layers[0].vector(dve)
            dve.wait_ge(loaded, NLOAD)
            dve.tensor_copy(rows_f[:, :], mask_rows[:, :]).then_inc(rows_set, 1)
            dve.wait_ge(rows_ps, 1)
            dve.tensor_copy(m.mask_rows[:, :], m.banks[3][:, 0:NT]).then_inc(rows_turned, 1)
            dve.wait_ge(rows_turned, 1)
            if not late_inside:
                late.vector(dve)
            for L in layers[1:]:
                L.vector(dve)


_INS = [
    "x", "ctx_1024", "mask_BxS2_bf1", "mask_BxSxS2_bk0", "L0_xattn_Wq", "L0_xattn_bq", "L0_xattn_Wk",
    "L0_xattn_bk", "L0_xattn_Wv", "L0_xattn_bv", "L0_xattn_Wo", "L0_xattn_bo", "L0_ffn_w1", "L0_ffn_b1",
    "L0_ffn_w2", "L0_ffn_b2", "L1_xattn_ln_gamma", "L1_xattn_ln_beta", "L1_xattn_w_q", "L1_xattn_w_kv",
    "L1_xattn_w_out", "L1_xattn_b_out", "L1_xattn_gate", "L1_ffn_router_w", "L1_ffn_router_b", "L1_ffn_shared_w1",
    "L1_ffn_shared_b1", "L1_ffn_shared_w2", "L1_ffn_shared_b2", "L1_ffn_routed_w1", "L1_ffn_routed_b1",
    "L1_ffn_routed_w2", "L1_ffn_routed_b2", "L2_xattn_Wg", "L2_xattn_bg", "L2_xattn_W1", "L2_xattn_b1",
    "L2_xattn_W2", "L2_xattn_b2", "L2_ffn_w_router", "L2_ffn_w_gate", "L2_ffn_w_up", "L2_ffn_w_down",
    "L3_xattn_Wq", "L3_xattn_Wk", "L3_xattn_Wv", "L3_xattn_Wo", "L3_ffn_w_gate", "L3_ffn_w_up", "L3_ffn_w_down",
]


def kernel(**inputs):
    import numpy as np
    from concourse import bacc
    from concourse.bass_utils import run_bass_kernel_spmd

    nc = bacc.Bacc("TRN2", target_bir_lowering=False, num_devices=1)
    arrays, ins = {}, {}
    for name in _INS:
        a = np.ascontiguousarray(inputs[name])
        arrays[f"in_{name}"] = a
        ins[name] = nc.dram_tensor(f"in_{name}", a.shape, mybir.dt.from_np(a.dtype), kind="ExternalInput").ap()
    out = nc.dram_tensor("out", (B, S, D), F32, kind="ExternalOutput").ap()
    build(nc, ins, out)
    r = run_bass_kernel_spmd(nc, [arrays], core_ids=[0])
    return r.results[0]["out"]
```
